# Optimizing a Trainium2 kernel written in Bass

```python
import numpy as np
import jax
import jax.numpy as jnp

def _softmax(x, axis=-1):
    return jax.nn.softmax(x, axis=axis)

def _gelu(x):
    return jax.nn.gelu(x, approximate=True)

def _silu(x):
    return jax.nn.silu(x)

def _sigmoid(x):
    return jax.nn.sigmoid(x)

def _layernorm(x, axis=-1, eps=1e-05):
    m = jnp.mean(x, axis=axis, keepdims=True)
    v = jnp.var(x, axis=axis, keepdims=True)
    return (x - m) / jnp.sqrt(v + eps)

def _scatter_add(tgt, idx, src, axis=0):
    return tgt.at[idx].add(src)

def _segment_sum(src, seg, n):
    return jax.ops.segment_sum(src, seg, n)
kernel_name = 'mk_xattn_ffn_d4_seqx_r8_80b630'

def setup_inputs(seed: int=0):
    np.random.seed(seed)
    _w = jnp.asarray

    def _rec_inputs():
        import jax
        import jax.numpy as jnp
        _rk = jax.random.key(seed)
        x = -0.0002928 + 1 * jax.random.normal(jax.random.fold_in(_rk, 1), (16, 256, 128), jnp.float32)
        _lenS = 256 - jax.random.randint(jax.random.fold_in(_rk, 7), (16,), 0, max(1, 256 // 4) + 1, jnp.int32)
        _lenS2 = 1601 - jax.random.randint(jax.random.fold_in(_rk, 8), (16,), 0, max(1, 1601 // 4) + 1, jnp.int32)
        _ctx_1024P = jax.random.normal(jax.random.fold_in(_rk, 11), (16, 16, 128), jnp.float32)
        _ctx_1024c = jax.random.dirichlet(jax.random.fold_in(_rk, 511), 0.3 * jnp.ones((16,), jnp.float32), (16, 1601))
        _ctx_1024t = jnp.einsum('bsk,bkd->bsd', _ctx_1024c, _ctx_1024P)
        _ctx_1024t = _ctx_1024t * jax.lax.rsqrt(jnp.mean(jnp.square(_ctx_1024t)) + 1e-12) * 0.953939
        ctx_1024 = -1.39393e-06 + 0.999914 * (_ctx_1024t + 0.3 * jax.random.normal(jax.random.fold_in(_rk, 611), (16, 1601, 128), jnp.float32))
        _validS = jnp.arange(256)[None, :] < _lenS[:, None]
        _validS2 = jnp.arange(1601)[None, :] < _lenS2[:, None]
        _causal = jnp.tril(jnp.ones((256, 256), dtype=bool))
        mask_SxS_bc0 = jnp.logical_not(jnp.broadcast_to(_causal[:, :], (256, 256)))
        mask_Bx1xSxS2_ik1 = jnp.where(jnp.broadcast_to(_validS2[:, None, None, :], (16, 1, 256, 1601)), 1, 0).astype(jnp.int32)
        return (x, ctx_1024, mask_SxS_bc0, mask_Bx1xSxS2_ik1)
    x, ctx_1024, mask_SxS_bc0, mask_Bx1xSxS2_ik1 = _rec_inputs()

    def _L0_xattn_setup():
        import jax, jax.numpy as jnp
        import numpy as np
        HIDDEN = 128
        HEADS = 16
        HEAD_DIM = HIDDEN // HEADS

        def _split_heads(x):
            b, n, _ = x.shape
            return x.reshape(b, n, HEADS, HEAD_DIM).transpose(0, 2, 1, 3)
        key = jax.random.key(seed)
        ks = jax.random.split(key, 11)
        B, N, D = (2, 256, HIDDEN)
        scale = 1.0 / np.sqrt(D)
        inp = {'q': jax.random.normal(ks[0], (B, N, D), jnp.float32), 'k': jax.random.normal(ks[1], (B, N, D), jnp.float32), 'v': jax.random.normal(ks[2], (B, N, D), jnp.float32), 'Wq': jax.random.normal(ks[3], (D, D), jnp.float32) * scale, 'bq': jnp.zeros((D,), jnp.float32), 'Wk': jax.random.normal(ks[4], (D, D), jnp.float32) * scale, 'bk': jnp.zeros((D,), jnp.float32), 'Wv': jax.random.normal(ks[5], (D, D), jnp.float32) * scale, 'bv': jnp.zeros((D,), jnp.float32), 'Wo': jax.random.normal(ks[6], (D, D), jnp.float32) * scale, 'bo': jnp.zeros((D,), jnp.float32)}
        return inp
    _L0_xattn_all = _L0_xattn_setup()
    _L0_xattn_in = {k: v for k, v in _L0_xattn_all.items() if k in ('Wq', 'bq', 'Wk', 'bk', 'Wv', 'bv', 'Wo', 'bo')}
    del _L0_xattn_all

    def _L0_ffn_setup():
        import jax, jax.numpy as jnp
        import numpy as np
        INT8_MAX = 127.0

        def _absmax_scale(x, axes):
            amax = jnp.max(jnp.abs(x), axis=axes, keepdims=True)
            return jnp.maximum(amax, 1e-12) / INT8_MAX
        key = jax.random.key(seed)
        k1, k2 = jax.random.split(key)
        lhs = jax.random.normal(k1, (4, 1024, 128), dtype=jnp.float32)
        rhs = jax.random.normal(k2, (128, 128), dtype=jnp.float32)
        return {'lhs': lhs, 'rhs': rhs}
    _L0_ffn_all = _L0_ffn_setup()
    _L0_ffn_in = {k: v for k, v in _L0_ffn_all.items() if k in ('rhs',)}
    del _L0_ffn_all

    def _L1_xattn_setup():
        import jax, jax.numpy as jnp
        import numpy as np
        from jax import lax
        H = 16
        K1, K2 = (3, 3)
        LN_EPS = 1e-05

        def _ln(x, g, b):
            m = jnp.mean(x, axis=-1, keepdims=True)
            v = jnp.mean(jnp.square(x - m), axis=-1, keepdims=True)
            return (x - m) * lax.rsqrt(v + LN_EPS) * g + b

        def _gelu(x):
            return jax.nn.gelu(x, approximate=False)
        key = jax.random.key(seed)
        B, T, D, Th = (4, 128, 128, 32)
        C = 2 * D
        ks = jax.random.split(key, 16)

        def w(k, shape):
            fan_in = shape[0]
            return (jax.random.normal(k, shape, jnp.float32) / np.sqrt(fan_in)).astype(jnp.float32)
        inp = {'x': jax.random.normal(ks[0], (B, T, D), jnp.float32), 'historical_data': jax.random.normal(ks[1], (B, Th, D), jnp.float32), 'Wq': w(ks[2], (D, D)), 'Wk': w(ks[3], (D, D)), 'Wv': w(ks[4], (D, D)), 'hist_W': w(ks[5], (D, C)), 'hist_b': jnp.zeros((C,), jnp.float32), 'hist_ln_g': jnp.ones((C,), jnp.float32), 'hist_ln_b': jnp.zeros((C,), jnp.float32), 'ctx_W1': w(ks[6], (C, C // 4)), 'ctx_b1': jnp.zeros((C // 4,), jnp.float32), 'ctx_W2': w(ks[7], (C // 4, 1)), 'ctx_b2': jnp.zeros((1,), jnp.float32), 'kg_W1': w(ks[8], (C, D)), 'kg_b1': jnp.zeros((D,), jnp.float32), 'kg_ln_g': jnp.ones((D,), jnp.float32), 'kg_ln_b': jnp.zeros((D,), jnp.float32), 'kg_W2': w(ks[9], (D, H * K1 * K2)), 'kg_b2': jnp.zeros((H * K1 * K2,), jnp.float32), 'proj_W': w(ks[10], (D, D)), 'proj_b': jnp.zeros((D,), jnp.float32), 'causal_mask': jnp.triu(jnp.ones((T, T), bool), k=1)}
        return inp
    _L1_xattn_all = _L1_xattn_setup()
    _L1_xattn_in = {k: v for k, v in _L1_xattn_all.items() if k in ('Wq', 'Wk', 'Wv', 'hist_W', 'hist_b', 'hist_ln_g', 'hist_ln_b', 'ctx_W1', 'ctx_b1', 'ctx_W2', 'ctx_b2', 'kg_W1', 'kg_b1', 'kg_ln_g', 'kg_ln_b', 'kg_W2', 'kg_b2', 'proj_W', 'proj_b')}
    del _L1_xattn_all

    def _L1_ffn_setup():
        import jax, jax.numpy as jnp
        import numpy as np
        H, E, DFF = (128, 8, 512)
        key = jax.random.key(seed)
        ks = jax.random.split(key, 7)
        s = lambda *shape: 1.0 / np.sqrt(shape[-2] if len(shape) > 1 else shape[-1])
        x = jax.random.normal(ks[0], (2, 256, H), dtype=jnp.float32)
        Wr = jax.random.normal(ks[1], (H, E), dtype=jnp.float32) * (1.0 / np.sqrt(H))
        br = jnp.zeros((E,), dtype=jnp.float32)
        W1 = jax.random.normal(ks[2], (E, H, DFF), dtype=jnp.float32) * (1.0 / np.sqrt(H))
        b1 = jnp.zeros((E, DFF), dtype=jnp.float32)
        W2 = jax.random.normal(ks[3], (E, DFF, H), dtype=jnp.float32) * (1.0 / np.sqrt(DFF))
        b2 = jnp.zeros((E, H), dtype=jnp.float32)
        return {'x': x, 'Wr': Wr, 'br': br, 'W1': W1, 'b1': b1, 'W2': W2, 'b2': b2}
    _L1_ffn_all = _L1_ffn_setup()
    _L1_ffn_in = {k: v for k, v in _L1_ffn_all.items() if k in ('Wr', 'br', 'W1', 'b1', 'W2', 'b2')}
    del _L1_ffn_all

    def _L2_xattn_setup():
        import jax, jax.numpy as jnp
        import numpy as np
        B, LQ, LKV, D = (8, 256, 256, 128)
        key = jax.random.key(seed)
        k1, k2, k3, k4, k5, k6, k7 = jax.random.split(key, 7)
        s = 1.0 / np.sqrt(D)
        return {'query': jax.random.normal(k1, (B, LQ, D), jnp.float32), 'key': jax.random.normal(k2, (B, LKV, D), jnp.float32), 'value': jax.random.normal(k3, (B, LKV, D), jnp.float32), 'Wq': jax.random.uniform(k4, (D, D), jnp.float32, -s, s), 'bq': jax.random.uniform(k5, (D,), jnp.float32, -s, s), 'Wk': jax.random.uniform(k6, (D, D), jnp.float32, -s, s), 'bk': jax.random.uniform(k7, (D,), jnp.float32, -s, s), 'scale_factor': 32, 'dropout_p': 0}
    _L2_xattn_all = _L2_xattn_setup()
    _L2_xattn_in = {k: v for k, v in _L2_xattn_all.items() if k in ('Wq', 'bq', 'Wk', 'bk')}
    del _L2_xattn_all

    def _L2_ffn_setup():
        import jax, jax.numpy as jnp
        import numpy as np
        B, T, D, FF, E, TOP_K = (8, 256, 128, 512, 8, 2)
        key = jax.random.key(seed)
        kx, kr, k1, k2 = jax.random.split(key, 4)
        x = jax.random.normal(kx, (B, T, D), dtype=jnp.float32)
        Wr = jax.random.normal(kr, (E, D), dtype=jnp.float32) * 0.02
        W1 = jax.random.normal(k1, (E, D, FF), dtype=jnp.float32) * 0.02
        W2 = jax.random.normal(k2, (E, FF, D), dtype=jnp.float32) * 0.02
        return {'x': x, 'Wr': Wr, 'W1': W1, 'W2': W2}
    _L2_ffn_all = _L2_ffn_setup()
    _L2_ffn_in = {k: v for k, v in _L2_ffn_all.items() if k in ('Wr', 'W1', 'W2')}
    del _L2_ffn_all

    def _L3_xattn_setup():
        import jax, jax.numpy as jnp
        import numpy as np
        NUM_HEADS = 16
        rng = jax.random.key(seed)
        ks = jax.random.split(rng, 12)
        B, S, D = (2, 256, 128)
        sc = 1.0 / np.sqrt(D)
        inp = {'query': jax.random.normal(ks[0], (B, S, D), jnp.float32), 'key': jax.random.normal(ks[1], (B, S, D), jnp.float32), 'value': jax.random.normal(ks[2], (B, S, D), jnp.float32), 'mask': jax.random.randint(ks[3], (B, 1, S, S), 0, 2, jnp.int32), 'Wq': jax.random.normal(ks[4], (D, D), jnp.float32) * sc, 'bq': jnp.zeros((D,), jnp.float32), 'Wk': jax.random.normal(ks[5], (D, D), jnp.float32) * sc, 'bk': jnp.zeros((D,), jnp.float32), 'Wv': jax.random.normal(ks[6], (D, D), jnp.float32) * sc, 'bv': jnp.zeros((D,), jnp.float32), 'Wo': jax.random.normal(ks[7], (D, D), jnp.float32) * sc, 'bo': jnp.zeros((D,), jnp.float32)}
        return inp
    _L3_xattn_all = _L3_xattn_setup()
    _L3_xattn_in = {k: v for k, v in _L3_xattn_all.items() if k in ('Wq', 'bq', 'Wk', 'bk', 'Wv', 'bv', 'Wo', 'bo')}
    del _L3_xattn_all

    def _L3_ffn_setup():
        import jax, jax.numpy as jnp
        import numpy as np
        B, S, D_MODEL, D_HIDDEN = (4, 256, 128, 512)

        def act_quant(x):
            scale = 127.0 / jnp.clip(jnp.max(jnp.abs(x), axis=-1, keepdims=True), 1e-05)
            return jnp.clip(jnp.round(x * scale), -128, 127) / scale

        def weight_quant(w):
            scale = 1.0 / jnp.clip(jnp.mean(jnp.abs(w)), 1e-05)
            return jnp.clip(jnp.round(w * scale), -1, 1) / scale

        def bit_linear(x, w):
            xq = x + jax.lax.stop_gradient(act_quant(x) - x)
            wq = w + jax.lax.stop_gradient(weight_quant(w) - w)
            return jnp.einsum('bsd,hd->bsh', xq, wq)

        def depthwise_conv1d(x_bcl, w, b):
            y = jax.lax.conv_general_dilated(x_bcl, w, window_strides=(1,), padding=[(1, 1)], dimension_numbers=('NCH', 'OIH', 'NCH'), feature_group_count=x_bcl.shape[1])
            return y + b[None, :, None]
        key = jax.random.key(seed)
        ks = jax.random.split(key, 5)
        lim1 = 1.0 / np.sqrt(D_MODEL)
        lim2 = 1.0 / np.sqrt(D_HIDDEN)
        limc = 1.0 / np.sqrt(3.0)
        return {'x': jax.random.normal(ks[0], (B, S, D_MODEL), dtype=jnp.float32), 'w1': jax.random.uniform(ks[1], (D_HIDDEN, D_MODEL), jnp.float32, -lim1, lim1), 'conv_w': jax.random.uniform(ks[2], (D_HIDDEN, 1, 3), jnp.float32, -limc, limc), 'conv_b': jax.random.uniform(ks[3], (D_HIDDEN,), jnp.float32, -limc, limc), 'w2': jax.random.uniform(ks[4], (D_MODEL, D_HIDDEN), jnp.float32, -lim2, lim2)}
    _L3_ffn_all = _L3_ffn_setup()
    _L3_ffn_in = {k: v for k, v in _L3_ffn_all.items() if k in ('w1', 'conv_w', 'conv_b', 'w2')}
    del _L3_ffn_all
    return {'x': x, 'ctx_1024': ctx_1024, 'mask_SxS_bc0': mask_SxS_bc0, 'mask_Bx1xSxS2_ik1': mask_Bx1xSxS2_ik1, 'L0_xattn_Wq': _L0_xattn_in['Wq'], 'L0_xattn_bq': _L0_xattn_in['bq'], 'L0_xattn_Wk': _L0_xattn_in['Wk'], 'L0_xattn_bk': _L0_xattn_in['bk'], 'L0_xattn_Wv': _L0_xattn_in['Wv'], 'L0_xattn_bv': _L0_xattn_in['bv'], 'L0_xattn_Wo': _L0_xattn_in['Wo'], 'L0_xattn_bo': _L0_xattn_in['bo'], 'L0_ffn_rhs': _L0_ffn_in['rhs'], 'L1_xattn_Wq': _L1_xattn_in['Wq'], 'L1_xattn_Wk': _L1_xattn_in['Wk'], 'L1_xattn_Wv': _L1_xattn_in['Wv'], 'L1_xattn_hist_W': _L1_xattn_in['hist_W'], 'L1_xattn_hist_b': _L1_xattn_in['hist_b'], 'L1_xattn_hist_ln_g': _L1_xattn_in['hist_ln_g'], 'L1_xattn_hist_ln_b': _L1_xattn_in['hist_ln_b'], 'L1_xattn_ctx_W1': _L1_xattn_in['ctx_W1'], 'L1_xattn_ctx_b1': _L1_xattn_in['ctx_b1'], 'L1_xattn_ctx_W2': _L1_xattn_in['ctx_W2'], 'L1_xattn_ctx_b2': _L1_xattn_in['ctx_b2'], 'L1_xattn_kg_W1': _L1_xattn_in['kg_W1'], 'L1_xattn_kg_b1': _L1_xattn_in['kg_b1'], 'L1_xattn_kg_ln_g': _L1_xattn_in['kg_ln_g'], 'L1_xattn_kg_ln_b': _L1_xattn_in['kg_ln_b'], 'L1_xattn_kg_W2': _L1_xattn_in['kg_W2'], 'L1_xattn_kg_b2': _L1_xattn_in['kg_b2'], 'L1_xattn_proj_W': _L1_xattn_in['proj_W'], 'L1_xattn_proj_b': _L1_xattn_in['proj_b'], 'L1_ffn_Wr': _L1_ffn_in['Wr'], 'L1_ffn_br': _L1_ffn_in['br'], 'L1_ffn_W1': _L1_ffn_in['W1'], 'L1_ffn_b1': _L1_ffn_in['b1'], 'L1_ffn_W2': _L1_ffn_in['W2'], 'L1_ffn_b2': _L1_ffn_in['b2'], 'L2_xattn_Wq': _L2_xattn_in['Wq'], 'L2_xattn_bq': _L2_xattn_in['bq'], 'L2_xattn_Wk': _L2_xattn_in['Wk'], 'L2_xattn_bk': _L2_xattn_in['bk'], 'L2_ffn_Wr': _L2_ffn_in['Wr'], 'L2_ffn_W1': _L2_ffn_in['W1'], 'L2_ffn_W2': _L2_ffn_in['W2'], 'L3_xattn_Wq': _L3_xattn_in['Wq'], 'L3_xattn_bq': _L3_xattn_in['bq'], 'L3_xattn_Wk': _L3_xattn_in['Wk'], 'L3_xattn_bk': _L3_xattn_in['bk'], 'L3_xattn_Wv': _L3_xattn_in['Wv'], 'L3_xattn_bv': _L3_xattn_in['bv'], 'L3_xattn_Wo': _L3_xattn_in['Wo'], 'L3_xattn_bo': _L3_xattn_in['bo'], 'L3_ffn_w1': _L3_ffn_in['w1'], 'L3_ffn_conv_w': _L3_ffn_in['conv_w'], 'L3_ffn_conv_b': _L3_ffn_in['conv_b'], 'L3_ffn_w2': _L3_ffn_in['w2']}

def reference(x, ctx_1024, mask_SxS_bc0, mask_Bx1xSxS2_ik1, L0_xattn_Wq, L0_xattn_bq, L0_xattn_Wk, L0_xattn_bk, L0_xattn_Wv, L0_xattn_bv, L0_xattn_Wo, L0_xattn_bo, L0_ffn_rhs, L1_xattn_Wq, L1_xattn_Wk, L1_xattn_Wv, L1_xattn_hist_W, L1_xattn_hist_b, L1_xattn_hist_ln_g, L1_xattn_hist_ln_b, L1_xattn_ctx_W1, L1_xattn_ctx_b1, L1_xattn_ctx_W2, L1_xattn_ctx_b2, L1_xattn_kg_W1, L1_xattn_kg_b1, L1_xattn_kg_ln_g, L1_xattn_kg_ln_b, L1_xattn_kg_W2, L1_xattn_kg_b2, L1_xattn_proj_W, L1_xattn_proj_b, L1_ffn_Wr, L1_ffn_br, L1_ffn_W1, L1_ffn_b1, L1_ffn_W2, L1_ffn_b2, L2_xattn_Wq, L2_xattn_bq, L2_xattn_Wk, L2_xattn_bk, L2_ffn_Wr, L2_ffn_W1, L2_ffn_W2, L3_xattn_Wq, L3_xattn_bq, L3_xattn_Wk, L3_xattn_bk, L3_xattn_Wv, L3_xattn_bv, L3_xattn_Wo, L3_xattn_bo, L3_ffn_w1, L3_ffn_conv_w, L3_ffn_conv_b, L3_ffn_w2):
    import jax
    import jax.numpy as jnp

    def _L0_xattn_ref(q, k, v, Wq, bq, Wk, bk, Wv, bv, Wo, bo):
        import jax, jax.numpy as jnp
        import numpy as np
        HIDDEN = 128
        HEADS = 16
        HEAD_DIM = HIDDEN // HEADS

        def _split_heads(x):
            b, n, _ = x.shape
            return x.reshape(b, n, HEADS, HEAD_DIM).transpose(0, 2, 1, 3)
        Q = _split_heads(q @ Wq.T + bq)
        K = _split_heads(k @ Wk.T + bk)
        V = _split_heads(v @ Wv.T + bv)
        scale = 1.0 / jnp.sqrt(jnp.asarray(HEAD_DIM, Q.dtype))
        scores = jnp.einsum('bhnd,bhmd->bhnm', Q, K) * scale
        attn = jax.nn.softmax(scores, axis=-1)
        out = jnp.einsum('bhnm,bhmd->bhnd', attn, V)
        b, h, n, d = out.shape
        out = out.transpose(0, 2, 1, 3).reshape(b, n, h * d)
        return out @ Wo.T + bo

    def _L0_ffn_ref(lhs, rhs):
        import jax, jax.numpy as jnp
        import numpy as np
        INT8_MAX = 127.0

        def _absmax_scale(x, axes):
            amax = jnp.max(jnp.abs(x), axis=axes, keepdims=True)
            return jnp.maximum(amax, 1e-12) / INT8_MAX
        lhs_scale = _absmax_scale(lhs, (2,))
        rhs_scale = _absmax_scale(rhs, (0,))
        q_lhs = jnp.clip(jnp.round(lhs / lhs_scale), -INT8_MAX, INT8_MAX).astype(jnp.int8)
        q_rhs = jnp.clip(jnp.round(rhs / rhs_scale), -INT8_MAX, INT8_MAX).astype(jnp.int8)
        acc = jax.lax.dot_general(q_lhs, q_rhs, (((2,), (0,)), ((), ())), preferred_element_type=jnp.int32)
        return acc.astype(jnp.float32) * lhs_scale * rhs_scale

    def _L1_xattn_ref(x, historical_data, Wq, Wk, Wv, hist_W, hist_b, hist_ln_g, hist_ln_b, ctx_W1, ctx_b1, ctx_W2, ctx_b2, kg_W1, kg_b1, kg_ln_g, kg_ln_b, kg_W2, kg_b2, proj_W, proj_b, causal_mask):
        import jax, jax.numpy as jnp
        import numpy as np
        from jax import lax
        H = 16
        K1, K2 = (3, 3)
        LN_EPS = 1e-05

        def _ln(x, g, b):
            m = jnp.mean(x, axis=-1, keepdims=True)
            v = jnp.mean(jnp.square(x - m), axis=-1, keepdims=True)
            return (x - m) * lax.rsqrt(v + LN_EPS) * g + b

        def _gelu(x):
            return jax.nn.gelu(x, approximate=False)
        B, T, D = x.shape
        hd = D // H
        scale = hd ** (-0.5)
        q = (x @ Wq).reshape(B, T, H, hd).transpose(0, 2, 1, 3)
        k = (x @ Wk).reshape(B, T, H, hd).transpose(0, 2, 1, 3)
        v = (x @ Wv).reshape(B, T, H, hd).transpose(0, 2, 1, 3)
        attn = jnp.einsum('bhqd,bhkd->bhqk', q, k) * scale
        eh = _gelu(_ln(historical_data @ hist_W + hist_b, hist_ln_g, hist_ln_b))
        aw = _gelu(eh @ ctx_W1 + ctx_b1) @ ctx_W2 + ctx_b2
        aw = jax.nn.softmax(aw, axis=1)
        cc = jnp.sum(eh * aw, axis=1)
        kp = _gelu(_ln(cc @ kg_W1 + kg_b1, kg_ln_g, kg_ln_b)) @ kg_W2 + kg_b2
        kernels = jax.nn.softmax(kp.reshape(B, H, K1 * K2), axis=-1)
        kernels = kernels.reshape(B * H, 1, K1, K2)
        mask = causal_mask[None, None]
        attn0 = jnp.where(mask, 0.0, attn).reshape(1, B * H, T, T)
        attn = lax.conv_general_dilated(attn0, kernels, window_strides=(1, 1), padding=((K1 // 2, K1 // 2), (K2 // 2, K2 // 2)), feature_group_count=B * H, dimension_numbers=('NCHW', 'OIHW', 'NCHW')).reshape(B, H, T, T)
        attn = jnp.where(mask, -jnp.inf, attn)
        p = jax.nn.softmax(attn, axis=-1)
        out = jnp.einsum('bhqk,bhkd->bhqd', p, v)
        out = out.transpose(0, 2, 1, 3).reshape(B, T, D)
        return out @ proj_W + proj_b

    def _L1_ffn_ref(x, Wr, br, W1, b1, W2, b2):
        import jax, jax.numpy as jnp
        import numpy as np
        H, E, DFF = (128, 8, 512)
        B, S, Hd = x.shape
        n_exp = W1.shape[0]
        xt = x.reshape(-1, Hd)
        logits = xt @ Wr + br
        probs = jax.nn.softmax(logits, axis=-1)
        gate = jnp.max(probs, axis=-1)
        idx = jnp.argmax(probs, axis=-1)
        h1 = jnp.maximum(jnp.einsum('th,ehf->etf', xt, W1) + b1[:, None, :], 0.0)
        ye = jnp.einsum('etf,efh->eth', h1, W2) + b2[:, None, :]
        onehot = jax.nn.one_hot(idx, n_exp, dtype=xt.dtype)
        y = jnp.einsum('te,eth->th', onehot, ye) * gate[:, None]
        return y.reshape(B, S, Hd)

    def _L2_xattn_ref(query, key, value, Wq, bq, Wk, bk, scale_factor, dropout_p):
        import jax, jax.numpy as jnp
        import numpy as np
        B, LQ, LKV, D = (8, 256, 256, 128)
        q = jnp.einsum('bld,ed->ble', query, Wq) + bq
        k = jnp.einsum('bld,ed->ble', key, Wk) + bk
        scores = jnp.einsum('bqd,bkd->bqk', q, k) / jnp.float32(scale_factor)
        attn = jax.nn.softmax(scores, axis=-1)
        return jnp.einsum('bqk,bkd->bqd', attn, value)

    def _L2_ffn_ref(x, Wr, W1, W2):
        import jax, jax.numpy as jnp
        import numpy as np
        B, T, D, FF, E, TOP_K = (8, 256, 128, 512, 8, 2)
        Bs, Ts, Ds = x.shape
        Ne = Wr.shape[0]
        xf = x.reshape(-1, Ds)
        N = xf.shape[0]
        logits = xf @ Wr.T
        topk_vals, topk_idx = jax.lax.top_k(logits, TOP_K)
        w = jax.nn.softmax(topk_vals.astype(jnp.float32), axis=-1).astype(x.dtype)
        idx_flat = topk_idx.reshape(-1)
        w_flat = w.reshape(-1)
        sort_idx = jnp.argsort(idx_flat)
        rev = sort_idx // TOP_K
        sw = w_flat[sort_idx]
        perm = xf[rev]
        S = perm.shape[0]
        chunks = perm.reshape(Ne, S // Ne, Ds)
        h = jax.nn.gelu(jnp.einsum('ecd,edf->ecf', chunks, W1), approximate=False)
        eo = jnp.einsum('ecf,efd->ecd', h, W2).reshape(S, Ds)
        out = jnp.zeros((N, Ds), dtype=x.dtype).at[rev].add(eo * sw[:, None])
        return out.reshape(Bs, Ts, Ds)

    def _L3_xattn_ref(query, key, value, mask, Wq, bq, Wk, bk, Wv, bv, Wo, bo):
        import jax, jax.numpy as jnp
        import numpy as np
        NUM_HEADS = 16
        B, S, D = query.shape
        H = NUM_HEADS
        hd = D // H

        def split_heads(x):
            return x.reshape(B, -1, H, hd).transpose(0, 2, 1, 3)
        q = split_heads(query @ Wq.T + bq)
        k = split_heads(key @ Wk.T + bk)
        v = split_heads(value @ Wv.T + bv)
        attn = jnp.einsum('bhqd,bhkd->bhqk', q, k) * hd ** (-0.5)
        attn = jnp.where(mask == 0, jnp.float32(-1000000000.0), attn)
        p = jax.nn.softmax(attn, axis=-1)
        out = jnp.einsum('bhqk,bhkd->bhqd', p, v)
        out = out.transpose(0, 2, 1, 3).reshape(B, S, D)
        return out @ Wo.T + bo

    def _L3_ffn_ref(x, w1, conv_w, conv_b, w2):
        import jax, jax.numpy as jnp
        import numpy as np
        B, S, D_MODEL, D_HIDDEN = (4, 256, 128, 512)

        def act_quant(x):
            scale = 127.0 / jnp.clip(jnp.max(jnp.abs(x), axis=-1, keepdims=True), 1e-05)
            return jnp.clip(jnp.round(x * scale), -128, 127) / scale

        def weight_quant(w):
            scale = 1.0 / jnp.clip(jnp.mean(jnp.abs(w)), 1e-05)
            return jnp.clip(jnp.round(w * scale), -1, 1) / scale

        def bit_linear(x, w):
            xq = x + jax.lax.stop_gradient(act_quant(x) - x)
            wq = w + jax.lax.stop_gradient(weight_quant(w) - w)
            return jnp.einsum('bsd,hd->bsh', xq, wq)

        def depthwise_conv1d(x_bcl, w, b):
            y = jax.lax.conv_general_dilated(x_bcl, w, window_strides=(1,), padding=[(1, 1)], dimension_numbers=('NCH', 'OIH', 'NCH'), feature_group_count=x_bcl.shape[1])
            return y + b[None, :, None]
        h = bit_linear(x, w1)
        h = depthwise_conv1d(h.transpose(0, 2, 1), conv_w, conv_b)
        h = h.transpose(0, 2, 1)
        h = jax.nn.silu(h)
        return bit_linear(h, w2)
    x = x + _L0_xattn_ref(_layernorm(x, axis=-1), ctx_1024, ctx_1024, L0_xattn_Wq, L0_xattn_bq, L0_xattn_Wk, L0_xattn_bk, L0_xattn_Wv, L0_xattn_bv, L0_xattn_Wo, L0_xattn_bo)
    x = x + _L0_ffn_ref(_layernorm(x, axis=-1), L0_ffn_rhs)
    x = x + _L1_xattn_ref(_layernorm(x, axis=-1), ctx_1024, L1_xattn_Wq, L1_xattn_Wk, L1_xattn_Wv, L1_xattn_hist_W, L1_xattn_hist_b, L1_xattn_hist_ln_g, L1_xattn_hist_ln_b, L1_xattn_ctx_W1, L1_xattn_ctx_b1, L1_xattn_ctx_W2, L1_xattn_ctx_b2, L1_xattn_kg_W1, L1_xattn_kg_b1, L1_xattn_kg_ln_g, L1_xattn_kg_ln_b, L1_xattn_kg_W2, L1_xattn_kg_b2, L1_xattn_proj_W, L1_xattn_proj_b, mask_SxS_bc0)
    x = x + _L1_ffn_ref(_layernorm(x, axis=-1), L1_ffn_Wr, L1_ffn_br, L1_ffn_W1, L1_ffn_b1, L1_ffn_W2, L1_ffn_b2)
    x = x + _L2_xattn_ref(_layernorm(x, axis=-1), ctx_1024, ctx_1024, L2_xattn_Wq, L2_xattn_bq, L2_xattn_Wk, L2_xattn_bk, 32, 0)
    x = x + _L2_ffn_ref(_layernorm(x, axis=-1), L2_ffn_Wr, L2_ffn_W1, L2_ffn_W2)
    x = x + _L3_xattn_ref(_layernorm(x, axis=-1), ctx_1024, ctx_1024, mask_Bx1xSxS2_ik1, L3_xattn_Wq, L3_xattn_bq, L3_xattn_Wk, L3_xattn_bk, L3_xattn_Wv, L3_xattn_bv, L3_xattn_Wo, L3_xattn_bo)
    x = x + _L3_ffn_ref(_layernorm(x, axis=-1), L3_ffn_w1, L3_ffn_conv_w, L3_ffn_conv_b, L3_ffn_w2)
    return x

_drawn_inputs = setup_inputs


def setup_inputs(seed=0):
    import zlib

    import numpy as np

    out = dict(_drawn_inputs(seed))
    spreads = {'L0_xattn_bq': (0.0, 0.364),
     'L0_xattn_bk': (0.0, 0.8),
     'L0_xattn_bv': (0.0, 0.1),
     'L0_xattn_bo': (0.0, 0.1),
     'L1_xattn_hist_b': (0.0, 0.8),
     'L1_xattn_hist_ln_g': (1.0, 0.6),
     'L1_xattn_hist_ln_b': (0.0, 0.8),
     'L1_xattn_ctx_b1': (0.0, 0.8),
     'L1_xattn_kg_b1': (0.0, 0.8),
     'L1_xattn_kg_ln_g': (1.0, 0.6),
     'L1_xattn_kg_ln_b': (0.0, 0.8),
     'L1_xattn_kg_b2': (0.0, 0.8),
     'L1_xattn_proj_b': (0.0, 0.8),
     'L1_ffn_br': (0.0, 0.8),
     'L1_ffn_b1': (0.0, 0.8),
     'L1_ffn_b2': (0.0, 0.8),
     'L3_xattn_bq': (0.0, 0.8),
     'L3_xattn_bk': (0.0, 0.8),
     'L3_xattn_bv': (0.0, 0.8),
     'L3_xattn_bo': (0.0, 0.8)}
    factors = {'L1_xattn_Wq': 8.0,
     'L1_xattn_Wk': 8.0,
     'L1_xattn_hist_W': 8.0,
     'L1_xattn_ctx_W1': 8.0,
     'L1_xattn_ctx_W2': 8.0,
     'L1_xattn_kg_W1': 8.0,
     'L1_xattn_kg_W2': 8.0,
     'L1_ffn_W1': 2.787,
     'L2_xattn_Wq': 8.0,
     'L2_xattn_bq': 8.0,
     'L2_xattn_Wk': 8.0,
     'L2_xattn_bk': 8.0,
     'L2_ffn_Wr': 8.0,
     'L2_ffn_W1': 8.0,
     'L2_ffn_W2': 8.0,
     'L3_xattn_Wq': 3.147,
     'L3_xattn_Wk': 3.135,
     'L3_ffn_w1': 8.0,
     'L3_ffn_conv_w': 8.0,
     'L3_ffn_conv_b': 8.0,
     'L3_ffn_w2': 7.016}
    for name, (base, spread) in spreads.items():
        noise = np.random.default_rng([zlib.crc32(name.encode()), seed]).standard_normal(out[name].shape)
        drawn = base * np.exp(spread * noise) if base else spread * noise
        out[name] = jnp.asarray(drawn.astype(out[name].dtype))
    for name, factor in factors.items():
        out[name] = (out[name] * factor).astype(out[name].dtype)
    return out
```

```python
from contextlib import ExitStack

import concourse.bass as bass
from concourse import mybir

F32 = mybir.dt.float32
BF16 = mybir.dt.bfloat16
I32 = mybir.dt.int32
U8 = mybir.dt.uint8
ACT = mybir.ActivationFunctionType
ALU = mybir.AluOpType
AX = mybir.AxisListType

P = 128
B, S, D = 16, 256, 128
S2 = 1601
QT = S // P
NT = B * QT
TOK = B * S
H, HD = 16, 8
NPAIR = H // 2
KT = (S2 + P - 1) // P
LAST = S2 - (KT - 1) * P
LN_EPS = 1e-5
MAGIC = 12582912.0
BIG = float(2 ** 100)
NTERM = 6
Q_PART = (0, 0, 1, 1, 0, 2)
K_PART = (0, 1, 0, 1, 2, 0)


class Count:

    def __init__(self, r, a, c):
        self.r, self.a, self.c = r, a, c

    def __add__(self, n):
        return Count(self.r, self.a, self.c + n)

    def __sub__(self, n):
        return self + -n

    def __mul__(self, n):
        return Count(self.r, self.a * n, self.c * n)

    def half(self):
        return Count(self.r, self.a // 2, self.c // 2)

    @property
    def v(self):
        if self.r is None or self.a == 0:
            return self.c
        x = self.r * self.a if self.a != 1 else self.r
        return x + self.c if self.c else x


def wait(engine, sem, count):
    if count.r is None and count.c <= 0:
        return
    engine.wait_ge(sem, count.v)


def own_wait(engine, sem, count, passed):
    wait(engine, sem, count)
    if count.r is not None:
        engine.sem_inc(passed, 1)


def rows_of(t):
    return P if t < KT - 1 else LAST


class Scope:

    def __init__(self, nc, stage):
        self.nc, self.stage, self.stack, self.sems = nc, stage, ExitStack(), []

    def __enter__(self):
        self.stack.__enter__()
        return self

    def __exit__(self, *e):
        self.stack.__exit__(*e)
        if self.sems and e[0] is None:
            self.nc.clear_and_free_semaphores(self.sems)
            self.nc.all_engine_barrier()

    def sb(self, name, shape, dt=F32):
        return self.stack.enter_context(self.nc.sbuf_tensor(f"{self.stage}_{name}", shape, dt))

    def ps(self, name, shape, dt=F32):
        return self.stack.enter_context(self.nc.psum_tensor(f"{self.stage}_{name}", shape, dt))

    def sem(self, name):
        self.sems.append(self.nc.alloc_semaphore(name=f"{self.stage}_{name}"))
        return self.sems[-1]

    def block(self):
        return self.stack.enter_context(self.nc.Block())


def constants_stage(nc, A, R):
    with Scope(nc, "const") as sc:
        made = sc.sem("made")
        x_loaded = sc.sem("x_loaded")
        block = sc.block()

        @block.sync
        def _(sp):
            sp.dma_start(R["X"][:, :, :], A["x"].rearrange("(n p) d -> p n d", p=P)).then_inc(x_loaded, 16)
            sp.wait_ge(x_loaded, 16)

        @block.gpsimd
        def _(pool):
            nc.gpsimd.memset(R["ident"][:, :], 0.0).then_inc(made, 1)
            nc.gpsimd.memset(R["identb"][:, :], 0.0).then_inc(made, 1)
            pool.wait_ge(made, 2)
            for m in (R["ident"], R["identb"]):
                nc.gpsimd.affine_select(out=m[:, :], in_=m[:, :], compare_op=ALU.not_equal, fill=1.0,
                                        base=0, pattern=[[-1, P]], channel_multiplier=1).then_inc(made, 1)
            pool.wait_ge(made, 4)


def layernorm_stage(nc, stage, R, XT=None, XN=None, XR=None):
    G = 4
    X = R["X"]
    with Scope(nc, stage) as sc:
        st = sc.sb("st", [P, NT, 6])
        mv = sc.sb("mv", [P, NT, 2])
        sd = sc.sb("sd", [P, NT])
        rstd = sc.sb("rstd", [P, NT])
        nmr = sc.sb("nmr", [P, NT])
        eps = sc.sb("eps", [P, 1])
        xn = None if XT is None else sc.sb("xn", [P, 2, G, D])
        tp = [sc.ps(f"tp{i}", [P, G * P]) for i in range(2)] if XT is not None else None
        if XR is not None:
            rp = [sc.ps(f"rp{i}", [P, G * P]) for i in range(2)]
            flip = sc.sb("flip", [P, P])
            flip_made = sc.sem("flip_made")
        eps_set, stats, aggr, root, scaled = (sc.sem(n) for n in ("eps_set", "stats", "aggr", "root", "scaled"))
        normed, turned, kept = (sc.sem(n) for n in ("normed", "turned", "kept"))
        block = sc.block()
        NG = NT // G

        @block.vector
        def _(dve):
            nc.vector.memset(eps[:, :], LN_EPS).then_inc(eps_set, 1)
            with dve.Fori(0, NT) as n:
                nc.vector.bn_stats(st[:, n, :], X[:, n, :]).then_inc(stats, 1)
            for n in range(NT):
                dve.wait_ge(stats, n + 1)
                nc.vector.bn_aggr(mv[:, n, :], st[:, n, :]).then_inc(aggr, 1)
            dve.wait_ge(root, 1)
            nc.vector.reciprocal(rstd[:, :], sd[:, :]).then_inc(scaled, 1)
            dve.wait_ge(scaled, 1)
            nc.vector.scalar_tensor_tensor(out=nmr[:, :], in0=mv[:, :, 0], scalar=-1.0, in1=rstd[:, :],
                                           op0=ALU.mult, op1=ALU.mult).then_inc(scaled, 1)
            if XT is not None:
                with dve.Fori(0, NG // 2) as g2:
                    for u in range(2):
                        dve.wait_ge(turned, g2 * 2 + u + 1)
                        if XR is not None:
                            nc.vector.tensor_copy(XR[:, bass.ts(g2 * 2 + u, G * P)], rp[u][:, :])
                        nc.vector.tensor_copy(XT[:, bass.ts(g2 * 2 + u, G * P)], tp[u][:, :]).then_inc(kept, 1)

        @block.scalar
        def _(act):
            act.wait_ge(eps_set, 1)
            act.wait_ge(aggr, NT)
            nc.scalar.activation(sd[:, :], mv[:, :, 1], ACT.Sqrt, bias=eps[:, 0:1]).then_inc(root, 1)
            act.wait_ge(scaled, 2)
            if XT is None:
                with act.Fori(0, NT) as n:
                    nc.scalar.activation(XN[:, n, :], X[:, n, :], ACT.Identity, scale=rstd[:, bass.ts(n, 1)],
                                         bias=nmr[:, bass.ts(n, 1)]).then_inc(normed, 1)
            else:
                def normalise(g, u):
                    for k in range(G):
                        n = g * G + k
                        last = nc.scalar.activation(xn[:, u, k, :], X[:, n, :], ACT.Identity,
                                                    scale=rstd[:, bass.ts(n, 1)], bias=nmr[:, bass.ts(n, 1)])
                    last.then_inc(normed, 1)

                for g in range(2):
                    normalise(g, g)
                with act.Fori(1, NG // 2) as g2:
                    for u in range(2):
                        act.wait_ge(turned, g2 * 2 + u - 1)
                        normalise(g2 * 2 + u, u)

        if XR is not None:
            @block.gpsimd
            def _(pool):
                nc.gpsimd.memset(flip[:, :], 0.0).then_inc(flip_made, 1)
                pool.wait_ge(flip_made, 1)
                nc.gpsimd.affine_select(out=flip[:, :], in_=flip[:, :], compare_op=ALU.not_equal, fill=1.0,
                                        base=1 - P, pattern=[[1, P]], channel_multiplier=1).then_inc(flip_made, 1)

        if XT is not None:
            @block.tensor
            def _(pe):
                def turn(g, u):
                    pe.wait_ge(normed, g + 1)
                    for k in range(G):
                        last = nc.tensor.transpose(tp[u][:, k * P:(k + 1) * P], xn[:, u, k, :], R["ident"][:, :])
                        if XR is not None:
                            last = nc.tensor.matmul(rp[u][:, k * P:(k + 1) * P], xn[:, u, k, :], flip[:, :],
                                                    start=True, stop=True)
                    last.then_inc(turned, 1)

                if XR is not None:
                    pe.wait_ge(flip_made, 2)

                for g in range(2):
                    turn(g, g)
                with pe.Fori(1, NG // 2) as g2:
                    for u in range(2):
                        pe.wait_ge(kept, g2 * 2 + u - 1)
                        turn(g2 * 2 + u, u)


def head_operands_stage(nc, stage, XT, wq, bq, qs, parts=Q_PART):
    C = 512
    NC = TOK // C
    with Scope(nc, stage) as sc:
        w = sc.sb("w", [D, D])
        b = sc.sb("b", [D, 1])
        q = sc.sb("q", [P, 2, C])
        part = [sc.sb(f"part{k}", [P, 2, C], BF16) for k in range(3)]
        ps = [sc.ps(f"ps{u}", [P, C]) for u in range(2)]
        w_loaded, proj, biased, step = (sc.sem(n) for n in ("w_loaded", "proj", "biased", "step"))
        stored = [sc.sem(f"stored{u}") for u in range(2)]
        passed = sc.sem("passed")
        block = sc.block()
        NW = 16 if bq is None else 32
        NSTEP = 4

        @block.sync
        def _(sp):
            sp.dma_start(w[:, :], wq).then_inc(w_loaded, 16)
            if bq is not None:
                sp.dma_start(b[:, :], bq).then_inc(w_loaded, 16)
            with sp.Fori(0, NC // 2) as c2:
                for u in range(2):
                    c = c2 * 2 + u
                    sp.wait_ge(step, NSTEP * c + NSTEP)
                    sp.sem_inc(passed, 1)
                    for t in range(NTERM):
                        sp.dma_start(qs[:, t, bass.ts(c, C)], part[parts[t]][:, u, :]).then_inc(stored[u], 16)
            for u in range(2):
                sp.wait_ge(stored[u], 16 * NTERM * NC // 2)

        @block.tensor
        def _(pe):
            def project(c, u):
                nc.tensor.matmul(ps[u][:, :], w[:, :], XT[:, bass.ts(c, C)], start=True, stop=True).then_inc(proj, 1)

            pe.wait_ge(w_loaded, NW)
            for c in range(2):
                project(c, c)
            with pe.Fori(1, NC // 2) as c2:
                for u in range(2):
                    pe.wait_ge(biased, c2 * 2 + u - 1)
                    project(c2 * 2 + u, u)

        @block.scalar
        def _(act):
            def add_bias(c, u):
                act.wait_ge(proj, c + 1)
                nc.scalar.activation(q[:, u, :], ps[u][:, :], ACT.Identity,
                                     bias=0.0 if bq is None else b[:, 0:1]).then_inc(biased, 1)

            act.wait_ge(w_loaded, NW)
            for c in range(2):
                add_bias(c, c)
            with act.Fori(1, NC // 2) as c2:
                for u in range(2):
                    act.wait_ge(step, NSTEP * (c2 * 2 + u - 1))
                    add_bias(c2 * 2 + u, u)

        @block.vector
        def _(dve):
            def split(c, u):
                dve.wait_ge(biased, c + 1)
                nc.vector.tensor_copy(part[0][:, u, :], q[:, u, :]).then_inc(step, 1)
                dve.wait_ge(step, NSTEP * c + 1)
                nc.vector.tensor_tensor(q[:, u, :], q[:, u, :], part[0][:, u, :], ALU.subtract).then_inc(step, 1)
                dve.wait_ge(step, NSTEP * c + 2)
                nc.vector.tensor_copy(part[1][:, u, :], q[:, u, :]).then_inc(step, 1)
                dve.wait_ge(step, NSTEP * c + 3)
                nc.vector.tensor_tensor(part[2][:, u, :], q[:, u, :], part[1][:, u, :], ALU.subtract).then_inc(step, 1)

            for c in range(2):
                split(c, c)
            with dve.Fori(1, NC // 2) as c2:
                for u in range(2):
                    dve.wait_ge(stored[u], 16 * NTERM * c2)
                    split(c2 * 2 + u, u)



NQUAD = H // 4
NSLOT = NQUAD * KT
CH = 401
CSTEP = 400
NCH = H * QT * 4
HALF = NPAIR // 2
SHARED = {
    (0, 3): ("turn_o", 3), (0, 5): ("turn_on", 0), (0, 7): ("out_proj", 0), (0, 9): ("turn_max", 1),
    (0, 11): ("k", 0), (1, 1): ("k", 1), (1, 3): ("turn_o", 0), (1, 5): ("k", 2), (1, 7): ("k", 3),
    (1, 9): ("v", 0), (1, 11): ("v", 1), (2, 1): ("v", 2), (2, 3): ("turn_o", 1), (2, 5): ("v", 3),
    (2, 9): ("turn_max", 0), (3, 3): ("turn_o", 2),
}
PER_BATCH = {"turn_o": 4, "turn_on": 1, "out_proj": 1, "turn_max": 2, "k": 4, "v": 4}


class Step:

    def __init__(self, i, parity, fin=True, exp=True, top=True, prep=True):
        self.i, self.u = i, parity
        self.fin, self.exp, self.top, self.prep = fin, exp, top, prep

    def use(self, kind, n):
        if kind in ("turn_on", "out_proj") or (kind, n) == ("turn_o", 3):
            return self.fin, self.i - 1
        if kind == "turn_o" or (kind, n) == ("turn_max", 1):
            return self.exp, self.i
        if kind in ("v", "turn_max"):
            return self.top, self.i + 1
        return self.prep, self.i + 2

    def shared(self, slot):
        e = SHARED.get(divmod(slot, KT))
        return e if e and self.use(*e)[0] else None

    def before(self, slot):
        for at in range(slot - 1, -1, -1):
            if self.shared(at):
                return self.shared(at), self.use(*self.shared(at))[1]
        return ((("turn_o", 2), self.i - 1) if self.fin else (("turn_max", 0), self.i))


def run_steps(engine, emit):
    def at(i):
        return Count(None, 0, i)

    emit(Step(at(-2), 0, fin=False, exp=False, top=False))
    emit(Step(at(-1), 1, fin=False, exp=False))
    emit(Step(at(0), 0, fin=False))
    with engine.Fori(0, 6) as r:
        for v in range(2):
            emit(Step(Count(r, 2, 1 + v), (1 + v) % 2))
    emit(Step(at(13), 1))
    emit(Step(at(14), 0, prep=False))
    emit(Step(at(15), 1, prep=False, top=False))
    emit(Step(at(16), 0, prep=False, top=False, exp=False))


def chunks_of(slot):
    return range(slot * NCH // NSLOT, (slot + 1) * NCH // NSLOT)


def chunk_place(c):
    h, qt, j = c // (4 * QT), c // 4 % QT, c % 4
    p, g = h // 2, h % 2
    return h, qt, CSTEP * j, (p // HALF) * 16 + g * 8 + (p % HALF) * QT + qt, j


K_COLS = ((0, 400), (400, 400), (800, 400), (1200, S2 - 1200))


def attention_stage(nc, stage, A, R, w, qs, ks, mrow, masked):
    SCALE = float(HD) ** -0.5
    X = R["X"]
    with Scope(nc, stage) as sc:
        wk, wv, wo = (sc.sb(n, [D, D]) for n in ("wk", "wv", "wo"))
        bk, bv = sc.sb("bk", [D, 1]), sc.sb("bv", [D, 1])
        bo = sc.sb("bo", [P, D])
        ctx = [sc.sb(f"ctx{u}", [D, S2]) for u in range(2)]
        k32 = sc.sb("k32", [P, S2])
        kpart = [sc.sb(f"kpart{k}", [P, S2], BF16) for k in range(3)]
        K6 = [sc.sb(f"K6{u}", [P, NPAIR, S2], BF16) for u in range(2)]
        QM = [sc.sb(f"QM{u}", [P, H, S], BF16) for u in range(2)]
        QE = [sc.sb(f"QE{u}", [P, H, S], BF16) for u in range(2)]
        V = [sc.sb(f"V{u}", [P, KT, H, HD + 1]) for u in range(2)]
        E = [sc.sb(f"E{u}", [P, 2, 2 * S]) for u in range(2)]
        osb = sc.sb("osb", [P, S])
        on = sc.sb("on", [P, QT, H, HD])
        rl = sc.sb("rl", [P, QT, 4])
        oT = sc.sb("oT", [P, S])
        xo = sc.sb("xo", [P, QT, D])
        mpart = sc.sb("mpart", [P, H * QT, 4])
        negm = sc.sb("negm", [P, 2, 16])
        mhi = sc.sb("mhi", [16, P], BF16)
        mrest = sc.sb("mrest", [16, P])
        mlo = sc.sb("mlo", [16, P], BF16)
        if masked:
            mask_in = sc.sb("mask_in", [P, S2], I32)
            MB = [sc.sb(f"MB{u}", [P, QT, S2], BF16) for u in range(2)]
            MT = [sc.sb(f"MT{u}", [P, KT, S], BF16) for u in range(2)]
            junk = sc.sb("junk", [P, 2, CH], BF16)
        sc_ps = [sc.ps(f"sc{u}", [P, 2, 2 * S]) for u in range(2)]
        mx_ps = [sc.ps(f"mx{u}", [P, 512]) for u in range(2)]
        o_ps = sc.ps("o", [P, 512])
        sh_ps = sc.ps("sh", [P, 512])

        w_loaded = sc.sem("w_loaded")
        cleared = sc.sem("cleared")
        ctx_loaded = [sc.sem(f"ctx_loaded{u}") for u in range(2)]
        full = {k: sc.sem(f"{k}_full") for k in PER_BATCH}
        done = {k: sc.sem(f"{k}_done") for k in PER_BATCH}
        split = sc.sem("split")
        ks_stored = sc.sem("ks_stored")
        kq_loaded = [[sc.sem(f"kq_loaded{u}{h}") for h in range(2)] for u in range(2)]
        top_full, top_done = sc.sem("top_full"), sc.sem("top_done")
        neg_done = sc.sem("neg_done")
        msplit = sc.sem("msplit")
        m_stored = sc.sem("m_stored")
        m_loaded = [sc.sem(f"m_loaded{h}") for h in range(2)]
        sc_full, exp_done, pv_done, o_done = (sc.sem(n) for n in ("sc_full", "exp_done", "pv_done", "o_done"))
        rl_done, xo_done, x_done = sc.sem("rl_done"), sc.sem("xo_done"), sc.sem("x_done")
        if masked:
            mb_loaded, mb_done, mt_loaded, mt_done = (
                sc.sem(n) for n in ("mb_loaded", "mb_done", "mt_loaded", "mt_done"))
        NDMA = 6
        o_cleared = sc.sem("o_cleared")
        passed, passed_v = sc.sem("passed"), sc.sem("passed_v")
        NCLEAR = 10
        block = sc.block()

        def count(kind, n, b):
            return b * PER_BATCH[kind] + (n + 1)

        @block.sync
        def _(sp):
            for dst, src in ((wk, "wk"), (wv, "wv"), (wo, "wo"), (bk, "bk"), (bv, "bv")):
                sp.dma_start(dst[:, :], w[src]).then_inc(w_loaded, 16)
            sp.dma_start(bo[:, :], w["bo"].partition_broadcast(P)).then_inc(w_loaded, 16)
            sp.wait_ge(cleared, NCLEAR)

            def load_half(b, u, half):
                pairs = slice(half * HALF, (half + 1) * HALF)
                for g in range(2):
                    rows = slice(64 * g, 64 * g + HD * NTERM)
                    k_src = ks[u].rearrange("(p g d) t n -> g (d t) p n", g=2, d=HD)[g]
                    sp.dma_start(K6[u][rows, pairs, :], k_src[:, pairs, :]).then_inc(kq_loaded[u][half], 16)
                    q_src = qs.rearrange("(p g d) t n -> g (d t) p n", g=2, d=HD)[g][:, pairs, bass.ts(b.v, S)]
                    for dst in (QM[u], QE[u]):
                        d = dst[rows, :, :].rearrange("r (p g) n -> r g p n", g=2)[:, g, pairs, :]
                        sp.dma_start(d, q_src).then_inc(kq_loaded[u][half], 16)

            def load_max(b, u, half):
                n = b * 2 + half
                own_wait(sp, msplit, n * 3 + 3, passed)
                for part, src in enumerate((mhi, mlo)):
                    sp.dma_start(mrow[half, part], src[:, :]).then_inc(m_stored, 16)
                own_wait(sp, m_stored, n * 32 + 32, passed)
                pairs = slice(half * HALF, (half + 1) * HALF)
                for g in range(2):
                    row = 64 * g + HD * NTERM
                    d = QE[u][row:row + 2, :, :].rearrange("r (p g) n -> r g p n", g=2)[:, g, pairs, :]
                    src = mrow[half].rearrange("a (g p q) n -> a g p (q n)", g=2, q=QT)[:, g]
                    sp.dma_start(d, src).then_inc(m_loaded[half], 16)

            def emit(s):
                if s.prep:
                    b = s.i + 2
                    own_wait(sp, full["v"], (b - 1) * 4, passed)
                    sp.dma_start(ctx[s.u][:, :], A["ctxT"][b.v]).then_inc(ctx_loaded[s.u], 16)
                if s.top:
                    b = s.i + 1
                    own_wait(sp, sc_full, s.i * NSLOT, passed)
                    load_half(b, 1 - s.u, 1)
                if s.exp:
                    load_max(s.i, s.u, 1)
                if s.prep:
                    b = s.i + 2
                    own_wait(sp, split, b * 4 + 4, passed)
                    own_wait(sp, kq_loaded[s.u][1], b.half() * (16 * NDMA), passed)
                    for t in range(NTERM):
                        sp.dma_start(ks[s.u][:, t, :], kpart[K_PART[t]][:, :]).then_inc(ks_stored, 16)
                    own_wait(sp, ks_stored, b * (16 * NTERM) + 16 * NTERM, passed)
                    own_wait(sp, sc_full, s.i * NSLOT + 2 * KT, passed)
                    load_half(b, s.u, 0)
                if s.top:
                    load_max(s.i + 1, 1 - s.u, 0)

            run_steps(sp, emit)

        @block.gpsimd
        def _(pool):
            for t in QM + QE:
                nc.gpsimd.memset(t[:, :, :], 0.0).then_inc(cleared, 1)
            for t in V:
                nc.gpsimd.memset(t[:, :, :, :], 1.0).then_inc(cleared, 1)
            pool.wait_ge(cleared, 6)
            for t in K6:
                for row in (32, 96):
                    nc.gpsimd.memset(t[row:row + 32, :, :], 1.0).then_inc(cleared, 1)

            def convert(dst, cols, rows, sem):
                nc.gpsimd.tensor_scalar(dst, cols[0:rows], 0.0, -BIG, ALU.is_equal, ALU.mult).then_inc(sem, 1)

            def emit(s):
                if s.prep:
                    b = s.i + 2
                    own_wait(pool, done["k"], count("k", 3, b), passed)
                    own_wait(pool, ks_stored, b * (16 * NTERM), passed)
                    nc.gpsimd.tensor_copy(kpart[0][:, :], k32[:, :]).then_inc(split, 1)
                    own_wait(pool, split, b * 4 + 1, passed)
                    nc.gpsimd.tensor_tensor(k32[:, :], k32[:, :], kpart[0][:, :], ALU.subtract).then_inc(split, 1)
                    own_wait(pool, split, b * 4 + 2, passed)
                    nc.gpsimd.tensor_copy(kpart[1][:, :], k32[:, :]).then_inc(split, 1)
                    own_wait(pool, split, b * 4 + 3, passed)
                    nc.gpsimd.tensor_tensor(kpart[2][:, :], k32[:, :], kpart[1][:, :], ALU.subtract).then_inc(split, 1)
                if masked and s.top:
                    b = s.i + 1
                    own_wait(pool, sc_full, s.i * NSLOT, passed)
                    view = mask_in[:, 0:6 * S].rearrange("p (t q) -> p t q", q=S)
                    for n in range(3):
                        src = A["maskT"][b.v]
                        if n < 2:
                            src = src[768 * n:768 * (n + 1), :].rearrange("(t p) q -> p t q", p=P)
                            into, dst, rows = view, MT[1 - s.u][:, 6 * n:6 * n + 6, :], P
                        else:
                            src = src[(KT - 1) * P:S2, :]
                            into, dst, rows = view[0:LAST, 0, :], MT[1 - s.u][0:LAST, KT - 1, :], LAST
                        if n:
                            own_wait(pool, mt_done, b * 3 + n, passed)
                        elif not (s.i.r is None and s.i.c == -1):
                            own_wait(pool, mb_done, b * 2 + 2, passed)
                        else:
                            pool.wait_ge(mb_done, 2)
                        pool.dma_start(into, src).then_inc(mt_loaded, 16)
                        own_wait(pool, mt_loaded, b * 48 + 16 * (n + 1), passed)
                        convert(dst, into, rows, mt_done)
                if masked and s.prep:
                    b = s.i + 2
                    own_wait(pool, top_done, (s.i + 1) * NCH, passed)
                    for n in range(QT):
                        if n:
                            own_wait(pool, mb_done, b * 2 + n, passed)
                        else:
                            own_wait(pool, mt_done, (s.i + 2) * 3, passed)
                        pool.dma_start(mask_in[:, :], A["mask"][b.v, n * P:(n + 1) * P, :]).then_inc(mb_loaded, 16)
                        own_wait(pool, mb_loaded, b * 32 + 16 * (n + 1), passed)
                        convert(MB[s.u][:, n, :], mask_in, P, mb_done)

            run_steps(pool, emit)

        @block.scalar
        def _(act):
            act.wait_ge(w_loaded, 6 * 16)
            act.wait_ge(cleared, NCLEAR)

            def exp(s, slot):
                t = slot % KT
                rows = rows_of(t)
                wait(act, sc_full, s.i * NSLOT + slot + 1)
                wait(act, pv_done, s.i * NSLOT + slot - 1)
                nc.scalar.activation(E[slot % 2][0:rows, :, :], sc_ps[slot % 2][0:rows, :, :], ACT.Exp,
                                     scale=SCALE).then_inc(exp_done, 1)

            def read_shared(s, kind, n):
                b = s.use(kind, n)[1]
                if kind == "k":
                    at, width = K_COLS[n]
                    wait(act, full["k"], count("k", n, b))
                    wait(act, split, b * 4)
                    nc.scalar.activation(k32[:, at:at + width], sh_ps[:, 0:width], ACT.Identity,
                                         bias=bk[:, 0:1]).then_inc(done["k"], 1)
                elif kind == "v":
                    wait(act, full["v"], count("v", n, b))
                    wait(act, pv_done, (b - 1) * NSLOT)
                    tiles, rows = (4, P) if n < 3 else (1, LAST)
                    nc.scalar.activation(
                        V[1 - s.u][0:rows, 4 * n:4 * n + tiles, :, 0:HD],
                        sh_ps[0:rows, 0:tiles * D].rearrange("p (t h d) -> p t h d", h=H, d=HD),
                        ACT.Copy).then_inc(done["v"], 1)
                elif kind == "turn_on":
                    wait(act, full["turn_on"], count("turn_on", 0, b))
                    nc.scalar.activation(oT[:, :], sh_ps[:, 0:S], ACT.Identity, bias=bv[:, 0:1])\
                        .then_inc(done["turn_on"], 1)

            def emit(s):
                for slot in range(NSLOT):
                    if s.exp:
                        exp(s, slot)
                    if slot and s.shared(slot - 1):
                        read_shared(s, *s.shared(slot - 1))

            run_steps(act, emit)

        @block.vector
        def _(dve):
            nc.vector.memset(o_ps[:, :], 0.0).then_inc(o_cleared, 1)
            dve.wait_ge(w_loaded, 6 * 16)

            def row_max(s, c):
                b = s.i + 1
                h, qt, at, col, j = chunk_place(c)
                wait(dve, top_full, b * NCH + c + 1)
                if masked:
                    if b.r is not None:
                        dve.sem_inc(passed_v, 1)
                    nc.vector.tensor_tensor_reduce(
                        out=junk[:, c % 2, :], in0=mx_ps[c % 2][:, 0:CH], in1=MB[1 - s.u][:, qt, at:at + CH],
                        scale=1.0, scalar=-3.0e38, op0=ALU.add, op1=ALU.max,
                        accum_out=mpart[:, col, j:j + 1]).then_inc(top_done, 1)
                else:
                    nc.vector.reduce_max(mpart[:, col, j:j + 1], mx_ps[c % 2][:, 0:CH], AX.X).then_inc(top_done, 1)

            def negate_max(b, half):
                wait(dve, top_done, b * NCH + (half + 1) * NCH // 2)
                wait(dve, full["turn_max"], count("turn_max", half, b - 1))
                nc.vector.tensor_reduce(negm[:, half, :], mpart[:, 16 * half:16 * half + 16, :], axis=AX.X,
                                        op=ALU.max, negate=True).then_inc(neg_done, 1)

            def copy_o(b, quad):
                wait(dve, pv_done, b * NSLOT + (quad + 1) * KT)
                wait(dve, full["turn_o"], b * 4 + quad)
                nc.vector.tensor_copy(osb[:, :], o_ps[:, 0:S]).then_inc(o_done, 1)

            def read_shared(s, kind, n):
                b = s.use(kind, n)[1]
                if kind == "turn_o":
                    wait(dve, full[kind], count(kind, n, b))
                    o = sh_ps[:, 0:QT * P].rearrange("p (q h r) -> p q h r", q=QT, h=4)
                    nc.vector.reciprocal(rl[:, :, :], o[:, :, :, HD]).then_inc(rl_done, 1)
                    wait(dve, rl_done, b * 4 + (n + 1))
                    if n == 0:
                        wait(dve, full["turn_on"], b)
                    nc.vector.tensor_tensor(on[:, :, 4 * n:4 * n + 4, :], o[:, :, :, 0:HD],
                                            rl[:, :, :].unsqueeze(3).broadcast_to([P, QT, 4, HD]),
                                            ALU.mult).then_inc(done[kind], 1)
                elif kind == "out_proj":
                    wait(dve, full[kind], count(kind, 0, b))
                    wait(dve, x_done, b)
                    xb = X[:, bass.ds((b * QT).v, QT), :]
                    nc.vector.tensor_tensor(xo[:, :, :], sh_ps[:, 0:QT * D].rearrange("p (q d) -> p q d", q=QT),
                                            xb, ALU.add).then_inc(done[kind], 1)
                    wait(dve, done[kind], count(kind, 0, b))
                    nc.vector.tensor_tensor(xb, xo[:, :, :], bo[:, :].unsqueeze(1).broadcast_to([P, QT, D]),
                                            ALU.add).then_inc(x_done, 1)
                elif kind == "turn_max":
                    m = b * 2 + n
                    wait(dve, full[kind], count(kind, n, b))
                    wait(dve, m_stored, m * 32)
                    nc.vector.tensor_copy(mhi[:, :], sh_ps[0:16, 0:P]).then_inc(msplit, 1)
                    wait(dve, msplit, m * 3 + 1)
                    nc.vector.tensor_tensor(mrest[:, :], sh_ps[0:16, 0:P], mhi[:, :], ALU.subtract)\
                        .then_inc(msplit, 1)
                    wait(dve, msplit, m * 3 + 2)
                    nc.vector.tensor_copy(mlo[:, :], mrest[:, :]).then_inc(msplit, 1)
                    wait(dve, msplit, m * 3 + 3)
                    dve.sem_inc(done[kind], 1)

            def emit(s):
                for slot in range(NSLOT):
                    quad, t = divmod(slot, KT)
                    if s.top:
                        if masked and slot == 0:
                            wait(dve, mb_done, (s.i + 1) * 2 + 2)
                        for c in chunks_of(slot):
                            row_max(s, c)
                    if t == 0:
                        if quad == 0 and s.fin:
                            copy_o(s.i - 1, 3)
                        if quad > 0 and s.exp:
                            copy_o(s.i, quad - 1)
                    if slot == 3 and s.exp:
                        negate_max(s.i, 1)
                    if slot == 2 * KT + 3 and s.top:
                        negate_max(s.i + 1, 0)
                    if slot and s.shared(slot - 1):
                        read_shared(s, *s.shared(slot - 1))

            run_steps(dve, emit)

        @block.tensor
        def _(pe):
            pe.wait_ge(w_loaded, 6 * 16)
            pe.wait_ge(cleared, NCLEAR)
            pe.wait_ge(o_cleared, 1)

            def scores(s, slot):
                quad, t = divmod(slot, KT)
                rows = rows_of(t)
                wait(pe, exp_done, s.i * NSLOT + slot - 1)
                for e in range(2):
                    pair = 2 * quad + e
                    out = sc_ps[slot % 2][0:rows, e, :]
                    last = nc.tensor.matmul(out, K6[s.u][:, pair, t * P:t * P + rows],
                                            QE[s.u][:, 2 * pair:2 * pair + 2, :].rearrange("p h q -> p (h q)"),
                                            start=True, stop=not masked)
                    if masked:
                        last = nc.tensor.matmul(out.rearrange("p (h q) -> p h q", h=2), R["identb"][0:rows, 0:rows],
                                                MT[s.u][0:rows, t, :].unsqueeze(1).broadcast_to([rows, 2, S]),
                                                start=False, stop=True)
                last.then_inc(sc_full, 1)

            def product(s, slot):
                quad, t = divmod(slot, KT)
                rows = rows_of(t)
                wait(pe, exp_done, s.i * NSLOT + slot + 1)
                if t == 0:
                    wait(pe, o_done, s.i * 4 + quad)
                for k in range(4):
                    last = nc.tensor.matmul(o_ps[32 * k:32 * k + HD + 1, 0:S], V[s.u][0:rows, t, 4 * quad + k, :],
                                            E[slot % 2][0:rows, k // 2, (k % 2) * S:(k % 2 + 1) * S],
                                            start=(t == 0), stop=(t == KT - 1), tile_position=(0, 32 * k))
                last.then_inc(pv_done, 1)

            def top_scores(s, c):
                h, qt, at, _, _ = chunk_place(c)
                b = s.i + 1
                wait(pe, top_done, b * NCH + c - 1)
                nc.tensor.matmul(mx_ps[c % 2][:, 0:CH], QM[1 - s.u][:, h, qt * P:(qt + 1) * P],
                                 K6[1 - s.u][:, h // 2, at:at + CH], start=True, stop=True).then_inc(top_full, 1)

            def use_shared(s, slot, kind, n):
                b = s.use(kind, n)[1]
                (pk, pn), pb = s.before(slot)
                wait(pe, done[pk], count(pk, pn, pb))
                if kind == "k":
                    at, width = K_COLS[n]
                    wait(pe, ctx_loaded[s.u], b.half() * 16 + 16)
                    last = nc.tensor.matmul(sh_ps[:, 0:width], wk[:, :], ctx[s.u][:, at:at + width],
                                            start=True, stop=True)
                elif kind == "v":
                    for t in range(4 * n, min(4 * n + 4, KT)):
                        rows = rows_of(t)
                        last = nc.tensor.matmul(sh_ps[0:rows, (t % 4) * D:(t % 4 + 1) * D],
                                                ctx[1 - s.u][:, t * P:t * P + rows], wv[:, :],
                                                start=True, stop=True)
                elif kind == "turn_o":
                    wait(pe, o_done, b * 4 + (n + 1))
                    for q in range(QT):
                        last = nc.tensor.transpose(sh_ps[:, q * P:(q + 1) * P], osb[:, q * P:(q + 1) * P],
                                                   R["ident"][:, :])
                elif kind == "turn_on":
                    for q in range(QT):
                        last = nc.tensor.transpose(sh_ps[:, q * P:(q + 1) * P],
                                                   on[:, q, :, :].rearrange("p h d -> p (h d)"), R["ident"][:, :])
                elif kind == "out_proj":
                    for q in range(QT):
                        last = nc.tensor.matmul(sh_ps[:, q * D:(q + 1) * D], oT[:, q * P:(q + 1) * P], wo[:, :],
                                                start=True, stop=True)
                elif kind == "turn_max":
                    wait(pe, neg_done, b * 2 + (n + 1))
                    last = nc.tensor.transpose(sh_ps[0:16, 0:P], negm[:, n, :], R["ident"][:, :])
                last.then_inc(full[kind], 1)

            def emit(s):
                for slot in range(NSLOT):
                    chunks = list(chunks_of(slot)) if s.top else []
                    if s.exp:
                        if slot == 0:
                            wait(pe, m_loaded[0], s.i * 32 + 32)
                            wait(pe, done["v"], s.i * 4 + 4)
                            if masked:
                                wait(pe, mt_done, s.i * 3 + 3)
                        if slot == 2 * KT:
                            wait(pe, m_loaded[1], s.i * 32 + 32)
                        scores(s, slot)
                    if s.top and slot == 0:
                        wait(pe, kq_loaded[1 - s.u][0], ((s.i + 1).half() + 1) * (16 * NDMA))
                    for n, c in enumerate(chunks):
                        if c == NCH // 2:
                            wait(pe, kq_loaded[1 - s.u][1], ((s.i + 1).half() + 1) * (16 * NDMA))
                        if n == len(chunks) - 1 and s.exp and slot:
                            product(s, slot - 1)
                        top_scores(s, c)
                    if not chunks and s.exp and slot:
                        product(s, slot - 1)
                    if s.shared(slot):
                        use_shared(s, slot, *s.shared(slot))
                if s.exp:
                    product(s, NSLOT - 1)

            run_steps(pe, emit)


def scratch(nc, name, shape, dt):
    return nc.dram_tensor(name, shape, dt).ap()


def quantised_ffn_stage(nc, stage, A, R, XN):
    G = 4
    NG = NT // G
    X = R["X"]
    with Scope(nc, stage) as sc:
        rT = sc.sb("rT", [D, D])
        rscale, rinv = sc.sb("rscale", [D, 1]), sc.sb("rinv", [D, 1])
        rq = sc.sb("rq", [D, D])
        rqb = sc.sb("rqb", [D, D], BF16)
        rhs = sc.sb("rhs", [D, D], BF16)
        rrow = sc.sb("rrow", [P, D])
        amax, scale, inv = sc.sb("amax", [P, NT]), sc.sb("scale", [P, NT]), sc.sb("inv", [P, NT])
        q = sc.sb("q", [P, 2, G, D])
        qb = sc.sb("qb", [P, 2, G, D], BF16)
        qT = sc.sb("qT", [P, 2, G * P], BF16)
        y = sc.sb("y", [P, 2, G, D])
        tp = [sc.ps(f"tp{u}", [P, G * P], BF16) for u in range(2)]
        mm = [sc.ps(f"mm{u}", [P, G * D]) for u in range(2)]
        rt_ps = sc.ps("rt_ps", [D, D], BF16)
        rr_ps = sc.ps("rr_ps", [P, D])
        r_loaded, wstep, w_turned, scaled = (sc.sem(n) for n in ("r_loaded", "wstep", "w_turned", "scaled"))
        qstep, turned, kept, multiplied, ystep = (
            sc.sem(n) for n in ("qstep", "turned", "kept", "multiplied", "ystep"))
        block = sc.block()
        NQ, NY = 4, 3

        @block.sync
        def _(sp):
            sp.dma_start(rT[:, :], A["L0_rhsT"]).then_inc(r_loaded, 16)
            sp.wait_ge(r_loaded, 16)

        @block.vector
        def _(dve):
            dve.wait_ge(r_loaded, 16)
            nc.vector.tensor_reduce(rscale[:, :], rT[:, :], axis=AX.X, op=ALU.max,
                                    apply_absolute_value=True).then_inc(wstep, 1)
            dve.wait_ge(wstep, 1)
            nc.vector.tensor_scalar(rscale[:, :], rscale[:, :], 1e-12, 1.0 / 127.0, ALU.max, ALU.mult).then_inc(wstep, 1)
            dve.wait_ge(wstep, 2)
            nc.vector.reciprocal(rinv[:, :], rscale[:, :]).then_inc(wstep, 1)
            dve.wait_ge(wstep, 3)
            nc.vector.tensor_scalar(rq[:, :], rT[:, :], rinv[:, 0:1], MAGIC, ALU.mult, ALU.add).then_inc(wstep, 1)
            dve.wait_ge(wstep, 4)
            nc.vector.tensor_scalar(rq[:, :], rq[:, :], -MAGIC, 127.0, ALU.add, ALU.min).then_inc(wstep, 1)
            dve.wait_ge(wstep, 5)
            nc.vector.tensor_scalar(rqb[:, :], rq[:, :], -127.0, None, ALU.max).then_inc(wstep, 1)
            dve.wait_ge(w_turned, 1)
            nc.vector.tensor_copy(rhs[:, :], rt_ps[:, :]).then_inc(wstep, 1)
            dve.wait_ge(w_turned, 2)
            nc.vector.tensor_copy(rrow[:, :], rr_ps[:, :]).then_inc(wstep, 1)
            nc.vector.tensor_reduce(amax[:, :], XN[:, :, :], axis=AX.X, op=ALU.max,
                                    apply_absolute_value=True).then_inc(scaled, 1)
            dve.wait_ge(scaled, 1)
            nc.vector.tensor_scalar(scale[:, :], amax[:, :], 1e-12, 1.0 / 127.0, ALU.max, ALU.mult).then_inc(scaled, 1)
            dve.wait_ge(scaled, 2)
            nc.vector.reciprocal(inv[:, :], scale[:, :]).then_inc(scaled, 1)
            dve.wait_ge(scaled, 3)
            dve.wait_ge(wstep, 8)

            def quantise(g, u):
                nc.vector.tensor_tensor(q[:, u, :, :], XN[:, bass.ds((g * G).v, G), :],
                                        inv[:, bass.ds((g * G).v, G)].unsqueeze(2).broadcast_to([P, G, D]),
                                        ALU.mult).then_inc(qstep, 1)
                wait(dve, qstep, g * NQ + 1)
                nc.vector.tensor_scalar(q[:, u, :, :], q[:, u, :, :], MAGIC, -MAGIC, ALU.add, ALU.add).then_inc(qstep, 1)
                wait(dve, qstep, g * NQ + 2)
                wait(dve, turned, g - 1)
                nc.vector.tensor_scalar(qb[:, u, :, :], q[:, u, :, :], -127.0, 127.0, ALU.max, ALU.min).then_inc(qstep, 1)
                wait(dve, qstep, g * NQ + 3)
                dve.sem_inc(qstep, 1)

            def add(g, u):
                wait(dve, multiplied, g + 1)
                nc.vector.tensor_tensor(y[:, u, :, :], mm[u][:, :].rearrange("p (g d) -> p g d", g=G),
                                        scale[:, bass.ds((g * G).v, G)].unsqueeze(2).broadcast_to([P, G, D]),
                                        ALU.mult).then_inc(ystep, 1)
                wait(dve, ystep, g * NY + 1)
                nc.vector.tensor_tensor(y[:, u, :, :], y[:, u, :, :], rrow[:, :].unsqueeze(1).broadcast_to([P, G, D]),
                                        ALU.mult).then_inc(ystep, 1)
                wait(dve, ystep, g * NY + 2)
                xg = X[:, bass.ds((g * G).v, G), :]
                nc.vector.tensor_tensor(xg, xg, y[:, u, :, :], ALU.add).then_inc(ystep, 1)

            quantise(Count(None, 0, 0), 0)
            quantise(Count(None, 0, 1), 1)
            with dve.Fori(0, NG // 2 - 1) as r:
                for u in range(2):
                    quantise(Count(r, 2, 2 + u), u)
                    add(Count(r, 2, u), u)
            for u in range(2):
                add(Count(None, 0, NG - 2 + u), u)

        @block.tensor
        def _(pe):
            pe.wait_ge(wstep, 6)
            nc.tensor.transpose(rt_ps[:, :], rqb[:, :], R["identb"][:, :]).then_inc(w_turned, 1)
            nc.tensor.matmul(rr_ps[:, :], rscale[:, 0:1].broadcast_to([D, P]), R["ident"][:, :],
                             start=True, stop=True).then_inc(w_turned, 1)
            pe.wait_ge(wstep, 8)

            def turn(g, u):
                wait(pe, qstep, g * NQ + NQ)
                wait(pe, kept, g - 1)
                for k in range(G):
                    last = nc.tensor.transpose(tp[u][:, k * P:(k + 1) * P], qb[:, u, k, :], R["identb"][:, :])
                last.then_inc(turned, 1)

            def multiply(g, u):
                wait(pe, kept, g + 1)
                wait(pe, ystep, g * NY - (2 * NY - 1))
                for k in range(G):
                    last = nc.tensor.matmul(mm[u][:, k * D:(k + 1) * D], qT[:, u, k * P:(k + 1) * P], rhs[:, :],
                                            start=True, stop=True)
                last.then_inc(multiplied, 1)

            turn(Count(None, 0, 0), 0)
            turn(Count(None, 0, 1), 1)
            multiply(Count(None, 0, 0), 0)
            multiply(Count(None, 0, 1), 1)
            with pe.Fori(1, NG // 2) as r:
                for u in range(2):
                    turn(Count(r, 2, u), u)
                    multiply(Count(r, 2, u), u)

        @block.scalar
        def _(act):
            def keep(g, u):
                wait(act, turned, g + 1)
                wait(act, multiplied, g - 1)
                nc.scalar.activation(qT[:, u, :], tp[u][:, :], ACT.Copy).then_inc(kept, 1)

            keep(Count(None, 0, 0), 0)
            keep(Count(None, 0, 1), 1)
            with act.Fori(1, NG // 2) as r:
                for u in range(2):
                    keep(Count(r, 2, u), u)


NE = 8
DFF = 512
NF = DFF // P


def first_of(nc, link, out, values, top, rank, tmp, red):
    shape = [P, NT, NE]
    link(nc.vector.tensor_tensor(tmp[:, :, :], values, top.unsqueeze(2).broadcast_to(shape), ALU.is_equal))
    link(nc.vector.tensor_tensor(tmp[:, :, :], tmp[:, :, :], rank[:, :].unsqueeze(1).broadcast_to(shape), ALU.mult))
    link(nc.vector.tensor_reduce(red[:, :], tmp[:, :, :], axis=AX.X, op=ALU.max))
    link(nc.vector.tensor_tensor(out, tmp[:, :, :], red[:, :].unsqueeze(2).broadcast_to(shape), ALU.is_equal))


def top1_router_stage(nc, stage, A, R, XT, coef):
    X = R["X"]
    with Scope(nc, stage) as sc:
        wr = sc.sb("wr", [D, NE])
        br = sc.sb("br", [P, NE])
        b2 = sc.sb("b2", [NE, D])
        rank = sc.sb("rank", [P, NE])
        lg, ex, tmp = (sc.sb(n, [P, NT, NE]) for n in ("lg", "ex", "tmp"))
        top, total, gate, red = (sc.sb(n, [P, NT]) for n in ("top", "total", "gate", "red"))
        cT = sc.sb("cT", [NE, 2, P])
        lg_ps = sc.ps("lg_ps", [P, NT, NE])
        ct_ps = [sc.ps(f"ct_ps{u}", [NE, P]) for u in range(2)]
        y_ps = [sc.ps(f"y_ps{u}", [P, D]) for u in range(2)]
        loaded, ranked, logits, step, lowered, exps, turned, kept, product, added = (
            sc.sem(n) for n in ("loaded", "ranked", "logits", "step", "lowered", "exps", "turned", "kept",
                                "product", "added"))
        block = sc.block()

        @block.sync
        def _(sp):
            sp.dma_start(wr[:, :], A["L1_Wr"]).then_inc(loaded, 16)
            sp.dma_start(br[:, :], A["L1_br"].partition_broadcast(P)).then_inc(loaded, 16)
            sp.dma_start(b2[:, :], A["L1_b2"]).then_inc(loaded, 16)

        @block.gpsimd
        def _(pool):
            for e in range(NE):
                nc.gpsimd.memset(rank[:, e:e + 1], float(NE - e)).then_inc(ranked, 1)

        @block.tensor
        def _(pe):
            pe.wait_ge(loaded, 48)
            for n in range(NT):
                last = nc.tensor.matmul(lg_ps[:, n, :], XT[:, n * P:(n + 1) * P], wr[:, :], start=True, stop=True)
            last.then_inc(logits, 1)
            pe.wait_ge(step, 100)
            for n in range(NT):
                u = n % 2
                if n >= 2:
                    pe.wait_ge(kept, n - 1)
                nc.tensor.transpose(ct_ps[u][:, :], coef[:, n, :], R["ident"][:, :]).then_inc(turned, 1)
                pe.wait_ge(kept, n + 1)
                if n >= 2:
                    pe.wait_ge(added, n - 1)
                nc.tensor.matmul(y_ps[u][:, :], cT[:, u, :], b2[:, :], start=True, stop=True).then_inc(product, 1)

        @block.scalar
        def _(act):
            act.wait_ge(lowered, 1)
            nc.scalar.activation(ex[:, :, :], lg[:, :, :], ACT.Exp).then_inc(exps, 1)
            for n in range(NT):
                act.wait_ge(turned, n + 1)
                if n >= 2:
                    act.wait_ge(product, n - 1)
                nc.scalar.activation(cT[:, n % 2, :], ct_ps[n % 2][:, :], ACT.Copy).then_inc(kept, 1)

        @block.vector
        def _(dve):
            shape = [P, NT, NE]
            links = [0]

            def link(ins):
                links[0] += 1
                ins.then_inc(step, 1)
                dve.wait_ge(step, links[0])

            dve.wait_ge(logits, 1)
            dve.wait_ge(loaded, 48)
            dve.wait_ge(ranked, NE)
            link(nc.vector.tensor_tensor(lg[:, :, :], lg_ps[:, :, :], br[:, :].unsqueeze(1).broadcast_to(shape), ALU.add))
            link(nc.vector.reduce_max(top[:, :], lg[:, :, :], AX.X))
            link(nc.vector.tensor_tensor(lg[:, :, :], lg[:, :, :], top[:, :].unsqueeze(2).broadcast_to(shape), ALU.subtract))
            dve.sem_inc(lowered, 1)
            dve.wait_ge(exps, 1)
            link(nc.vector.reduce_sum(total[:, :], ex[:, :, :], AX.X))
            link(nc.vector.reciprocal(gate[:, :], total[:, :]))
            link(nc.vector.reduce_max(top[:, :], ex[:, :, :], AX.X))
            first_of(nc, link, coef[:, :, :], ex[:, :, :], top[:, :], rank, tmp, red)
            link(nc.vector.tensor_tensor(gate[:, :], gate[:, :], top[:, :], ALU.mult))
            link(nc.vector.tensor_tensor(coef[:, :, :], coef[:, :, :], gate[:, :].unsqueeze(2).broadcast_to(shape), ALU.mult))
            dve.sem_inc(step, 100 - links[0])
            for n in range(NT):
                dve.wait_ge(product, n + 1)
                nc.vector.tensor_tensor(X[:, n, :], X[:, n, :], y_ps[n % 2][:, :], ALU.add).then_inc(added, 1)


def top2_router_stage(nc, stage, A, R, XT, coef):
    SHARE = 2 * TOK // NE
    with Scope(nc, stage) as sc:
        wr = sc.sb("wr", [D, NE])
        rank = sc.sb("rank", [P, NE])
        edge = sc.sb("edge", [P, NE + 1])
        before = sc.sb("before", [P, P])
        ones = sc.sb("ones", [P, P])
        lg, tmp, chosen, pos, t0, t1 = (sc.sb(n, [P, NT, NE]) for n in ("lg", "tmp", "chosen", "pos", "t0", "t1"))
        pick = [sc.sb(f"pick{k}", [P, NT, NE]) for k in range(2)]
        top = [sc.sb(f"top{k}", [P, NT]) for k in range(2)]
        at = [sc.sb(f"at{k}", [P, NT]) for k in range(2)]
        weight = [sc.sb(f"weight{k}", [P, NT]) for k in range(2)]
        red, gap, eg = (sc.sb(n, [P, NT]) for n in ("red", "gap", "eg"))
        over = sc.sb("over", [P, NT, NE + 1])
        tot = [sc.sb(f"tot{k}", [P, NE]) for k in range(2)]
        lg_ps = sc.ps("lg_ps", [P, NT, NE])
        ahead_ps = sc.ps("ahead_ps", [P, NT, NE])
        sum_ps = sc.ps("sum_ps", [P, NT, NE])
        loaded, made, logits, step, picked, counted, gapped, exps = (
            sc.sem(n) for n in ("loaded", "made", "logits", "step", "picked", "counted", "gapped", "exps"))
        block = sc.block()

        @block.sync
        def _(sp):
            sp.dma_start(wr[:, :], A["L2_Wr"]).then_inc(loaded, 16)

        @block.gpsimd
        def _(pool):
            for e in range(NE):
                nc.gpsimd.memset(rank[:, e:e + 1], float(NE - e)).then_inc(made, 1)
            for e in range(NE + 1):
                nc.gpsimd.memset(edge[:, e:e + 1], float(SHARE * e)).then_inc(made, 1)
            nc.gpsimd.memset(ones[:, :], 1.0).then_inc(made, 1)
            pool.wait_ge(made, 2 * NE + 2)
            nc.gpsimd.affine_select(out=before[:, :], in_=ones[:, :], compare_op=ALU.is_ge, fill=0.0, base=-1,
                                    pattern=[[1, P]], channel_multiplier=-1).then_inc(made, 1)

        @block.tensor
        def _(pe):
            pe.wait_ge(loaded, 16)
            for n in range(NT):
                last = nc.tensor.matmul(lg_ps[:, n, :], XT[:, n * P:(n + 1) * P], wr[:, :], start=True, stop=True)
            last.then_inc(logits, 1)
            pe.wait_ge(made, 2 * NE + 3)
            pe.wait_ge(picked, 1)
            nc.tensor.matmul(ahead_ps[:, :, :], before[:, :], chosen[:, :, :], start=True, stop=True)
            nc.tensor.matmul(sum_ps[:, :, :], ones[:, :], chosen[:, :, :], start=True, stop=True).then_inc(counted, 1)

        @block.scalar
        def _(act):
            act.wait_ge(gapped, 1)
            nc.scalar.activation(eg[:, :], gap[:, :], ACT.Exp).then_inc(exps, 1)

        @block.vector
        def _(dve):
            shape = [P, NT, NE]
            links = [0]

            def link(ins):
                links[0] += 1
                ins.then_inc(step, 1)
                dve.wait_ge(step, links[0])

            def tt(out, a, b, op):
                link(nc.vector.tensor_tensor(out, a, b, op))

            dve.wait_ge(made, 2 * NE + 3)
            dve.wait_ge(logits, 1)
            link(nc.vector.tensor_copy(lg[:, :, :], lg_ps[:, :, :]))
            link(nc.vector.reduce_max(top[0][:, :], lg[:, :, :], AX.X))
            first_of(nc, link, pick[0][:, :, :], lg[:, :, :], top[0][:, :], rank, tmp, red)
            link(nc.vector.scalar_tensor_tensor(out=lg[:, :, :], in0=pick[0][:, :, :], scalar=-BIG, in1=lg[:, :, :],
                                                op0=ALU.mult, op1=ALU.add))
            link(nc.vector.reduce_max(top[1][:, :], lg[:, :, :], AX.X))
            first_of(nc, link, pick[1][:, :, :], lg[:, :, :], top[1][:, :], rank, tmp, red)
            tt(chosen[:, :, :], pick[0][:, :, :], pick[1][:, :, :], ALU.add)
            dve.sem_inc(picked, 1)
            tt(gap[:, :], top[1][:, :], top[0][:, :], ALU.subtract)
            dve.sem_inc(gapped, 1)
            dve.wait_ge(exps, 1)
            link(nc.vector.tensor_scalar(weight[1][:, :], eg[:, :], 1.0, None, ALU.add))
            link(nc.vector.reciprocal(weight[0][:, :], weight[1][:, :]))
            tt(weight[1][:, :], eg[:, :], weight[0][:, :], ALU.mult)
            dve.wait_ge(counted, 1)
            link(nc.vector.memset(t0[:, 0:1, :], 0.0))
            link(nc.vector.tensor_copy(t0[:, 1:NT, :], sum_ps[:, 0:NT - 1, :]))
            a, b = t0, t1
            for d in (1, 2, 4, 8, 16):
                link(nc.vector.tensor_copy(b[:, 0:d, :], a[:, 0:d, :]))
                tt(b[:, d:NT, :], a[:, d:NT, :], a[:, 0:NT - d, :], ALU.add)
                a, b = b, a
            tt(pos[:, :, :], ahead_ps[:, :, :], a[:, :, :], ALU.add)
            tt(tmp[:, 0, :], a[:, NT - 1, :], sum_ps[:, NT - 1, :], ALU.add)
            link(nc.vector.memset(tot[0][:, 0:1], 0.0))
            link(nc.vector.tensor_copy(tot[0][:, 1:NE], tmp[:, 0, 0:NE - 1]))
            a, b = tot
            for d in (1, 2, 4):
                link(nc.vector.tensor_copy(b[:, 0:d], a[:, 0:d]))
                tt(b[:, d:NE], a[:, d:NE], a[:, 0:NE - d], ALU.add)
                a, b = b, a
            tt(pos[:, :, :], pos[:, :, :], a[:, :].unsqueeze(1).broadcast_to(shape), ALU.add)
            for k in range(2):
                tt(tmp[:, :, :], pick[k][:, :, :], pos[:, :, :], ALU.mult)
                link(nc.vector.reduce_sum(at[k][:, :], tmp[:, :, :], AX.X))
                wide = [P, NT, NE + 1]
                tt(over[:, :, :], at[k][:, :].unsqueeze(2).broadcast_to(wide),
                   edge[:, :].unsqueeze(1).broadcast_to(wide), ALU.is_ge)
                tt(tmp[:, :, :], over[:, :, 0:NE], over[:, :, 1:NE + 1], ALU.subtract)
                tt((coef if k == 0 else tmp)[:, :, :], tmp[:, :, :],
                   weight[k][:, :].unsqueeze(2).broadcast_to(shape), ALU.mult)
            tt(coef[:, :, :], coef[:, :, :], tmp[:, :, :], ALU.add)


def expert_ffn_stage(nc, stage, R, XT, coef, W1, W2, b1, func):
    X = R["X"]
    C = 512
    NC = TOK // C
    TC = C // P
    with Scope(nc, stage) as sc:
        w1 = [sc.sb(f"w1{u}", [D, DFF]) for u in range(2)]
        w2 = [sc.sb(f"w2{u}", [P, NF, D]) for u in range(2)]
        bias = [sc.sb(f"bias{u}", [P, NF]) for u in range(2)]
        h = [sc.sb(f"h{u}", [P, NF, C]) for u in range(2)]
        h_ps = [sc.ps(f"h_ps{f}", [P, C]) for f in range(NF)]
        y_ps = [sc.ps(f"y_ps{u}", [P, TC, D]) for u in range(2)]
        w_loaded = [sc.sem(f"w_loaded{u}") for u in range(2)]
        hidden, acted, product, added = (sc.sem(n) for n in ("hidden", "acted", "product", "added"))
        NLOAD = 16 * (2 if b1 is None else 3)
        passed = sc.sem("passed")
        block = sc.block()

        @block.sync
        def _(sp):
            def load(e, v):
                sp.dma_start(w1[v][:, :], W1[e.v]).then_inc(w_loaded[v], 16)
                sp.dma_start(w2[v][:, :, :], W2[e.v].rearrange("(f p) d -> p f d", p=P)).then_inc(w_loaded[v], 16)
                if b1 is not None:
                    sp.dma_start(bias[v][:, :], b1[e.v]).then_inc(w_loaded[v], 16)

            for v in range(2):
                load(Count(None, 0, v), v)
            with sp.Fori(0, NE // 2 - 1) as r:
                for v in range(2):
                    own_wait(sp, product, Count(r, 2 * NC, (v + 1) * NC + 1), passed)
                    load(Count(r, 2, 2 + v), v)

        @block.tensor
        def _(pe):
            def up(m, v, c):
                wait(pe, w_loaded[v], Count(m.r, NLOAD, NLOAD))
                for f in range(NF):
                    wait(pe, acted, m * NF + f + 1)
                    nc.tensor.matmul(h_ps[f][:, :], w1[v][:, f * P:(f + 1) * P], XT[:, c * C:(c + 1) * C],
                                     start=True, stop=True).then_inc(hidden, 1)

            def down(m, v):
                u = m.c % 2
                wait(pe, acted, m * NF + 2 * NF)
                wait(pe, added, m)
                for k in range(TC):
                    for f in range(NF):
                        last = nc.tensor.matmul(y_ps[u][:, k, :], h[u][:, f, k * P:(k + 1) * P], w2[v][:, f, :],
                                                start=(f == 0), stop=(f == NF - 1))
                last.then_inc(product, 1)

            pe.sem_inc(product, 1)
            with pe.Fori(0, NE // 2) as r:
                for n in range(2 * NC):
                    up(Count(r, 2 * NC, n), n // NC, n % NC)
                    if n:
                        down(Count(r, 2 * NC, n - 1), (n - 1) // NC)
                down(Count(r, 2 * NC, 2 * NC - 1), 1)

        @block.scalar
        def _(act):
            act.sem_inc(acted, NF)
            with act.Fori(0, NE // 2) as r:
                for n in range(2 * NC):
                    m = Count(r, 2 * NC, n)
                    for f in range(NF):
                        wait(act, hidden, m * NF + (f + 1))
                        if f == 0:
                            wait(act, product, m)
                        at = 0.0 if b1 is None else bias[n // NC][:, f:f + 1]
                        nc.scalar.activation(h[n % 2][:, f, :], h_ps[f][:, :], func, bias=at).then_inc(acted, 1)

        @block.vector
        def _(dve):
            dve.sem_inc(added, 1)
            with dve.Fori(0, NE // 2) as r:
                for n in range(2 * NC):
                    m = Count(r, 2 * NC, n)
                    wait(dve, product, m + 2)
                    if n == 0:
                        wait(dve, added, m + 1)
                    for k in range(TC):
                        tile = n % NC * TC + k
                        e = Count(r, 2, n // NC).v
                        last = nc.vector.scalar_tensor_tensor(out=X[:, tile, :], in0=y_ps[n % 2][:, k, :],
                                                              scalar=coef[:, tile, bass.ds(e, 1)], in1=X[:, tile, :],
                                                              op0=ALU.mult, op1=ALU.add)
                    last.then_inc(added, 1)


def ternary_weights(nc, link, w, absum, total_ps, wait_total, mean, inv, out):
    n = w.shape[1] * P
    link(nc.vector.tensor_reduce(absum, w, axis=AX.X, op=ALU.add, apply_absolute_value=True))
    wait_total()
    link(nc.vector.tensor_scalar(mean, total_ps, 1.0 / n, 1e-5, ALU.mult, ALU.max))
    link(nc.vector.reciprocal(inv, mean))
    link(nc.vector.tensor_scalar(out, w, inv, MAGIC, ALU.mult, ALU.add))
    link(nc.vector.tensor_scalar(out, out, -MAGIC, 1.0, ALU.add, ALU.min))
    link(nc.vector.tensor_scalar(out, out, -1.0, None, ALU.max))


def bitnet_ffn_stage(nc, stage, A, R, XN):
    X = R["X"]
    HID = 512
    NH = HID // P
    with Scope(nc, stage) as sc:
        w1 = sc.sb("w1", [D, HID])
        w2 = sc.sb("w2", [P, NH * D])
        w2b = sc.sb("w2b", [P, NH, D], BF16)
        cw = sc.sb("cw", [P, NH, 3])
        cb = sc.sb("cb", [P, NH])
        absum, mean, minv = sc.sb("absum", [P, 2]), sc.sb("mean", [P, 2]), sc.sb("minv", [P, 2])
        ones = sc.sb("ones", [P, P])
        amax, sinv, sx = sc.sb("amax", [P, NT]), sc.sb("sinv", [P, NT]), sc.sb("sx", [P, NT])
        q = sc.sb("q", [P, 2, QT, D])
        qT = sc.sb("qT", [D, 2, S])
        c0 = sc.sb("c0", [P, NH, S])
        c1 = sc.sb("c1", [P, NH, S])
        c2 = sc.sb("c2", [P, NH, S])
        act_h = sc.sb("act_h", [P, NH, S])
        hmax, hs, hinv = (sc.sb(n, [P, QT, 2]) for n in ("hmax", "hs", "hinv"))
        hq = sc.sb("hq", [P, QT, HID])
        hqb = sc.sb("hqb", [P, QT, HID], BF16)
        hT = sc.sb("hT", [P, QT, HID], BF16)
        x_ps = sc.ps("x_ps", [P, 512])
        u_ps = [sc.ps(f"u_ps{k}", [P, 512]) for k in range(NH)]
        tot_ps = u_ps[0]
        t_ps = [sc.ps(f"t_ps{k}", [P, HID]) for k in range(QT)]
        r_ps = sc.ps("r_ps", [P, QT, HID], BF16)
        loaded, step, summed, made, tokens = (sc.sem(n) for n in ("loaded", "step", "summed", "made", "tokens"))
        qdone, qturned, qkept, up, conv0, conv, silu, hturned, hstep, hback, hkept, down, xadd = (
            sc.sem(n) for n in ("qdone", "qturned", "qkept", "up", "conv0", "conv", "silu", "hturned", "hstep",
                                "hback", "hkept", "down", "xadd"))
        block = sc.block()
        NQ, NCONV, NHS, NX = 3, 8, 8, 3

        @block.sync
        def _(sp):
            sp.dma_start(w1[:, :], A["L3_w1T"]).then_inc(loaded, 16)
            sp.dma_start(w2[:, :].rearrange("p (t d) -> p t d", t=NH), A["L3_w2T"].rearrange("(t p) d -> p t d", p=P))\
              .then_inc(loaded, 16)
            sp.dma_start(cw[:, :, :], A["L3_cw"].rearrange("(t p) k -> p t k", p=P)).then_inc(loaded, 16)
            sp.dma_start(cb[:, :], A["L3_cb"]).then_inc(loaded, 16)
            sp.wait_ge(loaded, 64)

        @block.gpsimd
        def _(pool):
            nc.gpsimd.memset(ones[:, :], 1.0).then_inc(made, 1)

        @block.tensor
        def _(pe):
            pe.wait_ge(made, 1)
            for k in range(2):
                pe.wait_ge(tokens, k + 1)
                nc.tensor.matmul(tot_ps[:, k:k + 1], ones[:, :], absum[:, k:k + 1], start=True, stop=True)\
                  .then_inc(summed, 1)
            pe.wait_ge(tokens, 3)
            with pe.Fori(0, B) as r:
                b = Count(r, 1, 0)
                wait(pe, qdone, b + 1)
                wait(pe, xadd, b * NX)
                for k in range(QT):
                    last = nc.tensor.transpose(x_ps[:, k * P:(k + 1) * P], q[:, 0, k, :], R["ident"][:, :])
                last.then_inc(qturned, 1)
                wait(pe, qkept, b + 1)
                for n in range(NH):
                    wait(pe, conv, b * NH + (n + 1))
                    nc.tensor.matmul(u_ps[n][:, 0:S], w1[:, n * P:(n + 1) * P], qT[:, 0, :],
                                     start=True, stop=True).then_inc(up, 1)
                for n in range(NH):
                    wait(pe, silu, b * NH + (n + 1))
                    for k in range(QT):
                        last = nc.tensor.transpose(t_ps[k][:, n * P:(n + 1) * P], act_h[:, n, k * P:(k + 1) * P],
                                                   R["ident"][:, :])
                last.then_inc(hturned, 1)
                wait(pe, hstep, b * NHS + NHS)
                for k in range(QT):
                    for n in range(NH):
                        last = nc.tensor.transpose(r_ps[:, k, n * P:(n + 1) * P], hqb[:, k, n * P:(n + 1) * P],
                                                   R["identb"][:, :])
                last.then_inc(hback, 1)
                wait(pe, hkept, b + 1)
                for k in range(QT):
                    for n in range(NH):
                        last = nc.tensor.matmul(x_ps[:, S + k * D:S + (k + 1) * D], hT[:, k, n * P:(n + 1) * P],
                                                w2b[:, n, :], start=(n == 0), stop=(n == NH - 1))
                last.then_inc(down, 1)

        @block.scalar
        def _(act):
            act.wait_ge(tokens, 3)
            with act.Fori(0, B) as r:
                b = Count(r, 1, 0)
                wait(act, qturned, b + 1)
                nc.scalar.activation(qT[:, 0, :], x_ps[:, 0:S], ACT.Copy).then_inc(qkept, 1)
                for n in range(NH):
                    wait(act, up, b * NH + (n + 1))
                    wait(act, conv, b * NH + (n + 1))
                    nc.scalar.activation(c0[:, n, :], u_ps[n][:, 0:S], ACT.Identity,
                                         scale=cw[:, n, 1:2], bias=cb[:, n:n + 1]).then_inc(conv0, 1)
                for n in range(NH):
                    wait(act, conv, b * NH + (NH + n + 1))
                    wait(act, hturned, b)
                    nc.scalar.activation(act_h[:, n, :], c2[:, n, :], ACT.Silu).then_inc(silu, 1)
                wait(act, hback, b + 1)
                nc.scalar.activation(hT[:, :, :], r_ps[:, :, :], ACT.Copy).then_inc(hkept, 1)

        @block.vector
        def _(dve):
            links = [0]

            def link(ins):
                links[0] += 1
                ins.then_inc(step, 1)
                dve.wait_ge(step, links[0])

            dve.wait_ge(loaded, 64)
            for k, w in enumerate((w1, w2)):
                def total():
                    dve.sem_inc(tokens, 1)
                    dve.wait_ge(summed, k + 1)
                ternary_weights(nc, link, w[:, :], absum[:, k:k + 1], tot_ps[:, k:k + 1], total,
                                mean[:, k:k + 1], minv[:, k:k + 1], w[:, :])
            link(nc.vector.tensor_copy(w2b[:, :, :], w2[:, :].rearrange("p (t d) -> p t d", t=NH)))
            link(nc.vector.tensor_scalar(cw[:, :, :], cw[:, :, :], mean[:, 0:1], None, ALU.mult))
            link(nc.vector.tensor_reduce(amax[:, :], XN[:, :, :], axis=AX.X, op=ALU.max, apply_absolute_value=True))
            link(nc.vector.tensor_scalar(amax[:, :], amax[:, :], 1e-5, None, ALU.max))
            link(nc.vector.reciprocal(sinv[:, :], amax[:, :]))
            link(nc.vector.tensor_scalar(sinv[:, :], sinv[:, :], 127.0, None, ALU.mult))
            link(nc.vector.tensor_scalar(sx[:, :], amax[:, :], 1.0 / 127.0, None, ALU.mult))
            dve.sem_inc(tokens, 1)
            dve.sem_inc(conv, NH)
            qstep_base = links[0]
            with dve.Fori(0, B) as r:
                b = Count(r, 1, 0)
                PER = 23

                def chained(k, ins):
                    ins.then_inc(step, 1)
                    wait(dve, step, b * PER + (qstep_base + k))

                xb = XN[:, bass.ds((b * QT).v, QT), :]
                per_token = [P, QT, D]
                qq = q[:, 0, :, :]
                wait(dve, qturned, b)
                chained(1, nc.vector.tensor_tensor(
                    qq, xb, sinv[:, bass.ds((b * QT).v, QT)].unsqueeze(2).broadcast_to(per_token), ALU.mult))
                chained(2, nc.vector.tensor_scalar(qq, qq, MAGIC, -MAGIC, ALU.add, ALU.add))
                chained(3, nc.vector.tensor_scalar(qq, qq, -128.0, 127.0, ALU.max, ALU.min))
                chained(4, nc.vector.tensor_tensor(
                    qq, qq, sx[:, bass.ds((b * QT).v, QT)].unsqueeze(2).broadcast_to(per_token), ALU.mult))
                dve.sem_inc(qdone, 1)
                for n in range(NH):
                    u = u_ps[n][:, 0:S]
                    wait(dve, conv0, b * NH + (n + 1))
                    if n == 0:
                        wait(dve, silu, b * NH)
                    nc.vector.tensor_copy(c1[:, n, 0:1], c0[:, n, 0:1])
                    chained(5 + 2 * n, nc.vector.scalar_tensor_tensor(
                        out=c1[:, n, 1:S], in0=u[:, 0:S - 1], scalar=cw[:, n, 0:1], in1=c0[:, n, 1:S],
                        op0=ALU.mult, op1=ALU.add))
                    nc.vector.tensor_copy(c2[:, n, S - 1:S], c1[:, n, S - 1:S])
                    chained(6 + 2 * n, nc.vector.scalar_tensor_tensor(
                        out=c2[:, n, 0:S - 1], in0=u[:, 1:S], scalar=cw[:, n, 2:3], in1=c1[:, n, 0:S - 1],
                        op0=ALU.mult, op1=ALU.add))
                    dve.sem_inc(conv, 1)
                wait(dve, hturned, b + 1)
                for k in range(QT):
                    ins = nc.vector.tensor_reduce(hmax[:, k, 0:1], t_ps[k][:, :], axis=AX.X, op=ALU.max,
                                                  apply_absolute_value=True)
                chained(13, ins)
                chained(14, nc.vector.tensor_scalar(hmax[:, :, 1], hmax[:, :, 0], 1e-5, None, ALU.max))
                chained(15, nc.vector.reciprocal(hinv[:, :, 0], hmax[:, :, 1]))
                chained(16, nc.vector.tensor_scalar(hinv[:, :, 1], hinv[:, :, 0], 127.0, None, ALU.mult))
                chained(17, nc.vector.tensor_scalar(hs[:, :, 0], hmax[:, :, 1], 1.0 / 127.0, mean[:, 1:2],
                                                    ALU.mult, ALU.mult))
                for k in range(QT):
                    ins = nc.vector.tensor_scalar(hq[:, k, :], t_ps[k][:, :], hinv[:, k, 1:2], MAGIC, ALU.mult, ALU.add)
                chained(18, ins)
                chained(19, nc.vector.tensor_scalar(hq[:, :, :], hq[:, :, :], -MAGIC, -128.0, ALU.add, ALU.max))
                wait(dve, hback, b)
                chained(20, nc.vector.tensor_scalar(hqb[:, :, :], hq[:, :, :], 127.0, None, ALU.min))
                dve.sem_inc(hstep, NHS)
                wait(dve, down, b + 1)
                xx = X[:, bass.ds((b * QT).v, QT), :]
                for k in range(QT):
                    ins = nc.vector.tensor_scalar(hq[:, k, 0:D], x_ps[:, S + k * D:S + (k + 1) * D], hs[:, k, 0:1],
                                                  None, ALU.mult)
                chained(21, ins)
                chained(22, nc.vector.tensor_tensor(xx, xx, hq[:, :, 0:D], ALU.add))
                nc.vector.sem_inc(step, 1)
                nc.vector.sem_inc(xadd, NX)


def context_rows_dma(nc, engine, dst, src, sem):
    engine.dma_start(dst[:, 0:KT - 1, 0:D], src[0:(KT - 1) * P, :].rearrange("(t p) d -> p t d", p=P)).then_inc(sem, 16)
    engine.dma_start(dst[0:LAST, KT - 1, 0:D], src[(KT - 1) * P:S2, :]).then_inc(sem, 16)


def wide_attention_stage(nc, stage, A, R, XT):
    X = R["X"]
    SCALE = 1.0 / 32.0
    NPROJ = 5
    NG = 4
    with Scope(nc, stage) as sc:
        wk, wq = sc.sb("wk", [D, D]), sc.sb("wq", [D, D])
        bk, bq = sc.sb("bk", [D, 1]), sc.sb("bq", [D, 1])
        ctxT = [sc.sb(f"ctxT{u}", [D, S2]) for u in range(2)]
        rows = [sc.sb(f"rows{u}", [P, KT, D + 1]) for u in range(2)]
        kT = [sc.sb(f"kT{u}", [D, S2]) for u in range(2)]
        qT = [sc.sb(f"qT{u}", [D, S]) for u in range(2)]
        E = [sc.sb(f"E{u}", [P, S2]) for u in range(2)]
        ET = sc.sb("ET", [P, KT, P])
        mpart = sc.sb("mpart", [P, 2, 4])
        negm = sc.sb("negm", [P, 2, 2])
        rl = sc.sb("rl", [P, 2])
        s_ps = [sc.ps(f"s_ps{j}", [P, 512]) for j in range(4)]
        t_ps = [sc.ps(f"t_ps{j}", [P, 512]) for j in range(2)]
        o_ps = sc.ps("o_ps", [P, D + 1])
        p_ps = sc.ps("p_ps", [P, 512])
        w_loaded, ones_set = sc.sem("w_loaded"), sc.sem("ones_set")
        t_loaded = [sc.sem(f"t_loaded{u}") for u in range(2)]
        r_loaded = [sc.sem(f"r_loaded{u}") for u in range(2)]
        proj, proj_kept, scored, maxed, negated, expd, turned, kept_a, kept_v, summed, recip, added, passed = (
            sc.sem(n) for n in ("proj", "proj_kept", "scored", "maxed", "negated", "expd", "turned", "kept_a",
                                "kept_v", "summed", "recip", "added", "passed"))
        block = sc.block()

        def run(engine, emit):
            with engine.Fori(0, B // 2 - 1) as r:
                for u in range(2):
                    emit(Count(r, 2, u), u, True, True)
            emit(Count(None, 0, B - 2), 0, True, False)
            emit(Count(None, 0, B - 1), 1, False, False)

        @block.sync
        def _(sp):
            for dst, src in ((wk, "L2_wk"), (wq, "L2_wq"), (bk, "L2_bk"), (bq, "L2_bq")):
                sp.dma_start(dst[:, :], A[src]).then_inc(w_loaded, 16)
            sp.dma_start(ctxT[0][:, :], A["ctxT"][0]).then_inc(t_loaded[0], 16)
            sp.dma_start(ctxT[1][:, :], A["ctxT"][1]).then_inc(t_loaded[1], 16)
            sp.wait_ge(ones_set, 2)
            context_rows_dma(nc, sp, rows[0], A["ctx"][0], r_loaded[0])

            def emit(b, u, nxt, after):
                if nxt:
                    own_wait(sp, summed, b * 2, passed)
                    context_rows_dma(nc, sp, rows[1 - u], A["ctx"][(b + 1).v], r_loaded[1 - u])
                if after:
                    own_wait(sp, proj, (b + 1) * NPROJ, passed)
                    sp.dma_start(ctxT[u][:, :], A["ctxT"][(b + 2).v]).then_inc(t_loaded[u], 16)

            run(sp, emit)

        @block.gpsimd
        def _(pool):
            for t in rows:
                nc.gpsimd.memset(t[:, :, :], 1.0).then_inc(ones_set, 1)

        @block.tensor
        def _(pe):
            def project(b, u, k):
                if k == 0:
                    wait(pe, t_loaded[u], b.half() * 16 + 16)
                wait(pe, proj_kept, b * NPROJ + k)
                if k < 4:
                    at, width = K_COLS[k]
                    nc.tensor.matmul(p_ps[:, 0:width], wk[:, :], ctxT[u][:, at:at + width],
                                     start=True, stop=True).then_inc(proj, 1)
                else:
                    nc.tensor.matmul(p_ps[:, 0:S], wq[:, :], XT[:, bass.ds((b * S).v, S)],
                                     start=True, stop=True).then_inc(proj, 1)

            def scores(n, u, qt):
                for j, (at, width) in enumerate(K_COLS):
                    wait(pe, expd, (n - 1) * 4 + (j + 1))
                    nc.tensor.matmul(s_ps[j][:, 0:width], qT[u][:, qt * P:(qt + 1) * P], kT[u][:, at:at + width],
                                     start=True, stop=True).then_inc(scored, 1)

            def emit(b, u, nxt, after):
                for qt in range(QT):
                    n = b * 2 + qt
                    if qt == 0:
                        scores(n + 1, u, 1)
                    elif nxt:
                        wait(pe, proj_kept, (b + 2) * NPROJ)
                        scores(n + 1, 1 - u, 0)
                    for g in range(NG):
                        wait(pe, expd, n * 4 + min(g + 2, 4))
                        wait(pe, kept_a if g % 2 == 0 else kept_v, n * 2 + g // 2)
                        for t in range(4 * g, min(4 * g + 4, KT)):
                            w = rows_of(t)
                            last = nc.tensor.transpose(t_ps[g % 2][0:w, (t % 4) * P:(t % 4 + 1) * P],
                                                       E[qt][:, t * P:t * P + w], R["ident"][:, :])
                        last.then_inc(turned, 1)
                        if nxt and qt == 0:
                            project(b + 1, 1 - u, g)
                    if nxt and qt == 0:
                        project(b + 1, 1 - u, 4)
                    if qt == 0:
                        wait(pe, r_loaded[u], b.half() * 32 + 32)
                    wait(pe, added, n)
                    for t in range(KT):
                        if t % 4 == 0:
                            g = t // 4
                            wait(pe, kept_a if g % 2 == 0 else kept_v, n * 2 + (g // 2 + 1))
                        w = rows_of(t)
                        last = nc.tensor.matmul(o_ps[:, :], ET[0:w, t, :], rows[u][0:w, t, :],
                                                start=(t == 0), stop=(t == KT - 1))
                    last.then_inc(summed, 1)

            pe.wait_ge(w_loaded, 4 * 16)
            first = Count(None, 0, 0)
            for k in range(NPROJ):
                project(first, 0, k)
            pe.wait_ge(proj_kept, NPROJ)
            scores(first, 0, 0)
            run(pe, emit)

        @block.scalar
        def _(act):
            def keep_projection(b, u, k):
                wait(act, proj, b * NPROJ + (k + 1))
                if k < 4:
                    at, width = K_COLS[k]
                    nc.scalar.activation(kT[u][:, at:at + width], p_ps[:, 0:width], ACT.Identity, bias=bk[:, 0:1])\
                      .then_inc(proj_kept, 1)
                else:
                    nc.scalar.activation(qT[u][:, :], p_ps[:, 0:S], ACT.Identity, bias=bq[:, 0:1])\
                      .then_inc(proj_kept, 1)

            def exp(n, qt):
                wait(act, negated, n * 2 + 2)
                for j, (at, width) in enumerate(K_COLS):
                    nc.scalar.activation(E[qt][:, at:at + width], s_ps[j][:, 0:width], ACT.Exp, scale=SCALE,
                                         bias=negm[:, qt, 1:2]).then_inc(expd, 1)

            def emit(b, u, nxt, after):
                for qt in range(QT):
                    n = b * 2 + qt
                    for g in range(NG):
                        if g % 2 == 0:
                            wait(act, turned, n * NG + (g + 1))
                            tiles, w = (4, P) if g < 3 else (1, LAST)
                            nc.scalar.activation(ET[0:w, 4 * g:4 * g + tiles, :], t_ps[0][0:w, 0:tiles * P]
                                                 .rearrange("p (t q) -> p t q", q=P), ACT.Copy).then_inc(kept_a, 1)
                        if nxt and qt == 0:
                            keep_projection(b + 1, 1 - u, g)
                    if nxt and qt == 0:
                        keep_projection(b + 1, 1 - u, 4)
                    if qt == 0 or nxt:
                        exp(n + 1, 1 - qt)

            act.wait_ge(w_loaded, 4 * 16)
            first = Count(None, 0, 0)
            for k in range(NPROJ):
                keep_projection(first, 0, k)
            exp(first, 0)
            run(act, emit)

        @block.vector
        def _(dve):
            def maximum(n, qt):
                for j, (at, width) in enumerate(K_COLS):
                    wait(dve, scored, n * 4 + (j + 1))
                    if j == 0:
                        wait(dve, negated, (n - 1) * 2)
                    last = nc.vector.reduce_max(mpart[:, qt, j:j + 1], s_ps[j][:, 0:width], AX.X).then_inc(maxed, 1)
                wait(dve, maxed, n * 4 + 4)
                wait(dve, expd, (n - 1) * 4)
                nc.vector.tensor_reduce(negm[:, qt, 0:1], mpart[:, qt, :], axis=AX.X, op=ALU.max,
                                        negate=True).then_inc(negated, 1)
                wait(dve, negated, n * 2 + 1)
                nc.vector.tensor_scalar(negm[:, qt, 1:2], negm[:, qt, 0:1], SCALE, None, ALU.mult).then_inc(negated, 1)

            def emit(b, u, nxt, after):
                for qt in range(QT):
                    n = b * 2 + qt
                    if qt == 0 or nxt:
                        maximum(n + 1, 1 - qt)
                    for g in (1, 3):
                        wait(dve, turned, n * NG + (g + 1))
                        tiles, w = (4, P) if g < 3 else (1, LAST)
                        nc.vector.tensor_copy(ET[0:w, 4 * g:4 * g + tiles, :], t_ps[1][0:w, 0:tiles * P]
                                              .rearrange("p (t q) -> p t q", q=P)).then_inc(kept_v, 1)
                    wait(dve, summed, n + 1)
                    nc.vector.reciprocal(rl[:, qt:qt + 1], o_ps[:, D:D + 1]).then_inc(recip, 1)
                    wait(dve, recip, n + 1)
                    xb = X[:, bass.ds(n.v, 1), :].rearrange("p a d -> p (a d)")
                    nc.vector.scalar_tensor_tensor(out=xb, in0=o_ps[:, 0:D], scalar=rl[:, qt:qt + 1], in1=xb,
                                                   op0=ALU.mult, op1=ALU.add).then_inc(added, 1)

            maximum(Count(None, 0, 0), 0)
            run(dve, emit)


def history_kernels_stage(nc, stage, A, R, taps):
    C = 2 * D
    C4 = C // 4
    NF = (KT + 1) // 2
    NG = (KT + 3) // 4
    W = 2 * P + 2
    with Scope(nc, stage) as sc:
        hw = sc.sb("hw", [D, C])
        hb, hg, hbeta = (sc.sb(n, [P, C]) for n in ("hb", "hg", "hbeta"))
        w1 = sc.sb("w1", [P, 2, C4])
        b1, w2 = sc.sb("b1", [C4, 1]), sc.sb("w2", [C4, 1])
        b2 = sc.sb("b2", [P, 1])
        kw1, kw2 = sc.sb("kw1", [P, 2, D]), sc.sb("kw2", [D, H * 9])
        kb1, kg, kbeta = (sc.sb(n, [B, D]) for n in ("kb1", "kg", "kbeta"))
        kb2 = sc.sb("kb2", [B, H * 9])
        eps, ones = sc.sb("eps", [P, 1]), sc.sb("ones", [P, P])
        ctxT = [sc.sb(f"ctxT{u}", [D, S2]) for u in range(2)]
        pre = [sc.sb(f"pre{u}", [P, KT, C]) for u in range(2)]
        eh = [sc.sb(f"eh{u}", [P, KT, C]) for u in range(2)]
        st = [sc.sb(f"st{u}", [P, KT, 6]) for u in range(2)]
        mv = [sc.sb(f"mv{u}", [P, KT, 2]) for u in range(2)]
        sd, rstd = sc.sb("sd", [P, 2, KT]), sc.sb("rstd", [P, 2, KT])
        ehT = [sc.sb(f"ehT{u}", [P, 2, 4 * P]) for u in range(2)]
        h1T = sc.sb("h1T", [C4, 4 * P])
        aw, e = sc.sb("aw", [P, 2, KT]), sc.sb("e", [P, 2, KT])
        amax = sc.sb("amax", [P, 2, 3])
        esum = sc.sb("esum", [P, 2, 2])
        cc = sc.sb("cc", [P, 2, B])
        g1, gT = sc.sb("g1", [B, D]), sc.sb("gT", [D, B])
        kst, kmv = sc.sb("kst", [B, 6]), sc.sb("kmv", [B, 4])
        kp, kmax = sc.sb("kp", [B, H, 9]), sc.sb("kmax", [B, 3, H])
        rows0 = sc.sb("rows0", [B, H * 3, W])
        h_ps = [sc.ps(f"h_ps{u}", [P, 2, C]) for u in range(2)]
        t_ps = [sc.ps(f"t_ps{u}", [P, 4 * P]) for u in range(2)]
        w_ps = sc.ps("w_ps", [P, 4 * P])
        aw_ps = sc.ps("aw_ps", [P, KT])
        cc_ps = sc.ps("cc_ps", [P, 3])
        w_loaded, made = sc.sem("w_loaded"), sc.sem("made")
        c_loaded = [sc.sem(f"c_loaded{u}") for u in range(2)]
        projected, biased, stats, aggr, rooted, scaled, centred, normed, eh_done, turned, kept, mixed, h1_done = (
            sc.sem(n) for n in ("projected", "biased", "stats", "aggr", "rooted", "scaled", "centred", "normed",
                                "eh_done", "turned", "kept", "mixed", "h1_done"))
        mlp, act_mlp, mstep, e_done, mvset, rows_done = (
            sc.sem(n) for n in ("mlp", "act_mlp", "mstep", "e_done", "mvset", "rows_done"))
        passed_v, divided = sc.sem("passed_v"), sc.sem("divided")
        weighed, aw_kept, pmax, allmax, negmax, exped, summed, pooled, cc_kept, passed, stored = (
            sc.sem(n) for n in ("weighed", "aw_kept", "pmax", "allmax", "negmax", "exped", "summed", "pooled",
                                "cc_kept", "passed", "stored"))
        block = sc.block()

        def run(engine, emit):
            def at(i):
                return Count(None, 0, i)

            emit(at(0), 0, False, True, True)
            emit(at(1), 1, True, True, True)
            with engine.Fori(0, (B - 4) // 2) as r:
                for u in range(2):
                    emit(Count(r, 2, 2 + u), u, True, True, True)
            emit(at(B - 2), 0, True, True, True)
            emit(at(B - 1), 1, True, True, False)
            emit(at(B), 0, True, False, False)

        def group(g):
            return range(4 * g, min(4 * g + 4, KT)), P if g < NG - 1 else LAST

        def fills_behind(g):
            return range(3 * g, min(3 * g + 3, NF))

        @block.sync
        def _(sp):
            loads = ((hw, A["hist_W"]), (hb, A["hist_b"].partition_broadcast(P)),
                     (hg, A["hist_ln_g"].partition_broadcast(P)), (hbeta, A["hist_ln_b"].partition_broadcast(P)),
                     (b1, A["ctx_b1"]), (w2, A["ctx_W2"]), (b2, A["ctx_b2"].partition_broadcast(P)),
                     (kw2, A["kg_W2"]), (kb1, A["kg_b1"].partition_broadcast(B)),
                     (kg, A["kg_ln_g"].partition_broadcast(B)), (kbeta, A["kg_ln_b"].partition_broadcast(B)),
                     (kb2, A["kg_b2"].partition_broadcast(B)))
            sp.dma_start(ctxT[0][:, :], A["ctxT"][0]).then_inc(c_loaded[0], 16)
            sp.dma_start(ctxT[1][:, :], A["ctxT"][1]).then_inc(c_loaded[1], 16)
            for dst, src in loads:
                sp.dma_start(dst[:, :], src).then_inc(w_loaded, 16)
            for dst, src in ((w1, A["ctx_W1"]), (kw1, A["kg_W1"])):
                sp.dma_start(dst[:, :, :], src.rearrange("(c p) n -> p c n", p=P)).then_inc(w_loaded, 16)

            def emit(b, u, prev, cur, nxt):
                if nxt and not (b.r is None and b.c == B - 2):
                    own_wait(sp, projected, b * NF + NF, passed)
                    sp.dma_start(ctxT[u][:, :], A["ctxT"][(b + 2).v]).then_inc(c_loaded[u], 16)

            run(sp, emit)
            sp.wait_ge(rows_done, 1)
            sp.dma_start(taps.rearrange("b h i w -> b (h i) w"), rows0[:, :, :]).then_inc(stored, 16)
            sp.wait_ge(stored, 16)

        NW = 14 * 16

        @block.gpsimd
        def _(pool):
            nc.gpsimd.memset(ones[:, :], 1.0).then_inc(made, 1)
            nc.gpsimd.memset(eps[:, :], LN_EPS).then_inc(made, 1)
            nc.gpsimd.memset(aw[:, :, :], -BIG).then_inc(made, 1)

            def emit(b, u, prev, cur, nxt):
                for g in range(NG if cur else 1):
                    if cur:
                        tiles, rows = group(g)
                        own_wait(pool, centred, b * NG + (g + 1), passed)
                        if g == 0:
                            own_wait(pool, scaled, b + 1, passed)
                        g_rows = pre[u][0:rows, tiles[0]:tiles[-1] + 1, :]
                        shape = [rows, len(tiles), C]
                        nc.gpsimd.tensor_tensor(g_rows, g_rows, rstd[0:rows, u, tiles[0]:tiles[-1] + 1]
                                                .unsqueeze(2).broadcast_to(shape), ALU.mult).then_inc(divided, 1)
                        own_wait(pool, divided, b * NG + (g + 1), passed)
                        nc.gpsimd.tensor_tensor(g_rows, g_rows, hbeta[0:rows, :].unsqueeze(1).broadcast_to(shape),
                                                ALU.add).then_inc(normed, 1)
                    if g == min(1, NG * cur) and prev:
                        p = b - 1
                        own_wait(pool, pmax, p + 1, passed)
                        nc.gpsimd.partition_all_reduce(amax[:, 1 - u, 1:2], amax[:, 1 - u, 0:1], channels=P,
                                                       reduce_op=bass.bass_isa.ReduceOp.max).then_inc(allmax, 1)

            run(pool, emit)

        @block.tensor
        def _(pe):
            pe.wait_ge(w_loaded, NW)
            pe.wait_ge(made, 3)

            def fill(b, u, f):
                if f == 0:
                    wait(pe, c_loaded[u], b.half() * 16 + 16)
                wait(pe, biased, b * NF + (f if f == 0 else f - 1))
                for t in range(2 * f, min(2 * f + 2, KT)):
                    rows = rows_of(t)
                    last = nc.tensor.matmul(h_ps[f % 2][0:rows, t % 2, :], ctxT[u][:, t * P:t * P + rows], hw[:, :],
                                            start=True, stop=True)
                last.then_inc(projected, 1)

            def turn(b, u, g):
                tiles, rows = group(g)
                wait(pe, eh_done, b * NG + (g + 1))
                wait(pe, kept, b * NG + g)
                for half in range(2):
                    for t in tiles:
                        last = nc.tensor.transpose(t_ps[half][:, (t % 4) * P:(t % 4) * P + rows],
                                                   eh[u][0:rows, t, half * P:(half + 1) * P],
                                                   R["ident"][0:rows, 0:rows])
                last.then_inc(turned, 1)

            def mix(b, g):
                width = 4 * P if g < NG - 1 else LAST
                wait(pe, kept, b * NG + (g + 1))
                wait(pe, h1_done, b * NG + g)
                for half in range(2):
                    last = nc.tensor.matmul(w_ps[0:C4, 0:width], w1[:, half, :], ehT[g % 2][:, half, 0:width],
                                            start=(half == 0), stop=(half == 1))
                last.then_inc(mixed, 1)

            def weigh(b, g):
                tiles, rows = group(g)
                wait(pe, h1_done, b * NG + (g + 1))
                if g == 0:
                    wait(pe, aw_kept, b)
                for t in tiles:
                    k = (t % 4) * P
                    last = nc.tensor.matmul(aw_ps[0:rows, t:t + 1], h1T[:, k:k + rows], w2[:, :],
                                            start=True, stop=True)
                if g == NG - 1:
                    last.then_inc(weighed, 1)

            def emit(b, u, prev, cur, nxt):
                for g in range(NG if cur else 1):
                    if nxt:
                        for f in fills_behind(g)[:2]:
                            fill(b + 1, 1 - u, f)
                    if cur:
                        turn(b, u, g)
                    before = (b - 1, NG - 1) if g == 0 else (b, g - 1)
                    if g or prev:
                        mix(*before)
                    if nxt:
                        for f in fills_behind(g)[2:]:
                            fill(b + 1, 1 - u, f)
                    if g or prev:
                        weigh(*before)
                if prev:
                    wait(pe, exped, b)
                    wait(pe, cc_kept, b - 1)
                    pool_rows(b - 1, 1 - u)

            def pool_rows(p, u):
                nc.tensor.matmul(cc_ps[:, 2:3], ones[:, :], esum[:, u, 0:1], start=True, stop=True)
                for half in range(2):
                    for t in range(KT):
                        rows = rows_of(t)
                        last = nc.tensor.matmul(cc_ps[:, half:half + 1], eh[u][0:rows, t, half * P:(half + 1) * P],
                                                e[0:rows, u, t:t + 1], start=(t == 0), stop=(t == KT - 1))
                last.then_inc(pooled, 1)

            first = Count(None, 0, 0)
            for f in range(NF):
                fill(first, 0, f)
            run(pe, emit)
            pe.wait_ge(cc_kept, B)
            for half in range(2):
                last = nc.tensor.matmul(w_ps[0:B, 0:D], cc[:, half, :], kw1[:, half, :],
                                        start=(half == 0), stop=(half == 1))
            last.then_inc(mlp, 1)
            pe.wait_ge(act_mlp, 2)
            nc.tensor.transpose(t_ps[0][:, 0:B], g1[:, :], R["ident"][0:B, 0:B]).then_inc(mlp, 1)
            pe.wait_ge(mstep, 7)
            nc.tensor.matmul(w_ps[0:B, 0:H * 9], gT[:, :], kw2[:, :], start=True, stop=True).then_inc(mlp, 1)

        @block.scalar
        def _(act):
            act.wait_ge(made, 3)
            act.wait_ge(w_loaded, NW)

            def root(b, u):
                wait(act, aggr, b * KT + KT)
                nc.scalar.activation(sd[:, u, :], mv[u][:, :, 1], ACT.Sqrt, bias=eps[:, 0:1]).then_inc(rooted, 1)

            def exp(b, u):
                wait(act, negmax, b + 1)
                nc.scalar.activation(e[:, u, :], aw[:, u, :], ACT.Exp, bias=amax[:, u, 2:3]).then_inc(e_done, 1)

            def gelu(b, u, g):
                tiles, rows = group(g)
                wait(act, normed, b * NG + (g + 1))
                if g == 0:
                    wait(act, pooled, b - 1)
                nc.scalar.activation(eh[u][0:rows, tiles[0]:tiles[-1] + 1, :],
                                     pre[u][0:rows, tiles[0]:tiles[-1] + 1, :], ACT.Gelu).then_inc(eh_done, 1)

            def keep(b, g):
                width = 4 * P if g < NG - 1 else LAST
                wait(act, turned, b * NG + (g + 1))
                wait(act, mixed, b * NG + (g - 1))
                nc.scalar.activation(ehT[g % 2][:, 0, 0:width], t_ps[0][:, 0:width], ACT.Copy)
                nc.scalar.activation(ehT[g % 2][:, 1, 0:width], t_ps[1][:, 0:width], ACT.Copy).then_inc(kept, 1)

            def mixed_gelu(b, g):
                width = 4 * P if g < NG - 1 else LAST
                wait(act, mixed, b * NG + (g + 1))
                nc.scalar.activation(h1T[:, 0:width], w_ps[0:C4, 0:width], ACT.Gelu, bias=b1[:, 0:1])\
                  .then_inc(h1_done, 1)

            def emit(b, u, prev, cur, nxt):
                if cur:
                    gelu(b, u, 0)
                    gelu(b, u, 1)
                for g in range(NG if cur else 1):
                    if cur:
                        keep(b, g)
                    if g or prev:
                        mixed_gelu(*((b - 1, NG - 1) if g == 0 else (b, g - 1)))
                    if not cur or g == 1:
                        if nxt:
                            root(b + 1, 1 - u)
                        if prev:
                            exp(b - 1, 1 - u)
                    if cur and g + 2 < NG:
                        gelu(b, u, g + 2)

            root(Count(None, 0, 0), 0)
            run(act, emit)
            act.wait_ge(mstep, 3)
            nc.scalar.activation(kmv[:, 2:3], kmv[:, 1:2], ACT.Sqrt, bias=eps[0:B, 0:1]).then_inc(act_mlp, 1)
            act.wait_ge(mstep, 6)
            nc.scalar.activation(g1[:, :], g1[:, :], ACT.Gelu).then_inc(act_mlp, 1)
            act.wait_ge(mstep, 10)
            nc.scalar.activation(kp[:, :, :], kp[:, :, :], ACT.Exp).then_inc(act_mlp, 1)

        @block.vector
        def _(dve):
            dve.wait_ge(w_loaded, NW)
            dve.wait_ge(made, 3)

            def add_bias(b, u, f):
                tiles = range(2 * f, min(2 * f + 2, KT))
                rows = rows_of(tiles[-1])
                wait(dve, projected, b * NF + (f + 1))
                dst = pre[u][0:rows, tiles[0]:tiles[-1] + 1, :]
                nc.vector.tensor_tensor(dst, h_ps[f % 2][0:rows, 0:len(tiles), :],
                                        hb[0:rows, :].unsqueeze(1).broadcast_to([rows, len(tiles), C]),
                                        ALU.add).then_inc(biased, 1)
                wait(dve, biased, b * NF + (f + 1))
                for t in tiles:
                    nc.vector.bn_stats(st[u][0:rows, t, :], pre[u][0:rows, t, :]).then_inc(stats, 1)

            def aggregate(b, u):
                wait(dve, stats, b * KT + KT)
                dve.sem_inc(passed_v, 1)
                for t in range(KT):
                    nc.vector.bn_aggr(mv[u][0:rows_of(t), t, :], st[u][0:rows_of(t), t, :]).then_inc(aggr, 1)

            def keep_pool(p, u):
                wait(dve, pooled, p + 1)
                nc.vector.reciprocal(esum[:, u, 1:2], cc_ps[:, 2:3]).then_inc(summed, 1)
                wait(dve, summed, p + 1)
                nc.vector.tensor_scalar(cc[:, :, bass.ds(p.v, 1)].rearrange("p a b -> p (a b)"), cc_ps[:, 0:2],
                                        esum[:, u, 1:2], None, ALU.mult).then_inc(cc_kept, 1)

            def centre(b, u, g):
                tiles, rows = group(g)
                if g == 0:
                    wait(dve, aggr, b * KT + KT)
                for t in tiles:
                    last = nc.vector.scalar_tensor_tensor(
                        out=pre[u][0:rows, t, :], in0=pre[u][0:rows, t, :], scalar=mv[u][0:rows, t, 0:1],
                        in1=hg[0:rows, :], op0=ALU.subtract, op1=ALU.mult)
                last.then_inc(centred, 1)

            def invert(b, u):
                wait(dve, rooted, b + 1)
                nc.vector.reciprocal(rstd[:, u, :], sd[:, u, :]).then_inc(scaled, 1)

            def keep_weights(b, u):
                wait(dve, weighed, b + 1)
                nc.vector.tensor_scalar(aw[:, u, 0:KT - 1], aw_ps[:, 0:KT - 1], b2[:, 0:1], None, ALU.add)
                nc.vector.tensor_scalar(aw[0:LAST, u, KT - 1:KT], aw_ps[0:LAST, KT - 1:KT], b2[0:LAST, 0:1], None,
                                        ALU.add).then_inc(aw_kept, 1)
                wait(dve, aw_kept, b + 1)
                nc.vector.reduce_max(amax[:, u, 0:1], aw[:, u, :], AX.X).then_inc(pmax, 1)

            def negate(b, u):
                wait(dve, allmax, b + 1)
                nc.vector.tensor_scalar(amax[:, u, 2:3], amax[:, u, 1:2], -1.0, None, ALU.mult).then_inc(negmax, 1)

            def sum_exp(b, u):
                wait(dve, e_done, b + 1)
                nc.vector.reduce_sum(esum[:, u, 0:1], e[:, u, :], AX.X).then_inc(exped, 1)

            def emit(b, u, prev, cur, nxt):
                for g in range(NG if cur else 1):
                    if g == 0 and prev and not cur:
                        keep_weights(b - 1, 1 - u)
                    if (g == 1 or not cur) and prev:
                        negate(b - 1, 1 - u)
                    if g == 1 and not (b.r is None and b.c < 2):
                        keep_pool(b - 2, u)
                    if nxt:
                        for f in fills_behind(g):
                            add_bias(b + 1, 1 - u, f)
                    if cur and g + 2 < NG:
                        centre(b, u, g + 2)
                    if g == 0 and prev and cur:
                        keep_weights(b - 1, 1 - u)
                if nxt:
                    aggregate(b + 1, 1 - u)
                    centre(b + 1, 1 - u, 0)
                    centre(b + 1, 1 - u, 1)
                    invert(b + 1, 1 - u)
                if not cur:
                    keep_pool(b - 2, u)
                if prev:
                    sum_exp(b - 1, 1 - u)

            for u in range(2):
                nc.vector.memset(mv[u][:, :, :], 1.0).then_inc(mvset, 1)
            dve.wait_ge(mvset, 2)
            first = Count(None, 0, 0)
            for f in range(NF):
                add_bias(first, 0, f)
            aggregate(first, 0)
            centre(first, 0, 0)
            centre(first, 0, 1)
            invert(first, 0)
            run(dve, emit)
            keep_pool(Count(None, 0, B - 1), (B - 1) % 2)

            links = [0]

            def link(ins):
                links[0] += 1
                ins.then_inc(mstep, 1)
                dve.wait_ge(mstep, links[0])

            dve.wait_ge(mlp, 1)
            link(nc.vector.tensor_tensor(g1[:, :], w_ps[0:B, 0:D], kb1[:, :], ALU.add))
            link(nc.vector.bn_stats(kst[:, :], g1[:, :]))
            link(nc.vector.bn_aggr(kmv[:, 0:2], kst[:, :]))
            dve.wait_ge(act_mlp, 1)
            link(nc.vector.reciprocal(kmv[:, 3:4], kmv[:, 2:3]))
            link(nc.vector.scalar_tensor_tensor(out=g1[:, :], in0=g1[:, :], scalar=kmv[:, 0:1], in1=kg[:, :],
                                                op0=ALU.subtract, op1=ALU.mult))
            link(nc.vector.scalar_tensor_tensor(out=g1[:, :], in0=g1[:, :], scalar=kmv[:, 3:4], in1=kbeta[:, :],
                                                op0=ALU.mult, op1=ALU.add))
            dve.wait_ge(mlp, 2)
            link(nc.vector.tensor_copy(gT[:, :], t_ps[0][:, 0:B]))
            dve.wait_ge(mlp, 3)
            flat = kp[:, :, :].rearrange("b h k -> b (h k)")
            link(nc.vector.tensor_tensor(flat, w_ps[0:B, 0:H * 9], kb2[:, :], ALU.add))
            link(nc.vector.tensor_reduce(kmax[:, 0, :], kp[:, :, :], axis=AX.X, op=ALU.max))
            link(nc.vector.tensor_tensor(kp[:, :, :], kp[:, :, :], kmax[:, 0, :].unsqueeze(2).broadcast_to([B, H, 9]),
                                         ALU.subtract))
            dve.wait_ge(act_mlp, 3)
            link(nc.vector.reduce_sum(kmax[:, 1, :], kp[:, :, :], AX.X))
            link(nc.vector.reciprocal(kmax[:, 2, :], kmax[:, 1, :]))
            link(nc.vector.memset(rows0[:, :, :], 0.0))
            k4 = kp[:, :, :].rearrange("b h (i j) -> b h i j", i=3)
            r4 = rows0[:, :, :].rearrange("b (h i) w -> b h i w", i=3)
            for j in range(3):
                link(nc.vector.tensor_tensor(r4[:, :, :, P - 1 + j:P + j], k4[:, :, :, 2 - j:3 - j],
                                             kmax[:, 2, :].unsqueeze(2).unsqueeze(3).broadcast_to([B, H, 3, 1]),
                                             ALU.mult))
            dve.sem_inc(rows_done, 1)


def head_values_stage(nc, stage, XT, w, V):
    G = 4
    with Scope(nc, stage) as sc:
        wv = sc.sb("wv", [D, D])
        ps = [sc.ps(f"ps{u}", [P, G * D]) for u in range(2)]
        w_loaded, ones_set, product, kept = (sc.sem(n) for n in ("w_loaded", "ones_set", "product", "kept"))
        block = sc.block()

        @block.sync
        def _(sp):
            sp.dma_start(wv[:, :], w).then_inc(w_loaded, 16)

        @block.gpsimd
        def _(pool):
            nc.gpsimd.memset(V[:, :, :, :], 1.0).then_inc(ones_set, 1)

        @block.tensor
        def _(pe):
            pe.wait_ge(w_loaded, 16)
            for g in range(NT // G):
                if g >= 2:
                    pe.wait_ge(kept, g - 1)
                for k in range(G):
                    n = g * G + k
                    last = nc.tensor.matmul(ps[g % 2][:, k * D:(k + 1) * D], XT[:, n * P:(n + 1) * P], wv[:, :],
                                            start=True, stop=True)
                last.then_inc(product, 1)

        @block.scalar
        def _(act):
            act.wait_ge(ones_set, 1)
            for g in range(NT // G):
                act.wait_ge(product, g + 1)
                nc.scalar.activation(V[:, g * G:(g + 1) * G, :, 0:HD],
                                     ps[g % 2][:, :].rearrange("p (t h d) -> p t h d", h=H, d=HD),
                                     ACT.Copy).then_inc(kept, 1)



BAND = P + 2


def conv_attention_stage(nc, stage, A, R, V, qs, ks, taps):
    SCALE = float(HD) ** -0.5
    X = R["X"]
    QP = S + 2
    NSLOTS = 4
    with Scope(nc, stage) as sc:
        wo, bo = sc.sb("wo", [D, D]), sc.sb("bo", [P, D])
        m8 = sc.sb("m8", [P, 2, QT, S], U8)
        keepT = sc.sb("keepT", [P, QT, S])
        neg = sc.sb("neg", [P, QT, S])
        K6 = [sc.sb(f"K6{u}", [P, NPAIR, S], BF16) for u in range(2)]
        Q6 = [sc.sb(f"Q6{u}", [P, H, S], BF16) for u in range(2)]
        band = [sc.sb(f"band{k}", [P, 2, 3, BAND]) for k in range(NSLOTS)]
        A0 = [sc.sb(f"A0{u}", [P, 2, QT, QP]) for u in range(2)]
        E = [sc.sb(f"E{u}", [P, QT, S]) for u in range(2)]
        ET = [sc.sb(f"ET{u}", [P, QT, QT, P]) for u in range(2)]
        mx = sc.sb("mx", [P, 2, QT])
        negm = sc.sb("negm", [P, 2, QT])
        rl = sc.sb("rl", [P, QT, H])
        on = sc.sb("on", [P, QT, H, HD])
        oT = sc.sb("oT", [P, QT, P])
        xo = sc.sb("xo", [P, QT, D])
        qk_ps = [sc.ps(f"qk_ps{k}", [P, 2, S]) for k in range(QT)]
        c_ps = [sc.ps(f"c_ps{u}", [P, QT, S]) for u in range(2)]
        t_ps = [sc.ps(f"t_ps{u}", [P, QT, QT, P]) for u in range(2)]
        o_ps = sc.ps("o_ps", [P, QT, H, HD + 1])
        f_ps = sc.ps("f_ps", [P, QT, D])
        w_loaded, cleared, masks = (sc.sem(n) for n in ("w_loaded", "cleared", "masks"))
        kq_loaded = [sc.sem(f"kq_loaded{u}") for u in range(2)]
        band_loaded = [sc.sem(f"band_loaded{k}") for k in range(NSLOTS)]
        scored, masked, convolved, added, negated, exped, turned, kept, weighted = (
            sc.sem(n) for n in ("scored", "masked", "convolved", "added", "negated", "exped", "turned", "kept",
                                "weighted"))
        inverted, o_read, o_turned, o_kept, projected, summed, x_done, passed, passed_v = (
            sc.sem(n) for n in ("inverted", "o_read", "o_turned", "o_kept", "projected", "summed", "x_done",
                                "passed", "passed_v"))
        block = sc.block()
        NCLEAR = 6

        def run(engine, emit):
            emit(Count(None, 0, 0), 0, True, False)
            with engine.Fori(0, (B - 2) // 2) as r:
                for v in range(2):
                    emit(Count(r, 2, 1 + v), (1 + v) % 2, False, False)
            emit(Count(None, 0, B - 1), 1, False, True)

        @block.sync
        def _(sp):
            for dst, src in ((m8[:, 0, :, :], A["L1_maskT"]), (m8[:, 1, :, :], A["L1_mask"]),
                             (wo[:, :], A["proj_W"]), (bo[:, :], A["proj_b"].partition_broadcast(P))):
                sp.dma_start(dst, src).then_inc(w_loaded, 16)
            sp.wait_ge(cleared, NCLEAR)

            def load_kq(b, u):
                for g in range(2):
                    rows = slice(64 * g, 64 * g + HD * NTERM)
                    for dst, src in ((K6[u][rows, :, :], ks),
                                     (Q6[u][rows, :, :].rearrange("r (p g) n -> r g p n", g=2)[:, g], qs)):
                        src = src.rearrange("(p g d) t n -> g (d t) p n", g=2, d=HD)[g]
                        sp.dma_start(dst, src[:, :, bass.ds((b * S).v, S)]).then_inc(kq_loaded[u], 16)

            def load_band(b, j):
                src = taps[(b * H + 2 * j).v]
                src = bass.AP(tensor=src.tensor, offset=src.offset,
                              ap=[[1, P], [3 * (2 * P + 2), 2], [2 * P + 2, 3], [1, BAND]])
                sp.dma_start(band[j % NSLOTS][:, :, :, :], src).then_inc(band_loaded[j % NSLOTS], 16)

            first = Count(None, 0, 0)
            load_kq(first, 0)
            for j in range(NSLOTS - 1):
                load_band(first, j)

            def emit(b, u, start, end):
                if not end:
                    own_wait(sp, scored, b * NPAIR, passed)
                    load_kq(b + 1, 1 - u)
                for j in range(NPAIR):
                    ahead = j + NSLOTS - 1
                    if ahead < NPAIR or not end:
                        own_wait(sp, convolved, b * H + 2 * j, passed)
                        load_band(b + ahead // NPAIR, ahead % NPAIR)

            run(sp, emit)

        @block.gpsimd
        def _(pool):
            for t in K6 + Q6:
                nc.gpsimd.memset(t[:, :, :], 0.0).then_inc(cleared, 1)
            for t in A0:
                nc.gpsimd.memset(t[:, :, :, :], 0.0).then_inc(cleared, 1)

        @block.tensor
        def _(pe):
            pe.wait_ge(w_loaded, 4 * 16)
            pe.wait_ge(cleared, NCLEAR)

            def scores(b, u, j):
                if j == 0:
                    wait(pe, kq_loaded[u], b.half() * 64 + 64)
                wait(pe, masked, (b * NPAIR + j) * QT)
                for k in range(QT):
                    last = nc.tensor.matmul(qk_ps[k][:, :, :], K6[u][:, j, k * P:(k + 1) * P],
                                            Q6[u][:, 2 * j:2 * j + 2, :], start=True, stop=True)
                last.then_inc(scored, 1)

            def convolve(b, h):
                j, g = divmod(h, 2)
                n = b * H + h
                wait(pe, masked, (b * NPAIR + (j + 1)) * QT)
                wait(pe, band_loaded[j % NSLOTS], b * (16 * NPAIR // NSLOTS) + 16 * (j // NSLOTS + 1))
                wait(pe, added, (n - 1) * QT)
                for q in range(QT):
                    for k in range(QT):
                        first_col = 1 - k
                        out = c_ps[h % 2][:, q, k * (P - 1):k * (P - 1) + P + 1]
                        for a in range(3):
                            last = nc.tensor.matmul(
                                out, A0[j % 2][:, g, k, q * P + a:q * P + a + P],
                                band[j % NSLOTS][:, g, a, first_col:first_col + P + 1],
                                start=(q == 0 and k == 0 and a == 0), stop=(q == 1 and k == 1 and a == 2),
                                skip_group_check=True)
                last.then_inc(convolved, 1)

            def turn(b, h):
                n = b * H + h
                wait(pe, exped, n + 1)
                wait(pe, kept, n - 1)
                for k in range(QT):
                    for q in range(QT):
                        last = nc.tensor.transpose(t_ps[h % 2][:, k, q, :], E[h % 2][:, q, k * P:(k + 1) * P],
                                                   R["ident"][:, :])
                last.then_inc(turned, 1)

            def weight(b, h):
                n = b * H + h
                wait(pe, kept, n + 1)
                if h == 0:
                    wait(pe, o_read, b)
                for q in range(QT):
                    for k in range(QT):
                        last = nc.tensor.matmul(o_ps[:, q, h, :], ET[h % 2][:, k, q, :],
                                                V[:, bass.ds((b * QT + k).v, 1), h, :]
                                                .rearrange("p a d -> p (a d)"),
                                                start=(k == 0), stop=(k == QT - 1), skip_group_check=True)
                last.then_inc(weighted, 1)

            def turn_out(b):
                wait(pe, o_read, b + 1)
                for q in range(QT):
                    last = nc.tensor.transpose(f_ps[:, q, :], on[:, q, :, :].rearrange("p h d -> p (h d)"),
                                               R["ident"][:, :])
                last.then_inc(o_turned, 1)

            def project_out(b):
                wait(pe, o_kept, b + 1)
                for q in range(QT):
                    last = nc.tensor.matmul(f_ps[:, q, :], oT[:, q, :], wo[:, :], start=True, stop=True)
                last.then_inc(projected, 1)

            def emit(b, u, start, end):
                for h in range(H):
                    convolve(b, h)
                    if h % 2 == 0 and (h < H - 2 or not end):
                        if h < H - 2:
                            scores(b, u, h // 2 + 1)
                        else:
                            scores(b + 1, 1 - u, 0)
                    if h >= 1:
                        turn(b, h - 1)
                    elif not start:
                        turn(b - 1, H - 1)
                    if h >= 2:
                        weight(b, h - 2)
                    elif not start:
                        weight(b - 1, H - 2 + h)
                    if h == 4 and not start:
                        turn_out(b - 1)
                    if h == 6 and not start:
                        project_out(b - 1)

            scores(Count(None, 0, 0), 0, 0)
            run(pe, emit)
            end = Count(None, 0, B - 1)
            turn(end, H - 1)
            weight(end, H - 2)
            weight(end, H - 1)
            turn_out(end)
            project_out(end)

        @block.scalar
        def _(act):
            def exp(b, h):
                n = b * H + h
                wait(act, negated, n + 1)
                for q in range(QT):
                    last = nc.scalar.activation(E[h % 2][:, q, :], E[h % 2][:, q, :], ACT.Exp,
                                                bias=negm[:, h % 2, q:q + 1])
                last.then_inc(exped, 1)

            def keep(b, h):
                n = b * H + h
                wait(act, turned, n + 1)
                wait(act, weighted, n - 1)
                nc.scalar.activation(ET[h % 2][:, :, :, :], t_ps[h % 2][:, :, :, :], ACT.Copy).then_inc(kept, 1)

            def keep_out(b):
                wait(act, o_turned, b + 1)
                wait(act, projected, b)
                nc.scalar.activation(oT[:, :, :], f_ps[:, :, :], ACT.Copy).then_inc(o_kept, 1)

            def emit(b, u, start, end):
                for h in range(H):
                    if h:
                        keep(b, h - 1)
                    elif not start:
                        keep(b - 1, H - 1)
                    exp(b, h)
                    if h == 5 and not start:
                        keep_out(b - 1)

            run(act, emit)
            end = Count(None, 0, B - 1)
            keep(end, H - 1)
            keep_out(end)

        @block.vector
        def _(dve):
            dve.wait_ge(w_loaded, 4 * 16)
            dve.wait_ge(cleared, NCLEAR)
            nc.vector.tensor_scalar(keepT[:, :, :], m8[:, 0, :, :], 0.0, None, ALU.is_equal).then_inc(masks, 1)
            nc.vector.tensor_scalar(neg[:, :, :], m8[:, 1, :, :], 0.0, -BIG, ALU.not_equal, ALU.mult).then_inc(masks, 1)
            dve.wait_ge(masks, 2)

            def mask(b, j):
                m = b * NPAIR + j
                wait(dve, scored, m + 1)
                for k in range(QT):
                    nc.vector.scalar_tensor_tensor(
                        out=A0[j % 2][:, :, k, 1:S + 1], in0=qk_ps[k][:, :, :], scalar=SCALE,
                        in1=keepT[:, k, :].unsqueeze(1).broadcast_to([P, 2, S]),
                        op0=ALU.mult, op1=ALU.mult).then_inc(masked, 1)

            def maximum(b, h):
                n = b * H + h
                wait(dve, convolved, n + 1)
                wait(dve, turned, n - 1)
                if n.r is not None:
                    dve.sem_inc(passed_v, 1)
                for q in range(QT):
                    nc.vector.tensor_tensor_reduce(
                        out=E[h % 2][:, q, :], in0=c_ps[h % 2][:, q, :], in1=neg[:, q, :], scale=1.0,
                        scalar=-3.0e38, op0=ALU.add, op1=ALU.max, accum_out=mx[:, h % 2, q:q + 1])\
                      .then_inc(added, 1)
                wait(dve, added, n * QT + QT)
                nc.vector.tensor_scalar(negm[:, h % 2, :], mx[:, h % 2, :], -1.0, None, ALU.mult).then_inc(negated, 1)

            def normalise(b):
                wait(dve, weighted, b * H + H)
                nc.vector.reciprocal(rl[:, :, :], o_ps[:, :, :, HD]).then_inc(inverted, 1)
                wait(dve, inverted, b + 1)
                nc.vector.tensor_tensor(on[:, :, :, :], o_ps[:, :, :, 0:HD],
                                        rl[:, :, :].unsqueeze(3).broadcast_to([P, QT, H, HD]),
                                        ALU.mult).then_inc(o_read, 1)

            def add_out(b):
                wait(dve, projected, b + 1)
                xb = X[:, bass.ds((b * QT).v, QT), :]
                nc.vector.tensor_tensor(xo[:, :, :], f_ps[:, :, :], xb, ALU.add).then_inc(summed, 1)
                wait(dve, summed, b + 1)
                nc.vector.tensor_tensor(xb, xo[:, :, :], bo[:, :].unsqueeze(1).broadcast_to([P, QT, D]),
                                        ALU.add).then_inc(x_done, 1)

            def emit(b, u, start, end):
                for h in range(H):
                    maximum(b, h)
                    if h % 2 == 0 and (h < H - 2 or not end):
                        if h < H - 2:
                            mask(b, h // 2 + 1)
                        else:
                            mask(b + 1, 0)
                    if h == 1 and not start:
                        normalise(b - 1)
                    if h == 6 and not start:
                        add_out(b - 1)

            mask(Count(None, 0, 0), 0)
            run(dve, emit)
            end = Count(None, 0, B - 1)
            normalise(end)
            add_out(end)


def store_stage(nc, stage, R, out):
    with Scope(nc, stage) as sc:
        stored = sc.sem("stored")
        block = sc.block()

        @block.sync
        def _(sp):
            sp.dma_start(out.rearrange("(n p) d -> p n d", p=P), R["X"][:, :, :]).then_inc(stored, 16)
            sp.wait_ge(stored, 16)


def cross_attention_layer(nc, name, A, R, masked):
    qs = scratch(nc, f"{name}_qs", [P, NTERM, TOK], BF16)
    ks = [scratch(nc, f"{name}_ks{u}", [P, NTERM, S2], BF16) for u in range(2)]
    mrow = scratch(nc, f"{name}_mrow", [2, 2, 16, P], BF16)
    w = {k: A[f"{name}_{k}"] for k in ("wk", "wv", "wo", "bk", "bv", "bo")}
    with Scope(nc, f"{name}_in") as sc:
        XT = sc.sb("XT", [D, TOK])
        layernorm_stage(nc, f"{name}_ln", R, XT=XT)
        head_operands_stage(nc, f"{name}_q", XT, A[f"{name}_wq"], A[f"{name}_bq"], qs)
    attention_stage(nc, f"{name}_at", A, R, w, qs, ks, mrow, masked)


def conv_attention_layer(nc, name, A, R):
    taps = scratch(nc, f"{name}_taps", [B, H, 3, 2 * P + 2], F32)
    qs = scratch(nc, f"{name}_qs", [P, NTERM, TOK], BF16)
    ks = scratch(nc, f"{name}_ks", [P, NTERM, TOK], BF16)
    history_kernels_stage(nc, f"{name}_hk", A, R, taps)
    with Scope(nc, name) as sc:
        V = sc.sb("V", [P, NT, H, HD + 1])
        with Scope(nc, f"{name}_in") as inner:
            XT, XR = inner.sb("XT", [D, TOK]), inner.sb("XR", [D, TOK])
            layernorm_stage(nc, f"{name}_ln", R, XT=XT, XR=XR)
            head_operands_stage(nc, f"{name}_q", XT, A[f"{name}_wq"], None, qs)
            head_operands_stage(nc, f"{name}_k", XR, A[f"{name}_wk"], None, ks, K_PART)
            head_values_stage(nc, f"{name}_v", XT, A[f"{name}_wv"], V)
        conv_attention_stage(nc, f"{name}_at", A, R, V, qs, ks, taps.rearrange("b h i w -> (b h) i w"))


def build_program(nc, A, out):
    with ExitStack() as stack:
        R = {"X": stack.enter_context(nc.sbuf_tensor("x", [P, NT, D], F32)),
             "ident": stack.enter_context(nc.sbuf_tensor("ident", [P, P], F32)),
             "identb": stack.enter_context(nc.sbuf_tensor("identb", [P, P], BF16))}
        constants_stage(nc, A, R)
        cross_attention_layer(nc, "L0", A, R, masked=False)
        with Scope(nc, "L0f") as sc:
            XN = sc.sb("XN", [P, NT, D])
            layernorm_stage(nc, "L0f_ln", R, XN=XN)
            quantised_ffn_stage(nc, "L0f_mm", A, R, XN)
        conv_attention_layer(nc, "L1", A, R)
        with Scope(nc, "L1f") as sc:
            XT, coef = sc.sb("XT", [D, TOK]), sc.sb("coef", [P, NT, 8])
            layernorm_stage(nc, "L1f_ln", R, XT=XT)
            top1_router_stage(nc, "L1f_r", A, R, XT, coef)
            expert_ffn_stage(nc, "L1f_e", R, XT, coef, A["L1_W1"], A["L1_W2"], A["L1_b1"], ACT.Relu)
        with Scope(nc, "L2a") as sc:
            XT = sc.sb("XT", [D, TOK])
            layernorm_stage(nc, "L2a_ln", R, XT=XT)
            wide_attention_stage(nc, "L2a_at", A, R, XT)
        with Scope(nc, "L2f") as sc:
            XT, coef = sc.sb("XT", [D, TOK]), sc.sb("coef", [P, NT, 8])
            layernorm_stage(nc, "L2f_ln", R, XT=XT)
            top2_router_stage(nc, "L2f_r", A, R, XT, coef)
            expert_ffn_stage(nc, "L2f_e", R, XT, coef, A["L2_W1"], A["L2_W2"], None, ACT.Gelu)
        cross_attention_layer(nc, "L3", A, R, masked=True)
        with Scope(nc, "L3f") as sc:
            XN = sc.sb("XN", [P, NT, D])
            layernorm_stage(nc, "L3f_ln", R, XN=XN)
            bitnet_ffn_stage(nc, "L3f_mm", A, R, XN)
        store_stage(nc, "store", R, out)


def kernel(**inputs):
    import numpy as np
    import concourse.bacc as bacc
    from concourse.bass_utils import run_bass_kernel_spmd

    I = {k: np.asarray(v) for k, v in inputs.items()}
    mask = I["mask_Bx1xSxS2_ik1"].reshape(B, S, S2)
    causal = I["mask_SxS_bc0"]
    L = {"x": I["x"].reshape(TOK, D), "ctx": I["ctx_1024"], "ctxT": I["ctx_1024"].transpose(0, 2, 1),
         "mask": mask, "maskT": mask.transpose(0, 2, 1),
         "L1_mask": causal.reshape(QT, P, S).transpose(1, 0, 2),
         "L1_maskT": causal.reshape(S, QT, P)[:, :, ::-1].transpose(2, 1, 0),
         "L0_rhsT": I["L0_ffn_rhs"].T}
    for n in ("L0", "L3"):
        for k in "qkvo":
            L[f"{n}_w{k}"] = I[f"{n}_xattn_W{k}"].T
            L[f"{n}_b{k}"] = I[f"{n}_xattn_b{k}"].reshape((D,) if k == "o" else (D, 1))
    for k in "qkv":
        L[f"L1_w{k}"] = I[f"L1_xattn_W{k}"]
    for k in ("hist_W", "hist_b", "hist_ln_g", "hist_ln_b", "ctx_W1", "ctx_W2", "ctx_b2", "kg_W1", "kg_b1",
              "kg_ln_g", "kg_ln_b", "kg_W2", "kg_b2", "proj_W", "proj_b"):
        L[k] = I[f"L1_xattn_{k}"]
    L["ctx_b1"] = I["L1_xattn_ctx_b1"].reshape(-1, 1)
    for k in ("Wr", "br", "W1", "W2", "b2"):
        L[f"L1_{k}"] = I[f"L1_ffn_{k}"]
    L["L1_b1"] = I["L1_ffn_b1"].reshape(8, 4, P).transpose(0, 2, 1)
    for k in "qk":
        L[f"L2_w{k}"] = I[f"L2_xattn_W{k}"].T
        L[f"L2_b{k}"] = I[f"L2_xattn_b{k}"].reshape(D, 1)
    L.update({"L2_Wr": I["L2_ffn_Wr"].T, "L2_W1": I["L2_ffn_W1"], "L2_W2": I["L2_ffn_W2"],
              "L3_w1T": I["L3_ffn_w1"].T, "L3_w2T": I["L3_ffn_w2"].T, "L3_cw": I["L3_ffn_conv_w"].reshape(-1, 3),
              "L3_cb": I["L3_ffn_conv_b"].reshape(4, P).T})

    nc = bacc.Bacc("TRN2", target_bir_lowering=False, num_devices=1)
    arrays, A = {}, {}
    for name, a in L.items():
        arrays[f"in_{name}_dram"] = a = np.ascontiguousarray(a)
        A[name] = nc.dram_tensor(f"in_{name}_dram", a.shape, mybir.dt.from_np(a.dtype), kind="ExternalInput").ap()
    out = nc.dram_tensor("out_dram", (TOK, D), F32, kind="ExternalOutput").ap()
    build_program(nc, A, out)
    r = run_bass_kernel_spmd(nc, [arrays], core_ids=[0])
    return r.results[0]["out_dram"].reshape(B, S, D)
```

```python
from contextlib import ExitStack

import concourse.bass as bass
from concourse import mybir

F32 = mybir.dt.float32
BF16 = mybir.dt.bfloat16
I32 = mybir.dt.int32
U8 = mybir.dt.uint8
U32 = mybir.dt.uint32
ACT = mybir.ActivationFunctionType
ALU = mybir.AluOpType
AX = mybir.AxisListType

P = 128
B, S, D = 16, 256, 128
S2 = 1601
QT = S // P
NT = B * QT
TOK = B * S
H, HD = 16, 8
NPAIR = H // 2
KT = (S2 + P - 1) // P
LAST = S2 - (KT - 1) * P
LN_EPS = 1e-5
MAGIC = 12582912.0
BIG = float(2 ** 100)
TWO_ONES = 1.0019378662109375
NTERM = 6
Q_PART = (0, 0, 1, 1, 0, 2)
K_PART = (0, 1, 0, 1, 2, 0)


class Count:

    def __init__(self, r, a, c):
        self.r, self.a, self.c = r, a, c

    def __add__(self, n):
        return Count(self.r, self.a, self.c + n)

    def __sub__(self, n):
        return self + -n

    def __mul__(self, n):
        return Count(self.r, self.a * n, self.c * n)

    def half(self):
        return Count(self.r, self.a // 2, self.c // 2)

    @property
    def v(self):
        if self.r is None or self.a == 0:
            return self.c
        x = self.r * self.a if self.a != 1 else self.r
        return x + self.c if self.c else x


def wait(engine, sem, count):
    if count.r is None and count.c <= 0:
        return
    engine.wait_ge(sem, count.v)


def own_wait(engine, sem, count, passed):
    wait(engine, sem, count)
    if count.r is not None:
        engine.sem_inc(passed, 1)


def rows_of(t):
    return P if t < KT - 1 else LAST


class Scope:

    def __init__(self, nc, stage):
        self.nc, self.stage, self.stack, self.sems = nc, stage, ExitStack(), []

    def __enter__(self):
        self.stack.__enter__()
        return self

    def __exit__(self, *e):
        self.stack.__exit__(*e)
        if self.sems and e[0] is None:
            self.nc.clear_and_free_semaphores(self.sems)
            self.nc.all_engine_barrier()

    def sb(self, name, shape, dt=F32):
        return self.stack.enter_context(self.nc.sbuf_tensor(f"{self.stage}_{name}", shape, dt))

    def ps(self, name, shape, dt=F32):
        return self.stack.enter_context(self.nc.psum_tensor(f"{self.stage}_{name}", shape, dt))

    def sem(self, name):
        self.sems.append(self.nc.alloc_semaphore(name=f"{self.stage}_{name}"))
        return self.sems[-1]

    def block(self):
        return self.stack.enter_context(self.nc.Block())


def constants_stage(nc, A, R):
    with Scope(nc, "const") as sc:
        made = sc.sem("made")
        x_loaded = sc.sem("x_loaded")
        block = sc.block()

        @block.sync
        def _(sp):
            sp.dma_start(R["X"][:, :, :], A["x"].rearrange("(n p) d -> p n d", p=P)).then_inc(x_loaded, 16)
            sp.wait_ge(x_loaded, 16)

        @block.gpsimd
        def _(pool):
            nc.gpsimd.memset(R["ident"][:, :], 0.0).then_inc(made, 1)
            nc.gpsimd.memset(R["identb"][:, :], 0.0).then_inc(made, 1)
            pool.wait_ge(made, 2)
            for m in (R["ident"], R["identb"]):
                nc.gpsimd.affine_select(out=m[:, :], in_=m[:, :], compare_op=ALU.not_equal, fill=1.0,
                                        base=0, pattern=[[-1, P]], channel_multiplier=1).then_inc(made, 1)
            pool.wait_ge(made, 4)


def layernorm_stage(nc, stage, R, XT=None, XN=None, XR=None):
    G = 4
    NH = NT // 2
    X = R["X"]
    with Scope(nc, stage) as sc:
        st = sc.sb("st", [P, NT, 6])
        mv = sc.sb("mv", [P, NT, 2])
        sd = sc.sb("sd", [P, NT])
        rstd = sc.sb("rstd", [P, NT])
        nmr = sc.sb("nmr", [P, NT])
        eps = sc.sb("eps", [P, 1])
        xn = None if XT is None or XN is not None else sc.sb("xn", [P, 2, G, D])
        tp = [sc.ps(f"tp{i}", [P, G * P]) for i in range(2)] if XT is not None else None
        if XR is not None:
            rp = [sc.ps(f"rp{i}", [P, G * P]) for i in range(2)]
            flip = sc.sb("flip", [P, P])
            flip_made = sc.sem("flip_made")
        eps_set, stats, aggr, root, scaled = (sc.sem(n) for n in ("eps_set", "stats", "aggr", "root", "scaled"))
        normed, turned, kept = (sc.sem(n) for n in ("normed", "turned", "kept"))
        block = sc.block()
        NG = NT // G

        @block.vector
        def _(dve):
            nc.vector.memset(eps[:, :], LN_EPS).then_inc(eps_set, 1)
            def statistics(half):
                for n in range(half * NH, half * NH + NH):
                    nc.vector.bn_stats(st[:, n, :], X[:, n, :]).then_inc(stats, 1)

            def aggregate(half):
                for n in range(half * NH, half * NH + NH):
                    dve.wait_ge(stats, n + 1)
                    nc.vector.bn_aggr(mv[:, n, :], st[:, n, :]).then_inc(aggr, 1)

            def invert(half):
                t = slice(half * NH, half * NH + NH)
                dve.wait_ge(root, half + 1)
                nc.vector.reciprocal(rstd[:, t], sd[:, t]).then_inc(scaled, 1)
                dve.wait_ge(scaled, 2 * half + 1)
                nc.vector.scalar_tensor_tensor(out=nmr[:, t], in0=mv[:, t, 0], scalar=-1.0, in1=rstd[:, t],
                                               op0=ALU.mult, op1=ALU.mult).then_inc(scaled, 1)

            statistics(0)
            aggregate(0)
            statistics(1)
            invert(0)
            aggregate(1)
            invert(1)
            if XT is not None:
                with dve.Fori(0, NG // 2) as g2:
                    for u in range(2):
                        dve.wait_ge(turned, g2 * 2 + u + 1)
                        if XR is not None:
                            nc.vector.tensor_copy(XR[:, bass.ts(g2 * 2 + u, G * P)], rp[u][:, :])
                        nc.vector.tensor_copy(XT[:, bass.ts(g2 * 2 + u, G * P)], tp[u][:, :]).then_inc(kept, 1)

        @block.scalar
        def _(act):
            act.wait_ge(eps_set, 1)

            def take_root(half):
                t = slice(half * NH, half * NH + NH)
                act.wait_ge(aggr, (half + 1) * NH)
                nc.scalar.activation(sd[:, t], mv[:, t, 1], ACT.Sqrt, bias=eps[:, 0:1]).then_inc(root, 1)
                act.wait_ge(scaled, 2 * half + 2)

            if XN is not None:
                for half in range(2):
                    take_root(half)
                    with act.Fori(half * NG // 2, (half + 1) * NG // 2) as g:
                        for k in range(G):
                            n = g * G + k
                            last = nc.scalar.activation(XN[:, n, :], X[:, n, :], ACT.Identity,
                                                        scale=rstd[:, bass.ts(n, 1)], bias=nmr[:, bass.ts(n, 1)])
                        last.then_inc(normed, 1)
            else:
                def normalise(g, u):
                    for k in range(G):
                        n = g * G + k
                        last = nc.scalar.activation(xn[:, u, k, :], X[:, n, :], ACT.Identity,
                                                    scale=rstd[:, bass.ts(n, 1)], bias=nmr[:, bass.ts(n, 1)])
                    last.then_inc(normed, 1)

                take_root(0)
                for g in range(2):
                    normalise(g, g)
                for first, last_pair in ((1, NG // 4), (NG // 4, NG // 2)):
                    if first > 1:
                        take_root(1)
                    with act.Fori(first, last_pair) as g2:
                        for u in range(2):
                            act.wait_ge(turned, g2 * 2 + u - 1)
                            normalise(g2 * 2 + u, u)

        if XR is not None:
            @block.gpsimd
            def _(pool):
                nc.gpsimd.memset(flip[:, :], 0.0).then_inc(flip_made, 1)
                pool.wait_ge(flip_made, 1)
                nc.gpsimd.affine_select(out=flip[:, :], in_=flip[:, :], compare_op=ALU.not_equal, fill=1.0,
                                        base=1 - P, pattern=[[1, P]], channel_multiplier=1).then_inc(flip_made, 1)

        if XT is not None:
            @block.tensor
            def _(pe):
                def turn(g, u):
                    pe.wait_ge(normed, g + 1)
                    for k in range(G):
                        row = xn[:, u, k, :] if XN is None else XN[:, g * G + k, :]
                        last = nc.tensor.transpose(tp[u][:, k * P:(k + 1) * P], row, R["ident"][:, :])
                        if XR is not None:
                            last = nc.tensor.matmul(rp[u][:, k * P:(k + 1) * P], xn[:, u, k, :], flip[:, :],
                                                    start=True, stop=True)
                    last.then_inc(turned, 1)

                if XR is not None:
                    pe.wait_ge(flip_made, 2)

                for g in range(2):
                    turn(g, g)
                if XN is not None:
                    for g in range(2, NG):
                        pe.wait_ge(kept, g - 1)
                        turn(g, g % 2)
                    return
                with pe.Fori(1, NG // 2) as g2:
                    for u in range(2):
                        pe.wait_ge(kept, g2 * 2 + u - 1)
                        turn(g2 * 2 + u, u)


def head_operands_stage(nc, stage, jobs):
    C = 512
    NC = TOK // C
    NJ = len(jobs)
    with Scope(nc, stage) as sc:
        w = [sc.sb(f"w{j}", [D, D]) for j in range(NJ)]
        b = [sc.sb(f"b{j}", [D, 1]) for j in range(NJ)]
        q = sc.sb("q", [P, 2, C])
        part = [sc.sb(f"part{k}", [P, 2, C], BF16) for k in range(3)]
        ps = [sc.ps(f"ps{u}", [P, C]) for u in range(2)]
        w_loaded, proj, biased, step = (sc.sem(n) for n in ("w_loaded", "proj", "biased", "step"))
        stored = [sc.sem(f"stored{u}") for u in range(2)]
        passed = sc.sem("passed")
        block = sc.block()
        NSTEP = 4
        NW = 16 * sum(1 if bias is None else 2 for _, _, bias, _, _ in jobs)

        def run(engine, emit):
            for c in range(2):
                emit(0, c, c, True)
            for j in range(NJ):
                with engine.Fori(max(j * NC // 2, 1), (j + 1) * NC // 2) as c2:
                    for u in range(2):
                        emit(j, c2 * 2 + u, u, False)

        @block.sync
        def _(sp):
            for j, (_, wq, bias, _, _) in enumerate(jobs):
                sp.dma_start(w[j][:, :], wq).then_inc(w_loaded, 16)
                if bias is not None:
                    sp.dma_start(b[j][:, :], bias).then_inc(w_loaded, 16)

            def store(j, c, u, first):
                dst, parts = jobs[j][3:]
                sp.wait_ge(step, c * NSTEP + NSTEP)
                sp.sem_inc(passed, 1)
                for t in range(NTERM):
                    sp.dma_start(dst[:, t, bass.ds((c - j * NC) * C, C)], part[parts[t]][:, u, :])\
                      .then_inc(stored[u], 16)

            run(sp, store)
            for u in range(2):
                sp.wait_ge(stored[u], 16 * NTERM * NJ * NC // 2)

        @block.tensor
        def _(pe):
            def project(j, c, u, first):
                if not first:
                    pe.wait_ge(biased, c - 1)
                nc.tensor.matmul(ps[u][:, :], w[j][:, :], jobs[j][0][:, bass.ds((c - j * NC) * C, C)],
                                 start=True, stop=True).then_inc(proj, 1)

            pe.wait_ge(w_loaded, NW)
            run(pe, project)

        @block.scalar
        def _(act):
            def add_bias(j, c, u, first):
                act.wait_ge(proj, c + 1)
                if not first:
                    act.wait_ge(step, c * NSTEP - NSTEP)
                nc.scalar.activation(q[:, u, :], ps[u][:, :], ACT.Identity,
                                     bias=0.0 if jobs[j][2] is None else b[j][:, 0:1]).then_inc(biased, 1)

            act.wait_ge(w_loaded, NW)
            run(act, add_bias)

        @block.vector
        def _(dve):
            def split(j, c, u, first):
                if not first:
                    dve.wait_ge(stored[u], (c - u) * (8 * NTERM))
                dve.wait_ge(biased, c + 1)
                nc.vector.tensor_copy(part[0][:, u, :], q[:, u, :]).then_inc(step, 1)
                dve.wait_ge(step, c * NSTEP + 1)
                nc.vector.tensor_tensor(q[:, u, :], q[:, u, :], part[0][:, u, :], ALU.subtract).then_inc(step, 1)
                dve.wait_ge(step, c * NSTEP + 2)
                nc.vector.tensor_copy(part[1][:, u, :], q[:, u, :]).then_inc(step, 1)
                dve.wait_ge(step, c * NSTEP + 3)
                nc.vector.tensor_tensor(part[2][:, u, :], q[:, u, :], part[1][:, u, :], ALU.subtract).then_inc(step, 1)

            run(dve, split)



NQUAD = H // 4
NSLOT = NQUAD * KT
CH = 401
CSTEP = 400
NCH = H * QT * 4
HALF = NPAIR // 2
SHARED = {
    (0, 3): ("turn_o", 3), (0, 5): ("turn_on", 0), (0, 7): ("out_proj", 0), (0, 9): ("turn_max", 1),
    (0, 11): ("k", 0), (1, 1): ("k", 1), (1, 3): ("turn_o", 0), (1, 5): ("k", 2), (1, 7): ("k", 3),
    (1, 9): ("v", 0), (1, 11): ("v", 1), (2, 1): ("v", 2), (2, 3): ("turn_o", 1), (2, 5): ("v", 3),
    (2, 9): ("turn_max", 0), (3, 3): ("turn_o", 2),
}
PER_BATCH = {"turn_o": 4, "turn_on": 1, "out_proj": 1, "turn_max": 2, "k": 4, "v": 4}


class Step:

    def __init__(self, i, parity, fin=True, exp=True, top=True, prep=True):
        self.i, self.u = i, parity
        self.fin, self.exp, self.top, self.prep = fin, exp, top, prep

    def use(self, kind, n):
        if kind in ("turn_on", "out_proj") or (kind, n) == ("turn_o", 3):
            return self.fin, self.i - 1
        if kind == "turn_o" or (kind, n) == ("turn_max", 1):
            return self.exp, self.i
        if kind in ("v", "turn_max"):
            return self.top, self.i + 1
        return self.prep, self.i + 2

    def shared(self, slot):
        e = SHARED.get(divmod(slot, KT))
        return e if e and self.use(*e)[0] else None

    def before(self, slot):
        for at in range(slot - 1, -1, -1):
            if self.shared(at):
                return self.shared(at), self.use(*self.shared(at))[1]
        return ((("turn_o", 2), self.i - 1) if self.fin else (("turn_max", 0), self.i))


def run_steps(engine, emit):
    def at(i):
        return Count(None, 0, i)

    emit(Step(at(-2), 0, fin=False, exp=False, top=False))
    emit(Step(at(-1), 1, fin=False, exp=False))
    emit(Step(at(0), 0, fin=False))
    with engine.Fori(0, 6) as r:
        for v in range(2):
            emit(Step(Count(r, 2, 1 + v), (1 + v) % 2))
    emit(Step(at(13), 1))
    emit(Step(at(14), 0, prep=False))
    emit(Step(at(15), 1, prep=False, top=False))
    emit(Step(at(16), 0, prep=False, top=False, exp=False))


def chunks_of(slot):
    return range(slot * NCH // NSLOT, (slot + 1) * NCH // NSLOT)


def chunk_place(c):
    h, qt, j = c // (4 * QT), c // 4 % QT, c % 4
    p, g = h // 2, h % 2
    return h, qt, CSTEP * j, (p // HALF) * 16 + g * 8 + (p % HALF) * QT + qt, j


K_COLS = ((0, 400), (400, 400), (800, 400), (1200, S2 - 1200))


def attention_stage(nc, stage, A, R, w, qs, ks, mrow, masked):
    SCALE = float(HD) ** -0.5
    X = R["X"]
    with Scope(nc, stage) as sc:
        wk, wv, wo = (sc.sb(n, [D, D]) for n in ("wk", "wv", "wo"))
        bk, bv = sc.sb("bk", [D, 1]), sc.sb("bv", [D, 1])
        bo = sc.sb("bo", [P, D])
        ctx = [sc.sb(f"ctx{u}", [D, S2]) for u in range(2)]
        k32 = sc.sb("k32", [P, S2])
        kpart = [sc.sb(f"kpart{k}", [P, S2], BF16) for k in range(3)]
        K6_flat = [sc.sb(f"K6{u}", [P, NPAIR * S2], BF16) for u in range(2)]
        K6 = [t[:, :].rearrange("p (a n) -> p a n", a=NPAIR) for t in K6_flat]
        QM = [sc.sb(f"QM{u}", [P, H, S], BF16) for u in range(2)]
        QE = [sc.sb(f"QE{u}", [P, H, S], BF16) for u in range(2)]
        V = [sc.sb(f"V{u}", [P, KT, H, HD + 1]) for u in range(2)]
        E = [sc.sb(f"E{u}", [P, 2, 2 * S]) for u in range(2)]
        osb = sc.sb("osb", [P, S])
        on = sc.sb("on", [P, QT, H, HD])
        rl = sc.sb("rl", [P, QT, 4])
        oT = sc.sb("oT", [P, S])
        xo = sc.sb("xo", [P, QT, D])
        mpart = sc.sb("mpart", [P, H * QT, 4])
        negm = sc.sb("negm", [P, 2, 16])
        mhi = sc.sb("mhi", [16, P], BF16)
        mrest = sc.sb("mrest", [16, P])
        mlo = sc.sb("mlo", [16, P], BF16)
        if masked:
            mask_in = sc.sb("mask_in", [P, S2], I32)
            MB = [sc.sb(f"MB{u}", [P, QT, S2], BF16) for u in range(2)]
            MT = [sc.sb(f"MT{u}", [P, KT, S], BF16) for u in range(2)]
            junk = sc.sb("junk", [P, 2, CH], BF16)
        sc_ps = [sc.ps(f"sc{u}", [P, 2, 2 * S]) for u in range(2)]
        mx_ps = [sc.ps(f"mx{u}", [P, 512]) for u in range(2)]
        o_ps = sc.ps("o", [P, 512])
        sh_ps = sc.ps("sh", [P, 512])

        w_loaded = sc.sem("w_loaded")
        cleared = sc.sem("cleared")
        ctx_loaded = [sc.sem(f"ctx_loaded{u}") for u in range(2)]
        full = {k: sc.sem(f"{k}_full") for k in PER_BATCH}
        done = {k: sc.sem(f"{k}_done") for k in PER_BATCH}
        split = sc.sem("split")
        ks_stored = sc.sem("ks_stored")
        kq_loaded = [[sc.sem(f"kq_loaded{u}{h}") for h in range(2)] for u in range(2)]
        top_full, top_done = sc.sem("top_full"), sc.sem("top_done")
        neg_done = sc.sem("neg_done")
        msplit = sc.sem("msplit")
        m_stored = sc.sem("m_stored")
        m_loaded = [sc.sem(f"m_loaded{h}") for h in range(2)]
        sc_full, exp_done, pv_done, o_done = (sc.sem(n) for n in ("sc_full", "exp_done", "pv_done", "o_done"))
        rl_done, x_done = sc.sem("rl_done"), sc.sem("x_done")
        if masked:
            mb_loaded, mb_done, mt_loaded, mt_done = (
                sc.sem(n) for n in ("mb_loaded", "mb_done", "mt_loaded", "mt_done"))
        NDMA = 6
        o_cleared = sc.sem("o_cleared")
        passed, passed_v = sc.sem("passed"), sc.sem("passed_v")
        ones_set = sc.sem("ones_set")
        NCLEAR = 6
        block = sc.block()

        def count(kind, n, b):
            return b * PER_BATCH[kind] + (n + 1)

        @block.sync
        def _(sp):
            for dst, src in ((wk, "wk"), (wv, "wv"), (wo, "wo"), (bk, "bk"), (bv, "bv")):
                sp.dma_start(dst[:, :], w[src]).then_inc(w_loaded, 16)
            sp.dma_start(bo[:, :], w["bo"].partition_broadcast(P)).then_inc(w_loaded, 16)
            def load_half(b, u, half):
                pairs = slice(half * HALF, (half + 1) * HALF)
                for g in range(2):
                    rows = slice(64 * g, 64 * g + HD * NTERM)
                    k_src = ks[u].rearrange("(p g d) t n -> g (d t) p n", g=2, d=HD)[g]
                    sp.dma_start(K6[u][rows, pairs, :], k_src[:, pairs, :]).then_inc(kq_loaded[u][half], 16)
                    q_src = qs.rearrange("(p g d) t n -> g (d t) p n", g=2, d=HD)[g][:, pairs, bass.ts(b.v, S)]
                    for dst in (QM[u], QE[u]):
                        d = dst[rows, :, :].rearrange("r (p g) n -> r g p n", g=2)[:, g, pairs, :]
                        sp.dma_start(d, q_src).then_inc(kq_loaded[u][half], 16)

            def load_max(b, u, half):
                n = b * 2 + half
                own_wait(sp, msplit, n * 3 + 3, passed)
                for part, src in enumerate((mhi, mlo)):
                    sp.dma_start(mrow[half, part], src[:, :]).then_inc(m_stored, 16)
                own_wait(sp, m_stored, n * 32 + 32, passed)
                pairs = slice(half * HALF, (half + 1) * HALF)
                for g in range(2):
                    row = 64 * g + HD * NTERM
                    d = QE[u][row:row + 2, :, :].rearrange("r (p g) n -> r g p n", g=2)[:, g, pairs, :]
                    src = mrow[half].rearrange("a (g p q) n -> a g p (q n)", g=2, q=QT)[:, g]
                    sp.dma_start(d, src).then_inc(m_loaded[half], 16)

            def emit(s):
                if s.prep:
                    b = s.i + 2
                    own_wait(sp, full["v"], (b - 1) * 4, passed)
                    sp.dma_start(ctx[s.u][:, :], A["ctxT"][b.v]).then_inc(ctx_loaded[s.u], 16)
                if s.top:
                    b = s.i + 1
                    own_wait(sp, sc_full, s.i * NSLOT, passed)
                    load_half(b, 1 - s.u, 1)
                if s.exp:
                    load_max(s.i, s.u, 1)
                if s.prep:
                    b = s.i + 2
                    own_wait(sp, split, b * 4 + 4, passed)
                    own_wait(sp, kq_loaded[s.u][1], b.half() * (16 * NDMA), passed)
                    if s.i.r is None and s.i.c == -1:
                        sp.wait_ge(ones_set, 4)
                    if s.i.r is None and s.i.c == -2:
                        sp.wait_ge(cleared, NCLEAR)
                        sp.wait_ge(ones_set, 2)
                    for t in range(NTERM):
                        sp.dma_start(ks[s.u][:, t, :], kpart[K_PART[t]][:, :]).then_inc(ks_stored, 16)
                    own_wait(sp, ks_stored, b * (16 * NTERM) + 16 * NTERM, passed)
                    own_wait(sp, sc_full, s.i * NSLOT + 2 * KT, passed)
                    load_half(b, s.u, 0)
                if s.top:
                    load_max(s.i + 1, 1 - s.u, 0)

            run_steps(sp, emit)

        @block.gpsimd
        def _(pool):
            for t in QM + QE:
                nc.gpsimd.memset(t[:, :, :].rearrange("p h q -> p (h q)").bitcast(F32), 0.0).then_inc(cleared, 1)
            for t in V:
                nc.gpsimd.memset(t[:, :, :, :], 1.0).then_inc(cleared, 1)
            pool.wait_ge(cleared, NCLEAR)

            def convert(dst, cols, rows, sem):
                nc.gpsimd.tensor_scalar(dst, cols[0:rows], 0.0, -BIG, ALU.is_equal, ALU.mult).then_inc(sem, 1)

            def emit(s):
                if masked and s.top:
                    b = s.i + 1
                    own_wait(pool, split, b * 4 + 4, passed)
                    own_wait(pool, sc_full, s.i * NSLOT, passed)
                    view = mask_in[:, 0:6 * S].rearrange("p (t q) -> p t q", q=S)
                    for n in range(3):
                        src = A["maskT"][b.v]
                        if n < 2:
                            src = src[768 * n:768 * (n + 1), :].rearrange("(t p) q -> p t q", p=P)
                            into, dst, rows = view, MT[1 - s.u][:, 6 * n:6 * n + 6, :], P
                        else:
                            src = src[(KT - 1) * P:S2, :]
                            into, dst, rows = view[0:LAST, 0, :], MT[1 - s.u][0:LAST, KT - 1, :], LAST
                        if n:
                            own_wait(pool, mt_done, b * 3 + n, passed)
                        elif not (s.i.r is None and s.i.c == -1):
                            own_wait(pool, mb_done, b * 2 + 2, passed)
                        else:
                            pool.wait_ge(mb_done, 2)
                        pool.dma_start(into, src).then_inc(mt_loaded, 16)
                        own_wait(pool, mt_loaded, b * 48 + 16 * (n + 1), passed)
                        convert(dst, into, rows, mt_done)
                if masked and s.prep:
                    b = s.i + 2
                    own_wait(pool, top_done, (s.i + 1) * NCH, passed)
                    for n in range(QT):
                        if n:
                            own_wait(pool, mb_done, b * 2 + n, passed)
                        else:
                            own_wait(pool, mt_done, (s.i + 2) * 3, passed)
                        pool.dma_start(mask_in[:, :], A["mask"][b.v, n * P:(n + 1) * P, :]).then_inc(mb_loaded, 16)
                        own_wait(pool, mb_loaded, b * 32 + 16 * (n + 1), passed)
                        convert(MB[s.u][:, n, :], mask_in, P, mb_done)
                if s.prep:
                    b = s.i + 2
                    if masked:
                        own_wait(pool, mb_done, b * 2 + 2, passed)
                    own_wait(pool, done["k"], count("k", 3, b), passed)
                    own_wait(pool, ks_stored, b * (16 * NTERM), passed)
                    nc.gpsimd.tensor_copy(kpart[0][:, :], k32[:, :]).then_inc(split, 1)
                    own_wait(pool, split, b * 4 + 1, passed)
                    nc.gpsimd.tensor_tensor(k32[:, :], k32[:, :], kpart[0][:, :], ALU.subtract).then_inc(split, 1)
                    own_wait(pool, split, b * 4 + 2, passed)
                    nc.gpsimd.tensor_copy(kpart[1][:, :], k32[:, :]).then_inc(split, 1)
                    own_wait(pool, split, b * 4 + 3, passed)
                    nc.gpsimd.tensor_tensor(kpart[2][:, :], k32[:, :], kpart[1][:, :], ALU.subtract).then_inc(split, 1)

            run_steps(pool, emit)

        @block.scalar
        def _(act):
            act.wait_ge(w_loaded, 6 * 16)

            def exp(s, slot):
                t = slot % KT
                rows = rows_of(t)
                wait(act, sc_full, s.i * NSLOT + slot + 1)
                wait(act, pv_done, s.i * NSLOT + slot - 1)
                nc.scalar.activation(E[slot % 2][0:rows, :, :], sc_ps[slot % 2][0:rows, :, :], ACT.Exp,
                                     scale=SCALE).then_inc(exp_done, 1)

            def read_shared(s, kind, n):
                b = s.use(kind, n)[1]
                if kind == "k":
                    at, width = K_COLS[n]
                    wait(act, full["k"], count("k", n, b))
                    wait(act, split, b * 4)
                    nc.scalar.activation(k32[:, at:at + width], sh_ps[:, 0:width], ACT.Identity,
                                         bias=bk[:, 0:1]).then_inc(done["k"], 1)
                elif kind == "v":
                    wait(act, full["v"], count("v", n, b))
                    wait(act, pv_done, (b - 1) * NSLOT)
                    if b.r is None and b.c == 0:
                        act.wait_ge(cleared, NCLEAR)
                    tiles, rows = (4, P) if n < 3 else (1, LAST)
                    nc.scalar.activation(
                        V[1 - s.u][0:rows, 4 * n:4 * n + tiles, :, 0:HD],
                        sh_ps[0:rows, 0:tiles * D].rearrange("p (t h d) -> p t h d", h=H, d=HD),
                        ACT.Copy).then_inc(done["v"], 1)
                elif kind == "turn_on":
                    wait(act, full["turn_on"], count("turn_on", 0, b))
                    nc.scalar.activation(oT[:, :], sh_ps[:, 0:S], ACT.Identity, bias=bv[:, 0:1])\
                        .then_inc(done["turn_on"], 1)

            def emit(s):
                for slot in range(NSLOT):
                    if s.exp:
                        exp(s, slot)
                    if slot and s.shared(slot - 1):
                        read_shared(s, *s.shared(slot - 1))

            run_steps(act, emit)

        @block.vector
        def _(dve):
            nc.vector.memset(o_ps[:, :], 0.0).then_inc(o_cleared, 1)
            for k in K6_flat:
                for row in (32, 96):
                    nc.vector.memset(k[row:row + 32, :].bitcast(F32), TWO_ONES).then_inc(ones_set, 1)
            dve.wait_ge(w_loaded, 6 * 16)

            def row_max(s, c):
                b = s.i + 1
                h, qt, at, col, j = chunk_place(c)
                wait(dve, top_full, b * NCH + c + 1)
                if masked:
                    if b.r is not None:
                        dve.sem_inc(passed_v, 1)
                    nc.vector.tensor_tensor_reduce(
                        out=junk[:, c % 2, :], in0=mx_ps[c % 2][:, 0:CH], in1=MB[1 - s.u][:, qt, at:at + CH],
                        scale=1.0, scalar=-3.0e38, op0=ALU.add, op1=ALU.max,
                        accum_out=mpart[:, col, j:j + 1]).then_inc(top_done, 1)
                else:
                    nc.vector.reduce_max(mpart[:, col, j:j + 1], mx_ps[c % 2][:, 0:CH], AX.X).then_inc(top_done, 1)

            def negate_max(b, half):
                wait(dve, top_done, b * NCH + (half + 1) * NCH // 2)
                wait(dve, full["turn_max"], count("turn_max", half, b - 1))
                nc.vector.tensor_reduce(negm[:, half, :], mpart[:, 16 * half:16 * half + 16, :], axis=AX.X,
                                        op=ALU.max, negate=True).then_inc(neg_done, 1)

            def copy_o(b, quad):
                wait(dve, pv_done, b * NSLOT + (quad + 1) * KT)
                wait(dve, full["turn_o"], b * 4 + quad)
                nc.vector.tensor_copy(osb[:, :], o_ps[:, 0:S]).then_inc(o_done, 1)

            def read_shared(s, kind, n):
                b = s.use(kind, n)[1]
                if kind == "turn_o":
                    wait(dve, full[kind], count(kind, n, b))
                    o = sh_ps[:, 0:QT * P].rearrange("p (q h r) -> p q h r", q=QT, h=4)
                    nc.vector.reciprocal(rl[:, :, :], o[:, :, :, HD]).then_inc(rl_done, 1)
                    wait(dve, rl_done, b * 4 + (n + 1))
                    if n == 0:
                        wait(dve, full["turn_on"], b)
                    nc.vector.tensor_tensor(on[:, :, 4 * n:4 * n + 4, :], o[:, :, :, 0:HD],
                                            rl[:, :, :].unsqueeze(3).broadcast_to([P, QT, 4, HD]),
                                            ALU.mult).then_inc(done[kind], 1)
                elif kind == "out_proj":
                    wait(dve, full[kind], count(kind, 0, b))
                    wait(dve, x_done, b)
                    xb = X[:, bass.ds((b * QT).v, QT), :]
                    nc.vector.tensor_tensor(xo[:, :, :], sh_ps[:, 0:QT * D].rearrange("p (q d) -> p q d", q=QT),
                                            xb, ALU.add).then_inc(done[kind], 1)
                    wait(dve, done[kind], count(kind, 0, b))
                    nc.vector.tensor_tensor(xb, xo[:, :, :], bo[:, :].unsqueeze(1).broadcast_to([P, QT, D]),
                                            ALU.add).then_inc(x_done, 1)
                elif kind == "turn_max":
                    m = b * 2 + n
                    wait(dve, full[kind], count(kind, n, b))
                    wait(dve, m_stored, m * 32)
                    nc.vector.tensor_copy(mhi[:, :], sh_ps[0:16, 0:P]).then_inc(msplit, 1)
                    wait(dve, msplit, m * 3 + 1)
                    nc.vector.tensor_tensor(mrest[:, :], sh_ps[0:16, 0:P], mhi[:, :], ALU.subtract)\
                        .then_inc(msplit, 1)
                    wait(dve, msplit, m * 3 + 2)
                    nc.vector.tensor_copy(mlo[:, :], mrest[:, :]).then_inc(msplit, 1)
                    wait(dve, msplit, m * 3 + 3)
                    dve.sem_inc(done[kind], 1)

            def emit(s):
                for slot in range(NSLOT):
                    quad, t = divmod(slot, KT)
                    if s.top:
                        if masked and slot == 0:
                            wait(dve, mb_done, (s.i + 1) * 2 + 2)
                        for c in chunks_of(slot):
                            row_max(s, c)
                    if t == 0:
                        if quad == 0 and s.fin:
                            copy_o(s.i - 1, 3)
                        if quad > 0 and s.exp:
                            copy_o(s.i, quad - 1)
                    if slot == 3 and s.exp:
                        negate_max(s.i, 1)
                    if slot == 2 * KT + 3 and s.top:
                        negate_max(s.i + 1, 0)
                    if slot and s.shared(slot - 1):
                        read_shared(s, *s.shared(slot - 1))

            run_steps(dve, emit)

        @block.tensor
        def _(pe):
            pe.wait_ge(w_loaded, 6 * 16)
            pe.wait_ge(o_cleared, 1)

            def scores(s, slot):
                quad, t = divmod(slot, KT)
                rows = rows_of(t)
                wait(pe, exp_done, s.i * NSLOT + slot - 1)
                for e in range(2):
                    pair = 2 * quad + e
                    out = sc_ps[slot % 2][0:rows, e, :]
                    last = nc.tensor.matmul(out, K6[s.u][:, pair, t * P:t * P + rows],
                                            QE[s.u][:, 2 * pair:2 * pair + 2, :].rearrange("p h q -> p (h q)"),
                                            start=True, stop=not masked)
                    if masked:
                        last = nc.tensor.matmul(out.rearrange("p (h q) -> p h q", h=2), R["identb"][0:rows, 0:rows],
                                                MT[s.u][0:rows, t, :].unsqueeze(1).broadcast_to([rows, 2, S]),
                                                start=False, stop=True)
                last.then_inc(sc_full, 1)

            def product(s, slot):
                quad, t = divmod(slot, KT)
                rows = rows_of(t)
                wait(pe, exp_done, s.i * NSLOT + slot + 1)
                if t == 0:
                    wait(pe, o_done, s.i * 4 + quad)
                for k in range(4):
                    last = nc.tensor.matmul(o_ps[32 * k:32 * k + HD + 1, 0:S], V[s.u][0:rows, t, 4 * quad + k, :],
                                            E[slot % 2][0:rows, k // 2, (k % 2) * S:(k % 2 + 1) * S],
                                            start=(t == 0), stop=(t == KT - 1), tile_position=(0, 32 * k))
                last.then_inc(pv_done, 1)

            def top_scores(s, c):
                h, qt, at, _, _ = chunk_place(c)
                b = s.i + 1
                wait(pe, top_done, b * NCH + c - 1)
                nc.tensor.matmul(mx_ps[c % 2][:, 0:CH], QM[1 - s.u][:, h, qt * P:(qt + 1) * P],
                                 K6[1 - s.u][:, h // 2, at:at + CH], start=True, stop=True).then_inc(top_full, 1)

            def use_shared(s, slot, kind, n):
                b = s.use(kind, n)[1]
                (pk, pn), pb = s.before(slot)
                wait(pe, done[pk], count(pk, pn, pb))
                if kind == "k":
                    at, width = K_COLS[n]
                    wait(pe, ctx_loaded[s.u], b.half() * 16 + 16)
                    last = nc.tensor.matmul(sh_ps[:, 0:width], wk[:, :], ctx[s.u][:, at:at + width],
                                            start=True, stop=True)
                elif kind == "v":
                    for t in range(4 * n, min(4 * n + 4, KT)):
                        rows = rows_of(t)
                        last = nc.tensor.matmul(sh_ps[0:rows, (t % 4) * D:(t % 4 + 1) * D],
                                                ctx[1 - s.u][:, t * P:t * P + rows], wv[:, :],
                                                start=True, stop=True)
                elif kind == "turn_o":
                    wait(pe, o_done, b * 4 + (n + 1))
                    for q in range(QT):
                        last = nc.tensor.transpose(sh_ps[:, q * P:(q + 1) * P], osb[:, q * P:(q + 1) * P],
                                                   R["ident"][:, :])
                elif kind == "turn_on":
                    for q in range(QT):
                        last = nc.tensor.transpose(sh_ps[:, q * P:(q + 1) * P],
                                                   on[:, q, :, :].rearrange("p h d -> p (h d)"), R["ident"][:, :])
                elif kind == "out_proj":
                    for q in range(QT):
                        last = nc.tensor.matmul(sh_ps[:, q * D:(q + 1) * D], oT[:, q * P:(q + 1) * P], wo[:, :],
                                                start=True, stop=True)
                elif kind == "turn_max":
                    wait(pe, neg_done, b * 2 + (n + 1))
                    last = nc.tensor.transpose(sh_ps[0:16, 0:P], negm[:, n, :], R["ident"][:, :])
                last.then_inc(full[kind], 1)

            def emit(s):
                for slot in range(NSLOT):
                    chunks = list(chunks_of(slot)) if s.top else []
                    if s.exp:
                        if slot == 0:
                            wait(pe, m_loaded[0], s.i * 32 + 32)
                            wait(pe, done["v"], s.i * 4 + 4)
                            if masked:
                                wait(pe, mt_done, s.i * 3 + 3)
                        if slot == 2 * KT:
                            wait(pe, m_loaded[1], s.i * 32 + 32)
                        scores(s, slot)
                    if s.i.r is None and s.i.c == -1 and slot == 0:
                        pe.wait_ge(cleared, NCLEAR)
                        pe.wait_ge(ones_set, 4)
                    if s.top and slot == 0:
                        wait(pe, kq_loaded[1 - s.u][0], ((s.i + 1).half() + 1) * (16 * NDMA))
                    for n, c in enumerate(chunks):
                        if c == NCH // 2:
                            wait(pe, kq_loaded[1 - s.u][1], ((s.i + 1).half() + 1) * (16 * NDMA))
                        if n == len(chunks) - 1 and s.exp and slot:
                            product(s, slot - 1)
                        top_scores(s, c)
                    if not chunks and s.exp and slot:
                        product(s, slot - 1)
                    if s.shared(slot):
                        use_shared(s, slot, *s.shared(slot))
                if s.exp:
                    product(s, NSLOT - 1)

            run_steps(pe, emit)


def scratch(nc, name, shape, dt):
    return nc.dram_tensor(name, shape, dt).ap()


def quantised_ffn_stage(nc, stage, A, R, XN):
    G = 4
    NG = NT // G
    X = R["X"]
    with Scope(nc, stage) as sc:
        rT = sc.sb("rT", [D, D])
        rscale, rinv = sc.sb("rscale", [D, 1]), sc.sb("rinv", [D, 1])
        rq = sc.sb("rq", [D, D])
        rqb = sc.sb("rqb", [D, D], BF16)
        rhs = sc.sb("rhs", [D, D], BF16)
        rrow = sc.sb("rrow", [P, D])
        amax, scale, inv = sc.sb("amax", [P, NT]), sc.sb("scale", [P, NT]), sc.sb("inv", [P, NT])
        q = sc.sb("q", [P, 2, G, D])
        qb = sc.sb("qb", [P, 2, G, D], BF16)
        qT = sc.sb("qT", [P, 2, G * P], BF16)
        y = sc.sb("y", [P, 2, G, D])
        tp = [sc.ps(f"tp{u}", [P, G * P], BF16) for u in range(2)]
        mm = [sc.ps(f"mm{u}", [P, G * D]) for u in range(2)]
        rt_ps = sc.ps("rt_ps", [D, D], BF16)
        rr_ps = sc.ps("rr_ps", [P, D])
        r_loaded, wstep, w_turned, scaled = (sc.sem(n) for n in ("r_loaded", "wstep", "w_turned", "scaled"))
        qstep, turned, kept, multiplied, ystep = (
            sc.sem(n) for n in ("qstep", "turned", "kept", "multiplied", "ystep"))
        block = sc.block()
        NQ, NY = 4, 3

        @block.sync
        def _(sp):
            sp.dma_start(rT[:, :], A["L0_rhsT"]).then_inc(r_loaded, 16)
            sp.wait_ge(r_loaded, 16)

        @block.vector
        def _(dve):
            dve.wait_ge(r_loaded, 16)
            nc.vector.tensor_reduce(rscale[:, :], rT[:, :], axis=AX.X, op=ALU.max,
                                    apply_absolute_value=True).then_inc(wstep, 1)
            dve.wait_ge(wstep, 1)
            nc.vector.tensor_scalar(rscale[:, :], rscale[:, :], 1e-12, 1.0 / 127.0, ALU.max, ALU.mult).then_inc(wstep, 1)
            dve.wait_ge(wstep, 2)
            nc.vector.reciprocal(rinv[:, :], rscale[:, :]).then_inc(wstep, 1)
            dve.wait_ge(wstep, 3)
            nc.vector.tensor_scalar(rq[:, :], rT[:, :], rinv[:, 0:1], MAGIC, ALU.mult, ALU.add).then_inc(wstep, 1)
            dve.wait_ge(wstep, 4)
            nc.vector.tensor_scalar(rq[:, :], rq[:, :], -MAGIC, 127.0, ALU.add, ALU.min).then_inc(wstep, 1)
            dve.wait_ge(wstep, 5)
            nc.vector.tensor_scalar(rqb[:, :], rq[:, :], -127.0, None, ALU.max).then_inc(wstep, 1)
            dve.wait_ge(w_turned, 1)
            nc.vector.tensor_copy(rhs[:, :], rt_ps[:, :]).then_inc(wstep, 1)
            dve.wait_ge(w_turned, 2)
            nc.vector.tensor_copy(rrow[:, :], rr_ps[:, :]).then_inc(wstep, 1)
            nc.vector.tensor_reduce(amax[:, :], XN[:, :, :], axis=AX.X, op=ALU.max,
                                    apply_absolute_value=True).then_inc(scaled, 1)
            dve.wait_ge(scaled, 1)
            nc.vector.tensor_scalar(scale[:, :], amax[:, :], 1e-12, 1.0 / 127.0, ALU.max, ALU.mult).then_inc(scaled, 1)
            dve.wait_ge(scaled, 2)
            nc.vector.reciprocal(inv[:, :], scale[:, :]).then_inc(scaled, 1)
            dve.wait_ge(scaled, 3)
            dve.wait_ge(wstep, 8)

            def quantise(g, u):
                nc.vector.tensor_tensor(q[:, u, :, :], XN[:, bass.ds((g * G).v, G), :],
                                        inv[:, bass.ds((g * G).v, G)].unsqueeze(2).broadcast_to([P, G, D]),
                                        ALU.mult).then_inc(qstep, 1)
                wait(dve, qstep, g * NQ + 1)
                nc.vector.tensor_scalar(q[:, u, :, :], q[:, u, :, :], MAGIC, -MAGIC, ALU.add, ALU.add).then_inc(qstep, 1)
                wait(dve, qstep, g * NQ + 2)
                wait(dve, turned, g - 1)
                nc.vector.tensor_scalar(qb[:, u, :, :], q[:, u, :, :], -127.0, 127.0, ALU.max, ALU.min).then_inc(qstep, 1)
                wait(dve, qstep, g * NQ + 3)
                dve.sem_inc(qstep, 1)

            def add(g, u):
                wait(dve, multiplied, g + 1)
                nc.vector.tensor_tensor(y[:, u, :, :], mm[u][:, :].rearrange("p (g d) -> p g d", g=G),
                                        scale[:, bass.ds((g * G).v, G)].unsqueeze(2).broadcast_to([P, G, D]),
                                        ALU.mult).then_inc(ystep, 1)
                wait(dve, ystep, g * NY + 1)
                nc.vector.tensor_tensor(y[:, u, :, :], y[:, u, :, :], rrow[:, :].unsqueeze(1).broadcast_to([P, G, D]),
                                        ALU.mult).then_inc(ystep, 1)
                wait(dve, ystep, g * NY + 2)
                xg = X[:, bass.ds((g * G).v, G), :]
                nc.vector.tensor_tensor(xg, xg, y[:, u, :, :], ALU.add).then_inc(ystep, 1)

            quantise(Count(None, 0, 0), 0)
            quantise(Count(None, 0, 1), 1)
            with dve.Fori(0, NG // 2 - 1) as r:
                for u in range(2):
                    quantise(Count(r, 2, 2 + u), u)
                    add(Count(r, 2, u), u)
            for u in range(2):
                add(Count(None, 0, NG - 2 + u), u)

        @block.tensor
        def _(pe):
            pe.wait_ge(wstep, 6)
            nc.tensor.transpose(rt_ps[:, :], rqb[:, :], R["identb"][:, :]).then_inc(w_turned, 1)
            nc.tensor.matmul(rr_ps[:, :], rscale[:, 0:1].broadcast_to([D, P]), R["ident"][:, :],
                             start=True, stop=True).then_inc(w_turned, 1)
            pe.wait_ge(wstep, 8)

            def turn(g, u):
                wait(pe, qstep, g * NQ + NQ)
                wait(pe, kept, g - 1)
                for k in range(G):
                    last = nc.tensor.transpose(tp[u][:, k * P:(k + 1) * P], qb[:, u, k, :], R["identb"][:, :])
                last.then_inc(turned, 1)

            def multiply(g, u):
                wait(pe, kept, g + 1)
                wait(pe, ystep, g * NY - (2 * NY - 1))
                for k in range(G):
                    last = nc.tensor.matmul(mm[u][:, k * D:(k + 1) * D], qT[:, u, k * P:(k + 1) * P], rhs[:, :],
                                            start=True, stop=True)
                last.then_inc(multiplied, 1)

            turn(Count(None, 0, 0), 0)
            turn(Count(None, 0, 1), 1)
            multiply(Count(None, 0, 0), 0)
            multiply(Count(None, 0, 1), 1)
            with pe.Fori(1, NG // 2) as r:
                for u in range(2):
                    turn(Count(r, 2, u), u)
                    multiply(Count(r, 2, u), u)

        @block.scalar
        def _(act):
            def keep(g, u):
                wait(act, turned, g + 1)
                wait(act, multiplied, g - 1)
                nc.scalar.activation(qT[:, u, :], tp[u][:, :], ACT.Copy).then_inc(kept, 1)

            keep(Count(None, 0, 0), 0)
            keep(Count(None, 0, 1), 1)
            with act.Fori(1, NG // 2) as r:
                for u in range(2):
                    keep(Count(r, 2, u), u)


NE = 8
DFF = 512
NF = DFF // P


BLK = 256
NBLK = -(-((TOK + 8 * (BLK - 1)) // BLK) // 4) * 4


def first_of(nc, link, out, values, top, rank, tmp, red):
    shape = [P, NT, NE]
    link(nc.vector.tensor_tensor(tmp[:, :, :], values, top.unsqueeze(2).broadcast_to(shape), ALU.is_equal))
    link(nc.vector.tensor_tensor(tmp[:, :, :], tmp[:, :, :], rank[:, :].unsqueeze(1).broadcast_to(shape), ALU.mult))
    link(nc.vector.tensor_reduce(red[:, :], tmp[:, :, :], axis=AX.X, op=ALU.max))
    link(nc.vector.tensor_tensor(out, tmp[:, :, :], red[:, :].unsqueeze(2).broadcast_to(shape), ALU.is_equal))


def top1_router_stage(nc, stage, A, R, XT, slot, gate, weight_row, xs):
    G = 4
    X = R["X"]
    with Scope(nc, stage) as sc:
        wr = sc.sb("wr", [D, NE])
        br = sc.sb("br", [P, NE])
        b2 = sc.sb("b2", [NE, D])
        rank = sc.sb("rank", [P, NE])
        lg, ex, tmp = (sc.sb(n, [P, NT, NE]) for n in ("lg", "ex", "tmp"))
        coef, chosen, pos, t0, t1 = (sc.sb(n, [P, NT, NE]) for n in ("coef", "chosen", "pos", "t0", "t1"))
        top, total, red, at = (sc.sb(n, [P, NT]) for n in ("top", "total", "red", "at"))
        count, nblk, end0, end1 = (sc.sb(n, [P, NE]) for n in ("count", "nblk", "end0", "end1"))
        before, ones = sc.sb("before", [P, P]), sc.sb("ones", [P, P])
        pid = sc.sb("pid", [P, 1])
        number = sc.sb("number", [P, NBLK])
        passed_end = sc.sb("passed_end", [P, NBLK, NE])
        expert, row = sc.sb("expert", [P, NBLK]), sc.sb("row", [P, NBLK])
        zeros = sc.sb("zeros", [P, 4 * D])
        ahead_ps = sc.ps("ahead_ps", [P, NT, NE])
        sum_ps = sc.ps("sum_ps", [P, NT, NE])
        pid_ps = sc.ps("pid_ps", [P, 1])
        cleared, counted, chose = sc.sem("cleared"), sc.sem("counted"), sc.sem("chose")
        cT = sc.sb("cT", [NE, 2, G, P])
        lg_ps = sc.ps("lg_ps", [P, NT, NE])
        ct_ps = [sc.ps(f"ct_ps{u}", [NE, G, P]) for u in range(2)]
        y_ps = [sc.ps(f"y_ps{u}", [P, G, D]) for u in range(2)]
        loaded, ranked, logits, step, lowered, exps, turned, kept, product, added = (
            sc.sem(n) for n in ("loaded", "ranked", "logits", "step", "lowered", "exps", "turned", "kept",
                                "product", "added"))
        block = sc.block()

        @block.sync
        def _(sp):
            sp.dma_start(wr[:, :], A["L1_Wr"]).then_inc(loaded, 16)
            sp.dma_start(br[:, :], A["L1_br"].partition_broadcast(P)).then_inc(loaded, 16)
            sp.dma_start(b2[:, :], A["L1_b2"]).then_inc(loaded, 16)
            sp.wait_ge(ranked, NE + NBLK + 3)
            reps = NBLK * BLK // (4 * P)
            sp.dma_start(xs.rearrange("(a p r) d -> p a (r d)", p=P, r=4),
                         zeros[:, :].unsqueeze(1).broadcast_to([P, reps, 4 * D])).then_inc(cleared, 16)
            sp.wait_ge(cleared, 16)

        @block.gpsimd
        def _(pool):
            for e in range(NE):
                nc.gpsimd.memset(rank[:, e:e + 1], float(NE - e)).then_inc(ranked, 1)
            for j in range(NBLK):
                nc.gpsimd.memset(number[:, j:j + 1], float(j)).then_inc(ranked, 1)
            nc.gpsimd.memset(zeros[:, :], 0.0).then_inc(ranked, 1)
            nc.gpsimd.memset(ones[:, :], 1.0).then_inc(ranked, 1)
            pool.wait_ge(ranked, NE + NBLK + 2)
            nc.gpsimd.affine_select(out=before[:, :], in_=ones[:, :], compare_op=ALU.is_ge, fill=0.0, base=-1,
                                    pattern=[[1, P]], channel_multiplier=-1).then_inc(ranked, 1)

        @block.tensor
        def _(pe):
            pe.wait_ge(loaded, 48)
            for n in range(NT):
                last = nc.tensor.matmul(lg_ps[:, n, :], XT[:, n * P:(n + 1) * P], wr[:, :], start=True, stop=True)
            last.then_inc(logits, 1)
            pe.wait_ge(ranked, NE + NBLK + 3)
            pe.wait_ge(chose, 1)
            nc.tensor.matmul(pid_ps[:, :], before[:, :], ones[:, 0:1], start=True, stop=True)
            nc.tensor.matmul(ahead_ps[:, :, :], before[:, :], chosen[:, :, :], start=True, stop=True)
            nc.tensor.matmul(sum_ps[:, :, :], ones[:, :], chosen[:, :, :], start=True, stop=True).then_inc(counted, 1)
            pe.wait_ge(chose, 2)
            for g in range(NT // G + 1):
                if g < NT // G:
                    if g >= 2:
                        pe.wait_ge(kept, g - 1)
                    for k in range(G):
                        last = nc.tensor.transpose(ct_ps[g % 2][:, k, :], coef[:, g * G + k, :], R["ident"][:, :])
                    last.then_inc(turned, 1)
                if g:
                    u = (g - 1) % 2
                    pe.wait_ge(kept, g)
                    if g >= 3:
                        pe.wait_ge(added, g - 2)
                    for k in range(G):
                        last = nc.tensor.matmul(y_ps[u][:, k, :], cT[:, u, k, :], b2[:, :], start=True, stop=True)
                    last.then_inc(product, 1)

        @block.scalar
        def _(act):
            act.wait_ge(lowered, 1)
            nc.scalar.activation(ex[:, :, :], lg[:, :, :], ACT.Exp).then_inc(exps, 1)
            for g in range(NT // G):
                act.wait_ge(turned, g + 1)
                if g >= 2:
                    act.wait_ge(product, g - 1)
                nc.scalar.activation(cT[:, g % 2, :, :], ct_ps[g % 2][:, :, :], ACT.Copy).then_inc(kept, 1)

        @block.vector
        def _(dve):
            shape = [P, NT, NE]
            links = [0]

            def link(ins):
                links[0] += 1
                ins.then_inc(step, 1)
                dve.wait_ge(step, links[0])

            def tt(out, a, b, op):
                link(nc.vector.tensor_tensor(out, a, b, op))

            dve.wait_ge(logits, 1)
            dve.wait_ge(loaded, 48)
            dve.wait_ge(ranked, NE + NBLK + 3)
            link(nc.vector.tensor_tensor(lg[:, :, :], lg_ps[:, :, :], br[:, :].unsqueeze(1).broadcast_to(shape), ALU.add))
            link(nc.vector.reduce_max(top[:, :], lg[:, :, :], AX.X))
            link(nc.vector.tensor_tensor(lg[:, :, :], lg[:, :, :], top[:, :].unsqueeze(2).broadcast_to(shape), ALU.subtract))
            dve.sem_inc(lowered, 1)
            dve.wait_ge(exps, 1)
            link(nc.vector.reduce_sum(total[:, :], ex[:, :, :], AX.X))
            link(nc.vector.reciprocal(gate[:, :], total[:, :]))
            link(nc.vector.reduce_max(top[:, :], ex[:, :, :], AX.X))
            first_of(nc, link, chosen[:, :, :], ex[:, :, :], top[:, :], rank, tmp, red)
            dve.sem_inc(chose, 1)
            tt(gate[:, :], gate[:, :], top[:, :], ALU.mult)
            tt(coef[:, :, :], chosen[:, :, :], gate[:, :].unsqueeze(2).broadcast_to(shape), ALU.mult)
            dve.sem_inc(chose, 1)
            dve.wait_ge(counted, 1)
            link(nc.vector.tensor_copy(pid[:, :], pid_ps[:, :]))
            link(nc.vector.memset(t0[:, 0:1, :], 0.0))
            link(nc.vector.tensor_copy(t0[:, 1:NT, :], sum_ps[:, 0:NT - 1, :]))
            a, b = t0, t1
            for d in (1, 2, 4, 8, 16):
                link(nc.vector.tensor_copy(b[:, 0:d, :], a[:, 0:d, :]))
                tt(b[:, d:NT, :], a[:, d:NT, :], a[:, 0:NT - d, :], ALU.add)
                a, b = b, a
            tt(pos[:, :, :], ahead_ps[:, :, :], a[:, :, :], ALU.add)
            tt(count[:, :], a[:, NT - 1, :], sum_ps[:, NT - 1, :], ALU.add)
            link(nc.vector.tensor_scalar(nblk[:, :], count[:, :], 1.0 / BLK, 0.5 - 0.5 / BLK, ALU.mult, ALU.add))
            link(nc.vector.tensor_scalar(nblk[:, :], nblk[:, :], MAGIC, -MAGIC, ALU.add, ALU.add))
            link(nc.vector.tensor_copy(end0[:, :], nblk[:, :]))
            a, b = end0, end1
            for d in (1, 2, 4):
                link(nc.vector.tensor_copy(b[:, 0:d], a[:, 0:d]))
                tt(b[:, d:NE], a[:, d:NE], a[:, 0:NE - d], ALU.add)
                a, b = b, a
            tt(b[:, :], a[:, :], nblk[:, :], ALU.subtract)
            link(nc.vector.tensor_scalar(b[:, :], b[:, :], float(BLK), None, ALU.mult))
            tt(pos[:, :, :], pos[:, :, :], b[:, :].unsqueeze(1).broadcast_to(shape), ALU.add)
            tt(pos[:, :, :], pos[:, :, :], chosen[:, :, :], ALU.mult)
            link(nc.vector.reduce_sum(at[:, :], pos[:, :, :], AX.X))
            link(nc.vector.tensor_copy(slot[:, :], at[:, :]))
            wide = [P, NBLK, NE]
            tt(passed_end[:, :, :], number[:, :].unsqueeze(2).broadcast_to(wide),
               a[:, :].unsqueeze(1).broadcast_to(wide), ALU.is_ge)
            link(nc.vector.reduce_sum(expert[:, :], passed_end[:, :, :], AX.X))
            link(nc.vector.tensor_scalar(expert[:, :], expert[:, :], float(NE - 1), None, ALU.min))
            link(nc.vector.tensor_scalar(row[:, :], expert[:, :], float(P), pid[:, 0:1], ALU.mult, ALU.add))
            link(nc.vector.tensor_copy(weight_row[:, :], row[:, :]))
            for g in range(NT // G):
                dve.wait_ge(product, g + 1)
                xg = X[:, g * G:(g + 1) * G, :]
                nc.vector.tensor_tensor(xg, xg, y_ps[g % 2][:, :, :], ALU.add).then_inc(added, 1)


def top2_router_stage(nc, stage, A, XT, slot, weight):
    with Scope(nc, stage) as sc:
        wr = sc.sb("wr", [D, NE])
        rank = sc.sb("rank", [P, NE])
        before = sc.sb("before", [P, P])
        ones = sc.sb("ones", [P, P])
        lg, tmp, chosen, pos, t0, t1 = (sc.sb(n, [P, NT, NE]) for n in ("lg", "tmp", "chosen", "pos", "t0", "t1"))
        pick = [sc.sb(f"pick{k}", [P, NT, NE]) for k in range(2)]
        top = [sc.sb(f"top{k}", [P, NT]) for k in range(2)]
        at = [sc.sb(f"at{k}", [P, NT]) for k in range(2)]
        red, gap, eg = (sc.sb(n, [P, NT]) for n in ("red", "gap", "eg"))
        tot = [sc.sb(f"tot{k}", [P, NE]) for k in range(2)]
        lg_ps = sc.ps("lg_ps", [P, NT, NE])
        ahead_ps = sc.ps("ahead_ps", [P, NT, NE])
        sum_ps = sc.ps("sum_ps", [P, NT, NE])
        loaded, made, logits, step, picked, counted, gapped, exps = (
            sc.sem(n) for n in ("loaded", "made", "logits", "step", "picked", "counted", "gapped", "exps"))
        block = sc.block()

        @block.sync
        def _(sp):
            sp.dma_start(wr[:, :], A["L2_Wr"]).then_inc(loaded, 16)

        @block.gpsimd
        def _(pool):
            for e in range(NE):
                nc.gpsimd.memset(rank[:, e:e + 1], float(NE - e)).then_inc(made, 1)
            nc.gpsimd.memset(ones[:, :], 1.0).then_inc(made, 1)
            pool.wait_ge(made, NE + 1)
            nc.gpsimd.affine_select(out=before[:, :], in_=ones[:, :], compare_op=ALU.is_ge, fill=0.0, base=-1,
                                    pattern=[[1, P]], channel_multiplier=-1).then_inc(made, 1)

        @block.tensor
        def _(pe):
            pe.wait_ge(loaded, 16)
            for n in range(NT):
                last = nc.tensor.matmul(lg_ps[:, n, :], XT[:, n * P:(n + 1) * P], wr[:, :], start=True, stop=True)
            last.then_inc(logits, 1)
            pe.wait_ge(made, NE + 2)
            pe.wait_ge(picked, 1)
            nc.tensor.matmul(ahead_ps[:, :, :], before[:, :], chosen[:, :, :], start=True, stop=True)
            nc.tensor.matmul(sum_ps[:, :, :], ones[:, :], chosen[:, :, :], start=True, stop=True).then_inc(counted, 1)

        @block.scalar
        def _(act):
            act.wait_ge(gapped, 1)
            nc.scalar.activation(eg[:, :], gap[:, :], ACT.Exp).then_inc(exps, 1)

        @block.vector
        def _(dve):
            shape = [P, NT, NE]
            links = [0]

            def link(ins):
                links[0] += 1
                ins.then_inc(step, 1)
                dve.wait_ge(step, links[0])

            def tt(out, a, b, op):
                link(nc.vector.tensor_tensor(out, a, b, op))

            dve.wait_ge(made, NE + 2)
            dve.wait_ge(logits, 1)
            link(nc.vector.tensor_copy(lg[:, :, :], lg_ps[:, :, :]))
            link(nc.vector.reduce_max(top[0][:, :], lg[:, :, :], AX.X))
            first_of(nc, link, pick[0][:, :, :], lg[:, :, :], top[0][:, :], rank, tmp, red)
            link(nc.vector.scalar_tensor_tensor(out=lg[:, :, :], in0=pick[0][:, :, :], scalar=-BIG, in1=lg[:, :, :],
                                                op0=ALU.mult, op1=ALU.add))
            link(nc.vector.reduce_max(top[1][:, :], lg[:, :, :], AX.X))
            first_of(nc, link, pick[1][:, :, :], lg[:, :, :], top[1][:, :], rank, tmp, red)
            tt(chosen[:, :, :], pick[0][:, :, :], pick[1][:, :, :], ALU.add)
            dve.sem_inc(picked, 1)
            tt(gap[:, :], top[1][:, :], top[0][:, :], ALU.subtract)
            dve.sem_inc(gapped, 1)
            dve.wait_ge(exps, 1)
            link(nc.vector.tensor_scalar(weight[:, 1, :], eg[:, :], 1.0, None, ALU.add))
            link(nc.vector.reciprocal(weight[:, 0, :], weight[:, 1, :]))
            tt(weight[:, 1, :], eg[:, :], weight[:, 0, :], ALU.mult)
            dve.wait_ge(counted, 1)
            link(nc.vector.memset(t0[:, 0:1, :], 0.0))
            link(nc.vector.tensor_copy(t0[:, 1:NT, :], sum_ps[:, 0:NT - 1, :]))
            a, b = t0, t1
            for d in (1, 2, 4, 8, 16):
                link(nc.vector.tensor_copy(b[:, 0:d, :], a[:, 0:d, :]))
                tt(b[:, d:NT, :], a[:, d:NT, :], a[:, 0:NT - d, :], ALU.add)
                a, b = b, a
            tt(pos[:, :, :], ahead_ps[:, :, :], a[:, :, :], ALU.add)
            tt(tmp[:, 0, :], a[:, NT - 1, :], sum_ps[:, NT - 1, :], ALU.add)
            link(nc.vector.memset(tot[0][:, 0:1], 0.0))
            link(nc.vector.tensor_copy(tot[0][:, 1:NE], tmp[:, 0, 0:NE - 1]))
            a, b = tot
            for d in (1, 2, 4):
                link(nc.vector.tensor_copy(b[:, 0:d], a[:, 0:d]))
                tt(b[:, d:NE], a[:, d:NE], a[:, 0:NE - d], ALU.add)
                a, b = b, a
            tt(pos[:, :, :], pos[:, :, :], a[:, :].unsqueeze(1).broadcast_to(shape), ALU.add)
            for k in range(2):
                tt(tmp[:, :, :], pick[k][:, :, :], pos[:, :, :], ALU.mult)
                link(nc.vector.reduce_sum(at[k][:, :], tmp[:, :, :], AX.X))
                link(nc.vector.tensor_copy(slot[:, k, :], at[k][:, :]))


def dispatched_ffn_stage(nc, stage, R, XN, slot, weight, W1, W2, xs, ys, func):
    X = R["X"]
    C = 4 * P
    TC = C // P
    NC = 2 * TOK // NE // C
    NX = 4
    GRP = 4
    NGRP = NT // GRP
    with Scope(nc, stage) as sc:
        w1 = [sc.sb(f"w1{v}", [D, DFF]) for v in range(2)]
        w2 = [sc.sb(f"w2{v}", [P, NF, D]) for v in range(2)]
        xin = [sc.sb(f"xin{k}", [P, TC, D]) for k in range(NX)]
        xT = [sc.sb(f"xT{u}", [D, C]) for u in range(2)]
        h = [sc.sb(f"h{u}", [P, NF, C]) for u in range(2)]
        y = [sc.sb(f"y{u}", [P, TC, D]) for u in range(2)]
        back = sc.sb("back", [P, 2, NT, D])
        t_ps = [sc.ps(f"t_ps{u}", [D, C]) for u in range(2)]
        h_ps = [sc.ps(f"h_ps{f}", [P, C]) for f in range(NF)]
        y_ps = [sc.ps(f"y_ps{u}", [P, TC, D]) for u in range(2)]
        scattered = sc.sem("scattered")
        w_loaded = [sc.sem(f"w_loaded{v}") for v in range(2)]
        x_loaded = [sc.sem(f"x_loaded{k}") for k in range(NX)]
        y_stored = [sc.sem(f"y_stored{u}") for u in range(2)]
        gathered = [sc.sem(f"gathered{g}") for g in range(NGRP)]
        turned, kept, hidden, acted, product, copied, added, passed, all_stored = (
            sc.sem(n) for n in ("turned", "kept", "hidden", "acted", "product", "copied", "added", "passed",
                                "all_stored"))
        block = sc.block()
        NCH = NE * NC
        assert NC == 2

        @block.sync
        def _(sp):
            def load_expert(e, v):
                sp.dma_start(w1[v][:, :], W1[e.v]).then_inc(w_loaded[v], 16)
                sp.dma_start(w2[v][:, :, :], W2[e.v].rearrange("(f p) d -> p f d", p=P)).then_inc(w_loaded[v], 16)

            def load_rows(m, k):
                sp.dma_start(xin[k][:, :, :], xs[bass.ds((m * C).v, C), :].rearrange("(t p) d -> p t d", p=P))\
                  .then_inc(x_loaded[k], 16)

            def store(m, u):
                own_wait(sp, copied, m + 1, passed)
                sp.dma_start(ys[bass.ds((m * C).v, C), :].rearrange("(t p) d -> p t d", p=P), y[u][:, :, :])\
                  .then_inc(y_stored[u], 16)

            def expert(e, v, more):
                for c in range(NC):
                    m = e * NC + c
                    if more == 2:
                        own_wait(sp, turned, m + 1, passed)
                        load_rows(m + NX, NC * v + c)
                    store(m, c)
                if more:
                    own_wait(sp, product, e * NC + NC, passed)
                    if more == 2:
                        load_expert(e + 2, v)

            for e in range(2):
                load_expert(Count(None, 0, e), e)
            sp.wait_ge(scattered, 16 * 2 * NT)
            for m in range(NX):
                load_rows(Count(None, 0, m), m)
            with sp.Fori(0, NE // 2 - 1) as r:
                for v in range(2):
                    expert(Count(r, 2, v), v, 2)
            expert(Count(None, 0, NE - 2), 0, 1)
            expert(Count(None, 0, NE - 1), 1, 0)
            for u in range(2):
                sp.wait_ge(y_stored[u], 16 * NCH // 2)
            sp.sem_inc(all_stored, 1)

        @block.gpsimd
        def _(pool):
            for n in range(NT):
                for k in range(2):
                    pool.indirect_dma_start(xs, bass.IndirectOffsetOnAxis(ap=slot[:, k, n:n + 1], axis=0),
                                            XN[:, n, :], None).then_inc(scattered, 16)
            pool.wait_ge(all_stored, 1)
            for n in range(NT):
                for k in range(2):
                    pool.indirect_dma_start(back[:, k, n, :], None, ys,
                                            bass.IndirectOffsetOnAxis(ap=slot[:, k, n:n + 1], axis=0))\
                        .then_inc(gathered[n // GRP], 16)

        @block.tensor
        def _(pe):
            def turn(m, k, u):
                wait(pe, x_loaded[k], Count(m.r, m.a // NX, m.c // NX) * 16 + 16)
                wait(pe, kept, m - 1)
                for n in range(TC):
                    last = nc.tensor.transpose(t_ps[u][:, n * P:(n + 1) * P], xin[k][:, n, :], R["ident"][:, :])
                last.then_inc(turned, 1)

            def up(m, u, v):
                wait(pe, kept, m + 1)
                for f in range(NF):
                    wait(pe, acted, (m - 1) * NF + (f + 1))
                    nc.tensor.matmul(h_ps[f][:, :], w1[v][:, f * P:(f + 1) * P], xT[u][:, :],
                                     start=True, stop=True).then_inc(hidden, 1)

            def down(m, u, v):
                wait(pe, acted, m * NF + NF)
                wait(pe, copied, m - 1)
                for k in range(TC):
                    for f in range(NF):
                        last = nc.tensor.matmul(y_ps[u][:, k, :], h[u][:, f, k * P:(k + 1) * P], w2[v][:, f, :],
                                                start=(f == 0), stop=(f == NF - 1))
                last.then_inc(product, 1)

            def expert(e, v, first, more):
                for c in range(NC):
                    m = e * NC + c
                    if c == 0:
                        wait(pe, w_loaded[v], e.half() * 32 + 32)
                    up(m, c, v)
                    if more or c == 0:
                        turn(m + 1, (NC * v + c + 1) % NX, 1 - c)
                    if c:
                        down(m - 1, 0, v)
                    elif not first:
                        down(m - 1, 1, 1 - v)

            turn(Count(None, 0, 0), 0, 0)
            expert(Count(None, 0, 0), 0, True, True)
            with pe.Fori(0, NE // 2 - 1) as r:
                for v in range(2):
                    expert(Count(r, 2, 1 + v), 1 - v, False, True)
            expert(Count(None, 0, NE - 1), 1, False, False)
            down(Count(None, 0, NCH - 1), 1, 1)

        @block.scalar
        def _(act):
            def activate(m, u):
                for f in range(NF):
                    wait(act, hidden, m * NF + (f + 1))
                    if f == 0:
                        wait(act, product, m - 1)
                    nc.scalar.activation(h[u][:, f, :], h_ps[f][:, :], func).then_inc(acted, 1)

            for m in range(2):
                activate(Count(None, 0, m), m)
            with act.Fori(1, NCH // 2) as r:
                for u in range(2):
                    activate(Count(r, 2, u), u)

        @block.vector
        def _(dve):
            def keep_turned(m, u):
                wait(dve, turned, m + 1)
                wait(dve, hidden, (m - 1) * NF)
                nc.vector.tensor_copy(xT[u][:, :], t_ps[u][:, :]).then_inc(kept, 1)

            def keep_result(m, u):
                wait(dve, product, m + 1)
                wait(dve, y_stored[u], m.half() * 16)
                nc.vector.tensor_copy(y[u][:, :, :], y_ps[u][:, :, :]).then_inc(copied, 1)

            keep_turned(Count(None, 0, 0), 0)
            keep_turned(Count(None, 0, 1), 1)
            with dve.Fori(0, NCH // 2 - 1) as r:
                for u in range(2):
                    keep_turned(Count(r, 2, u + 2), u)
                    keep_result(Count(r, 2, u), u)
            for m in (NCH - 2, NCH - 1):
                keep_result(Count(None, 0, m), m % 2)
            for g in range(NGRP):
                dve.wait_ge(gathered[g], 16 * 2 * GRP)
                for k in range(2):
                    for n in range(g * GRP, (g + 1) * GRP):
                        last = nc.vector.scalar_tensor_tensor(
                            out=X[:, n, :], in0=back[:, k, n, :], scalar=weight[:, k, n:n + 1], in1=X[:, n, :],
                            op0=ALU.mult, op1=ALU.add)
                    last.then_inc(added, 1)
                    dve.wait_ge(added, 2 * g + k + 1)


def blocked_ffn_stage(nc, stage, R, XN, slot, gate, weight_row, W1, W2, b1, xs, ys, func):
    X = R["X"]
    TC = BLK // P
    NW = 4
    GRP = 8
    with Scope(nc, stage) as sc:
        w1 = [sc.sb(f"w1{v}", [D, DFF]) for v in range(NW)]
        w2 = [sc.sb(f"w2{v}", [P, NF * D]) for v in range(NW)]
        bias = [sc.sb(f"bias{v}", [P, NF]) for v in range(NW)]
        xin = [sc.sb(f"xin{v}", [P, TC, D]) for v in range(NW)]
        xT = [sc.sb(f"xT{u}", [D, BLK]) for u in range(2)]
        h = [sc.sb(f"h{u}", [P, NF, BLK]) for u in range(2)]
        y = [sc.sb(f"y{u}", [P, TC, D]) for u in range(2)]
        back = sc.sb("back", [P, NT, D])
        t_ps = [sc.ps(f"t_ps{u}", [D, 512]) for u in range(2)]
        h_ps = [sc.ps(f"h_ps{f}", [P, 512]) for f in range(NF)]
        y_ps = [sc.ps(f"y_ps{u}", [P, 512]) for u in range(2)]
        scattered = sc.sem("scattered")
        w_loaded = [sc.sem(f"w_loaded{v}") for v in range(NW)]
        x_loaded = [sc.sem(f"x_loaded{v}") for v in range(NW)]
        y_stored = [sc.sem(f"y_stored{u}") for u in range(2)]
        gathered = [sc.sem(f"gathered{g}") for g in range(NT // GRP)]
        turned, kept, hidden, acted, product, copied, added, passed, all_stored = (
            sc.sem(n) for n in ("turned", "kept", "hidden", "acted", "product", "copied", "added", "passed",
                                "all_stored"))
        block = sc.block()
        assert NBLK % NW == 0 and NW == 4

        def run(engine, emit):
            for c in range(NW):
                emit(Count(None, 0, c), c)
            with engine.Fori(1, NBLK // NW - 1) as r:
                for c in range(NW):
                    emit(Count(r, NW, c), c)
            for c in range(NW):
                emit(Count(None, 0, NBLK - NW + c), c)

        def exists(m, ahead):
            return m.r is not None or m.c + ahead < NBLK

        def rounds(m):
            return Count(m.r, m.a // NW, m.c // NW)

        @block.sync
        def _(sp):
            def load_rows(m, v):
                sp.dma_start(xin[v][:, :, :], xs[bass.ds((m * BLK).v, BLK), :].rearrange("(t p) d -> p t d", p=P))\
                  .then_inc(x_loaded[v], 16)

            def emit(m, c):
                u = c % 2
                if exists(m, NW):
                    own_wait(sp, turned, m + 1, passed)
                    load_rows(m + NW, c)
                own_wait(sp, copied, m + 1, passed)
                sp.dma_start(ys[bass.ds((m * BLK).v, BLK), :].rearrange("(t p) d -> p t d", p=P), y[u][:, :, :])\
                  .then_inc(y_stored[u], 16)

            sp.wait_ge(scattered, 16 * NT)
            for m in range(NW):
                load_rows(Count(None, 0, m), m)
            run(sp, emit)
            for u in range(2):
                sp.wait_ge(y_stored[u], 16 * NBLK // 2)
            sp.sem_inc(all_stored, 1)

        @block.gpsimd
        def _(pool):
            def load_weights(m):
                v = m % NW
                if m >= NW:
                    pool.wait_ge(product, m - NW + 1)
                at = bass.IndirectOffsetOnAxis(ap=weight_row[:, m:m + 1], axis=0)
                for dst, src in ((w1[v], W1), (w2[v], W2), (bias[v], b1)):
                    pool.indirect_dma_start(dst[:, :], None, src, at).then_inc(w_loaded[v], 16)

            for m in range(2):
                load_weights(m)
            for n in range(NT):
                pool.indirect_dma_start(xs, bass.IndirectOffsetOnAxis(ap=slot[:, n:n + 1], axis=0),
                                        XN[:, n, :], None).then_inc(scattered, 16)
            for m in range(2, NBLK):
                load_weights(m)
            pool.wait_ge(all_stored, 1)
            for n in range(NT):
                pool.indirect_dma_start(back[:, n, :], None, ys,
                                        bass.IndirectOffsetOnAxis(ap=slot[:, n:n + 1], axis=0))\
                    .then_inc(gathered[n // GRP], 16)

        @block.tensor
        def _(pe):
            def turn(m, c):
                u = c % 2
                wait(pe, x_loaded[c], rounds(m) * 16 + 16)
                wait(pe, kept, m - 1)
                for k in range(TC):
                    last = nc.tensor.transpose(t_ps[u][:, k * P:(k + 1) * P], xin[c][:, k, :], R["ident"][:, :])
                last.then_inc(turned, 1)

            def down(m, c):
                wait(pe, acted, m * NF + NF)
                wait(pe, copied, m - 1)
                for k in range(TC):
                    for f in range(NF):
                        last = nc.tensor.matmul(y_ps[c % 2][:, k * D:(k + 1) * D], h[c % 2][:, f, k * P:(k + 1) * P],
                                                w2[c % NW][:, f * D:(f + 1) * D],
                                                start=(f == 0), stop=(f == NF - 1))
                last.then_inc(product, 1)

            def emit(m, c):
                wait(pe, kept, m + 1)
                wait(pe, w_loaded[c], rounds(m) * 48 + 48)
                for f in range(NF):
                    wait(pe, acted, (m - 1) * NF + (f + 1))
                    nc.tensor.matmul(h_ps[f][:, 0:BLK], w1[c][:, f * P:(f + 1) * P], xT[c % 2][:, :],
                                     start=True, stop=True).then_inc(hidden, 1)
                if exists(m, 1):
                    turn(m + 1, (c + 1) % NW)
                if m.r is not None or m.c:
                    down(m - 1, (c - 1) % NW)

            turn(Count(None, 0, 0), 0)
            run(pe, emit)
            down(Count(None, 0, NBLK - 1), NW - 1)

        @block.scalar
        def _(act):
            def emit(m, c):
                for f in range(NF):
                    wait(act, hidden, m * NF + (f + 1))
                    if f == 0:
                        wait(act, product, m - 1)
                    nc.scalar.activation(h[c % 2][:, f, :], h_ps[f][:, 0:BLK], func, bias=bias[c][:, f:f + 1])\
                      .then_inc(acted, 1)

            run(act, emit)

        @block.vector
        def _(dve):
            def keep_turned(m, u):
                wait(dve, turned, m + 1)
                wait(dve, hidden, (m - 1) * NF)
                nc.vector.tensor_copy(xT[u][:, :], t_ps[u][:, 0:BLK]).then_inc(kept, 1)

            def emit(m, c):
                u = c % 2
                if exists(m, 2):
                    keep_turned(m + 2, u)
                wait(dve, product, m + 1)
                wait(dve, y_stored[u], m.half() * 16)
                nc.vector.tensor_copy(y[u][:, :, :], y_ps[u][:, 0:TC * D].rearrange("p (t d) -> p t d", d=D))\
                  .then_inc(copied, 1)

            keep_turned(Count(None, 0, 0), 0)
            keep_turned(Count(None, 0, 1), 1)
            run(dve, emit)
            for n in range(NT):
                if n % GRP == 0:
                    dve.wait_ge(gathered[n // GRP], 16 * GRP)
                nc.vector.scalar_tensor_tensor(out=X[:, n, :], in0=back[:, n, :], scalar=gate[:, n:n + 1],
                                               in1=X[:, n, :], op0=ALU.mult, op1=ALU.add).then_inc(added, 1)


def ternary_weights(nc, link, w, absum, total_ps, wait_total, mean, inv, out):
    n = w.shape[1] * P
    link(nc.vector.tensor_reduce(absum, w, axis=AX.X, op=ALU.add, apply_absolute_value=True))
    wait_total()
    link(nc.vector.tensor_scalar(mean, total_ps, 1.0 / n, 1e-5, ALU.mult, ALU.max))
    link(nc.vector.reciprocal(inv, mean))
    link(nc.vector.tensor_scalar(out, w, inv, MAGIC, ALU.mult, ALU.add))
    link(nc.vector.tensor_scalar(out, out, -MAGIC, 1.0, ALU.add, ALU.min))
    link(nc.vector.tensor_scalar(out, out, -1.0, None, ALU.max))


def bitnet_ffn_stage(nc, stage, A, R, XN):
    X = R["X"]
    HID = 512
    NH = HID // P
    with Scope(nc, stage) as sc:
        w1 = sc.sb("w1", [D, HID])
        w2 = sc.sb("w2", [P, NH * D])
        w2b = sc.sb("w2b", [P, NH, D], BF16)
        cw = sc.sb("cw", [P, NH, 3])
        cb = sc.sb("cb", [P, NH])
        absum, mean, minv = sc.sb("absum", [P, 2]), sc.sb("mean", [P, 2]), sc.sb("minv", [P, 2])
        ones = sc.sb("ones", [P, P])
        amax, sinv, sx = sc.sb("amax", [P, NT]), sc.sb("sinv", [P, NT]), sc.sb("sx", [P, NT])
        q = sc.sb("q", [P, 2, QT, D])
        qT = sc.sb("qT", [D, 2, S])
        c0 = sc.sb("c0", [P, NH, S])
        c1 = sc.sb("c1", [P, NH, S])
        c2 = sc.sb("c2", [P, NH, S])
        act_h = sc.sb("act_h", [P, NH, S])
        hmax, hs, hinv = (sc.sb(n, [P, QT, 2]) for n in ("hmax", "hs", "hinv"))
        hq = sc.sb("hq", [P, QT, HID])
        hqb = sc.sb("hqb", [P, QT, HID], BF16)
        hT = sc.sb("hT", [P, QT, HID], BF16)
        x_ps = sc.ps("x_ps", [P, 512])
        u_ps = [sc.ps(f"u_ps{k}", [P, 512]) for k in range(NH)]
        tot_ps = u_ps[0]
        t_ps = [sc.ps(f"t_ps{k}", [P, HID]) for k in range(QT)]
        r_ps = sc.ps("r_ps", [P, QT, HID], BF16)
        loaded, step, summed, made, tokens = (sc.sem(n) for n in ("loaded", "step", "summed", "made", "tokens"))
        qdone, qturned, qkept, up, conv0, conv, silu, hturned, hstep, hback, hkept, down, xadd = (
            sc.sem(n) for n in ("qdone", "qturned", "qkept", "up", "conv0", "conv", "silu", "hturned", "hstep",
                                "hback", "hkept", "down", "xadd"))
        block = sc.block()
        fstep, bstep, qstep, passed = (sc.sem(n) for n in ("fstep", "bstep", "qstep", "passed"))
        qq = q[:, 0, :, :]

        @block.sync
        def _(sp):
            sp.dma_start(w1[:, :], A["L3_w1T"]).then_inc(loaded, 16)
            sp.dma_start(w2[:, :].rearrange("p (t d) -> p t d", t=NH), A["L3_w2T"].rearrange("(t p) d -> p t d", p=P))\
              .then_inc(loaded, 16)
            sp.dma_start(cw[:, :, :], A["L3_cw"].rearrange("(t p) k -> p t k", p=P)).then_inc(loaded, 16)
            sp.dma_start(cb[:, :], A["L3_cb"]).then_inc(loaded, 16)
            sp.wait_ge(loaded, 64)

        @block.gpsimd
        def _(pool):
            nc.gpsimd.memset(ones[:, :], 1.0).then_inc(made, 1)
            pool.wait_ge(tokens, 3)
            with pool.Fori(0, B) as r:
                b = Count(r, 1, 0)
                at = bass.ds((b * QT).v, QT)
                per_token = [P, QT, D]
                own_wait(pool, qturned, b, passed)
                nc.gpsimd.tensor_tensor(qq, XN[:, at, :], sinv[:, at].unsqueeze(2).broadcast_to(per_token),
                                        ALU.mult).then_inc(qstep, 1)
                own_wait(pool, qstep, b * 4 + 1, passed)
                nc.gpsimd.tensor_scalar(qq, qq, MAGIC, -MAGIC, ALU.add, ALU.add).then_inc(qstep, 1)
                own_wait(pool, qstep, b * 4 + 2, passed)
                nc.gpsimd.tensor_scalar(qq, qq, -128.0, 127.0, ALU.max, ALU.min).then_inc(qstep, 1)
                own_wait(pool, qstep, b * 4 + 3, passed)
                nc.gpsimd.tensor_tensor(qq, qq, sx[:, at].unsqueeze(2).broadcast_to(per_token),
                                        ALU.mult).then_inc(qstep, 1)
                own_wait(pool, qstep, b * 4 + 4, passed)
                pool.sem_inc(qdone, 1)

        @block.tensor
        def _(pe):
            pe.wait_ge(made, 1)
            for k in range(2):
                pe.wait_ge(tokens, k + 1)
                nc.tensor.matmul(tot_ps[:, k:k + 1], ones[:, :], absum[:, k:k + 1], start=True, stop=True)\
                  .then_inc(summed, 1)
            pe.wait_ge(tokens, 3)
            def turn_hidden(b):
                for n in range(NH):
                    wait(pe, silu, b * NH + (n + 1))
                    if n == 0:
                        wait(pe, hstep, b)
                    for k in range(QT):
                        last = nc.tensor.transpose(t_ps[k][:, n * P:(n + 1) * P], act_h[:, n, k * P:(k + 1) * P],
                                                   R["ident"][:, :])
                last.then_inc(hturned, 1)

            def front(b):
                wait(pe, qdone, b + 1)
                wait(pe, xadd, b - 1)
                for k in range(QT):
                    last = nc.tensor.transpose(x_ps[:, k * P:(k + 1) * P], q[:, 0, k, :], R["ident"][:, :])
                last.then_inc(qturned, 1)
                wait(pe, qkept, b + 1)
                for n in range(NH):
                    wait(pe, conv, b * NH + (n + 1))
                    nc.tensor.matmul(u_ps[n][:, 0:S], w1[:, n * P:(n + 1) * P], qT[:, 0, :],
                                     start=True, stop=True).then_inc(up, 1)

            def back(b):
                wait(pe, hstep, b + 1)
                for k in range(QT):
                    for n in range(NH):
                        last = nc.tensor.transpose(r_ps[:, k, n * P:(n + 1) * P], hqb[:, k, n * P:(n + 1) * P],
                                                   R["identb"][:, :])
                last.then_inc(hback, 1)
                wait(pe, hkept, b + 1)
                for k in range(QT):
                    for n in range(NH):
                        last = nc.tensor.matmul(x_ps[:, S + k * D:S + (k + 1) * D], hT[:, k, n * P:(n + 1) * P],
                                                w2b[:, n, :], start=(n == 0), stop=(n == NH - 1))
                last.then_inc(down, 1)

            front(Count(None, 0, 0))
            with pe.Fori(0, B - 1) as r:
                b = Count(r, 1, 0)
                turn_hidden(b)
                front(b + 1)
                back(b)
            turn_hidden(Count(None, 0, B - 1))
            back(Count(None, 0, B - 1))

        @block.scalar
        def _(act):
            act.wait_ge(tokens, 3)
            def front(b):
                wait(act, qturned, b + 1)
                nc.scalar.activation(qT[:, 0, :], x_ps[:, 0:S], ACT.Copy).then_inc(qkept, 1)
                for n in range(NH):
                    wait(act, up, b * NH + (n + 1))
                    wait(act, conv, b * NH + (n + 1))
                    nc.scalar.activation(c0[:, n, :], u_ps[n][:, 0:S], ACT.Identity,
                                         scale=cw[:, n, 1:2], bias=cb[:, n:n + 1]).then_inc(conv0, 1)

            def apply_silu(b):
                for n in range(NH):
                    wait(act, conv, b * NH + (NH + n + 1))
                    if n == 0:
                        wait(act, hturned, b)
                    nc.scalar.activation(act_h[:, n, :], c2[:, n, :], ACT.Silu).then_inc(silu, 1)

            def back(b):
                wait(act, hback, b + 1)
                nc.scalar.activation(hT[:, :, :], r_ps[:, :, :], ACT.Copy).then_inc(hkept, 1)

            front(Count(None, 0, 0))
            apply_silu(Count(None, 0, 0))
            with act.Fori(0, B - 1) as r:
                b = Count(r, 1, 0)
                front(b + 1)
                back(b)
                apply_silu(b + 1)
            back(Count(None, 0, B - 1))

        @block.vector
        def _(dve):
            links = [0]

            def link(ins):
                links[0] += 1
                ins.then_inc(step, 1)
                dve.wait_ge(step, links[0])

            dve.wait_ge(loaded, 64)
            for k, w in enumerate((w1, w2)):
                def total():
                    dve.sem_inc(tokens, 1)
                    dve.wait_ge(summed, k + 1)
                ternary_weights(nc, link, w[:, :], absum[:, k:k + 1], tot_ps[:, k:k + 1], total,
                                mean[:, k:k + 1], minv[:, k:k + 1], w[:, :])
            link(nc.vector.tensor_copy(w2b[:, :, :], w2[:, :].rearrange("p (t d) -> p t d", t=NH)))
            link(nc.vector.tensor_scalar(cw[:, :, :], cw[:, :, :], mean[:, 0:1], None, ALU.mult))
            link(nc.vector.tensor_reduce(amax[:, :], XN[:, :, :], axis=AX.X, op=ALU.max, apply_absolute_value=True))
            link(nc.vector.tensor_scalar(amax[:, :], amax[:, :], 1e-5, None, ALU.max))
            link(nc.vector.reciprocal(sinv[:, :], amax[:, :]))
            link(nc.vector.tensor_scalar(sinv[:, :], sinv[:, :], 127.0, None, ALU.mult))
            link(nc.vector.tensor_scalar(sx[:, :], amax[:, :], 1.0 / 127.0, None, ALU.mult))
            dve.sem_inc(tokens, 1)
            dve.sem_inc(conv, NH)
            NB = 9

            def chained(sem, at, ins):
                ins.then_inc(sem, 1)
                wait(dve, sem, at)

            def convolve(b):
                for n in range(NH):
                    wait(dve, conv0, b * NH + (n + 1))
                    nc.vector.tensor_copy(c1[:, n, 0:1], c0[:, n, 0:1])
                    nc.vector.scalar_tensor_tensor(
                        out=c1[:, n, 1:S], in0=u_ps[n][:, 0:S - 1], scalar=cw[:, n, 0:1], in1=c0[:, n, 1:S],
                        op0=ALU.mult, op1=ALU.add).then_inc(fstep, 1)
                wait(dve, silu, b * NH)
                for n in range(NH):
                    wait(dve, fstep, b * NH + (n + 1))
                    nc.vector.tensor_copy(c2[:, n, S - 1:S], c1[:, n, S - 1:S])
                    nc.vector.scalar_tensor_tensor(
                        out=c2[:, n, 0:S - 1], in0=u_ps[n][:, 1:S], scalar=cw[:, n, 2:3], in1=c1[:, n, 0:S - 1],
                        op0=ALU.mult, op1=ALU.add).then_inc(conv, 1)

            def quantise_hidden(b):
                def link(k, ins):
                    chained(bstep, b * NB + k, ins)

                wait(dve, hturned, b + 1)
                for k in range(QT):
                    ins = nc.vector.tensor_reduce(hmax[:, k, 0:1], t_ps[k][:, :], axis=AX.X, op=ALU.max,
                                                  apply_absolute_value=True)
                link(1, ins)
                link(2, nc.vector.tensor_scalar(hmax[:, :, 1], hmax[:, :, 0], 1e-5, None, ALU.max))
                link(3, nc.vector.reciprocal(hinv[:, :, 0], hmax[:, :, 1]))
                nc.vector.tensor_scalar(hs[:, :, 0], hmax[:, :, 1], 1.0 / 127.0, mean[:, 1:2], ALU.mult, ALU.mult)
                link(4, nc.vector.tensor_scalar(hinv[:, :, 1], hinv[:, :, 0], 127.0, None, ALU.mult))
                for k in range(QT):
                    ins = nc.vector.tensor_scalar(hq[:, k, :], t_ps[k][:, :], hinv[:, k, 1:2], MAGIC, ALU.mult, ALU.add)
                link(5, ins)
                link(6, nc.vector.tensor_scalar(hq[:, :, :], hq[:, :, :], -MAGIC, -128.0, ALU.add, ALU.max))
                wait(dve, hback, b)
                link(7, nc.vector.tensor_scalar(hqb[:, :, :], hq[:, :, :], 127.0, None, ALU.min))
                dve.sem_inc(hstep, 1)

            def add_output(b):
                def link(k, ins):
                    chained(bstep, b * NB + k, ins)

                wait(dve, down, b + 1)
                xx = X[:, bass.ds((b * QT).v, QT), :]
                for k in range(QT):
                    ins = nc.vector.tensor_scalar(hq[:, k, 0:D], x_ps[:, S + k * D:S + (k + 1) * D], hs[:, k, 0:1],
                                                  None, ALU.mult)
                link(8, ins)
                link(9, nc.vector.tensor_tensor(xx, xx, hq[:, :, 0:D], ALU.add))
                dve.sem_inc(xadd, 1)

            convolve(Count(None, 0, 0))
            with dve.Fori(0, B - 1) as r:
                b = Count(r, 1, 0)
                quantise_hidden(b)
                convolve(b + 1)
                add_output(b)
            quantise_hidden(Count(None, 0, B - 1))
            add_output(Count(None, 0, B - 1))


def context_rows_dma(nc, engine, dst, src, sem):
    engine.dma_start(dst[:, 0:KT - 1, 0:D], src[0:(KT - 1) * P, :].rearrange("(t p) d -> p t d", p=P)).then_inc(sem, 16)
    engine.dma_start(dst[0:LAST, KT - 1, 0:D], src[(KT - 1) * P:S2, :]).then_inc(sem, 16)


def wide_attention_stage(nc, stage, A, R, XT):
    X = R["X"]
    SCALE = 1.0 / 32.0
    NPROJ = 5
    NG = 4
    with Scope(nc, stage) as sc:
        wk, wq = sc.sb("wk", [D, D]), sc.sb("wq", [D, D])
        bk, bq = sc.sb("bk", [D, 1]), sc.sb("bq", [D, 1])
        ctxT = [sc.sb(f"ctxT{u}", [D, S2]) for u in range(2)]
        rows = [sc.sb(f"rows{u}", [P, KT, D + 1]) for u in range(2)]
        kT = [sc.sb(f"kT{u}", [D, S2]) for u in range(2)]
        qT = [sc.sb(f"qT{u}", [D, S]) for u in range(2)]
        E = [sc.sb(f"E{u}", [P, S2]) for u in range(2)]
        ET = sc.sb("ET", [P, KT, P])
        mpart = sc.sb("mpart", [P, 2, 4])
        negm = sc.sb("negm", [P, 2, 2])
        rl = sc.sb("rl", [P, 2])
        s_ps = [sc.ps(f"s_ps{j}", [P, 512]) for j in range(4)]
        t_ps = [sc.ps(f"t_ps{j}", [P, 512]) for j in range(2)]
        o_ps = sc.ps("o_ps", [P, D + 1])
        p_ps = sc.ps("p_ps", [P, 512])
        w_loaded, ones_set = sc.sem("w_loaded"), sc.sem("ones_set")
        t_loaded = [sc.sem(f"t_loaded{u}") for u in range(2)]
        r_loaded = [sc.sem(f"r_loaded{u}") for u in range(2)]
        proj, proj_kept, scored, maxed, negated, expd, turned, kept_a, kept_v, summed, recip, added, passed = (
            sc.sem(n) for n in ("proj", "proj_kept", "scored", "maxed", "negated", "expd", "turned", "kept_a",
                                "kept_v", "summed", "recip", "added", "passed"))
        block = sc.block()

        def run(engine, emit):
            with engine.Fori(0, B // 2 - 1) as r:
                for u in range(2):
                    emit(Count(r, 2, u), u, True, True)
            emit(Count(None, 0, B - 2), 0, True, False)
            emit(Count(None, 0, B - 1), 1, False, False)

        @block.sync
        def _(sp):
            for dst, src in ((wk, "L2_wk"), (wq, "L2_wq"), (bk, "L2_bk"), (bq, "L2_bq")):
                sp.dma_start(dst[:, :], A[src]).then_inc(w_loaded, 16)
            sp.dma_start(ctxT[0][:, :], A["ctxT"][0]).then_inc(t_loaded[0], 16)
            sp.dma_start(ctxT[1][:, :], A["ctxT"][1]).then_inc(t_loaded[1], 16)
            sp.wait_ge(ones_set, 2)
            context_rows_dma(nc, sp, rows[0], A["ctx"][0], r_loaded[0])

            def emit(b, u, nxt, after):
                if nxt:
                    own_wait(sp, summed, b * 2, passed)
                    context_rows_dma(nc, sp, rows[1 - u], A["ctx"][(b + 1).v], r_loaded[1 - u])
                if after:
                    own_wait(sp, proj, (b + 1) * NPROJ, passed)
                    sp.dma_start(ctxT[u][:, :], A["ctxT"][(b + 2).v]).then_inc(t_loaded[u], 16)

            run(sp, emit)

        @block.gpsimd
        def _(pool):
            for t in rows:
                nc.gpsimd.memset(t[:, :, :], 1.0).then_inc(ones_set, 1)

        @block.tensor
        def _(pe):
            def project(b, u, k):
                if k == 0:
                    wait(pe, t_loaded[u], b.half() * 16 + 16)
                wait(pe, proj_kept, b * NPROJ + k)
                if k < 4:
                    at, width = K_COLS[k]
                    nc.tensor.matmul(p_ps[:, 0:width], wk[:, :], ctxT[u][:, at:at + width],
                                     start=True, stop=True).then_inc(proj, 1)
                else:
                    nc.tensor.matmul(p_ps[:, 0:S], wq[:, :], XT[:, bass.ds((b * S).v, S)],
                                     start=True, stop=True).then_inc(proj, 1)

            def scores(n, u, qt):
                for j, (at, width) in enumerate(K_COLS):
                    wait(pe, expd, (n - 1) * 4 + (j + 1))
                    nc.tensor.matmul(s_ps[j][:, 0:width], qT[u][:, qt * P:(qt + 1) * P], kT[u][:, at:at + width],
                                     start=True, stop=True).then_inc(scored, 1)

            def emit(b, u, nxt, after):
                for qt in range(QT):
                    n = b * 2 + qt
                    if qt == 0:
                        scores(n + 1, u, 1)
                    elif nxt:
                        wait(pe, proj_kept, (b + 2) * NPROJ)
                        scores(n + 1, 1 - u, 0)
                    for g in range(NG):
                        wait(pe, expd, n * 4 + min(g + 2, 4))
                        wait(pe, kept_a if g % 2 == 0 else kept_v, n * 2 + g // 2)
                        for t in range(4 * g, min(4 * g + 4, KT)):
                            w = rows_of(t)
                            last = nc.tensor.transpose(t_ps[g % 2][0:w, (t % 4) * P:(t % 4 + 1) * P],
                                                       E[qt][:, t * P:t * P + w], R["ident"][:, :])
                        last.then_inc(turned, 1)
                        if nxt and qt == 0:
                            project(b + 1, 1 - u, g)
                    if nxt and qt == 0:
                        project(b + 1, 1 - u, 4)
                    if qt == 0:
                        wait(pe, r_loaded[u], b.half() * 32 + 32)
                    wait(pe, added, n)
                    for t in range(KT):
                        if t % 4 == 0:
                            g = t // 4
                            wait(pe, kept_a if g % 2 == 0 else kept_v, n * 2 + (g // 2 + 1))
                        w = rows_of(t)
                        last = nc.tensor.matmul(o_ps[:, :], ET[0:w, t, :], rows[u][0:w, t, :],
                                                start=(t == 0), stop=(t == KT - 1))
                    last.then_inc(summed, 1)

            pe.wait_ge(w_loaded, 4 * 16)
            first = Count(None, 0, 0)
            for k in range(NPROJ):
                project(first, 0, k)
            pe.wait_ge(proj_kept, NPROJ)
            scores(first, 0, 0)
            run(pe, emit)

        @block.scalar
        def _(act):
            def keep_projection(b, u, k):
                wait(act, proj, b * NPROJ + (k + 1))
                if k < 4:
                    at, width = K_COLS[k]
                    nc.scalar.activation(kT[u][:, at:at + width], p_ps[:, 0:width], ACT.Identity, bias=bk[:, 0:1])\
                      .then_inc(proj_kept, 1)
                else:
                    nc.scalar.activation(qT[u][:, :], p_ps[:, 0:S], ACT.Identity, bias=bq[:, 0:1])\
                      .then_inc(proj_kept, 1)

            def exp(n, qt):
                wait(act, negated, n * 2 + 2)
                for j, (at, width) in enumerate(K_COLS):
                    nc.scalar.activation(E[qt][:, at:at + width], s_ps[j][:, 0:width], ACT.Exp, scale=SCALE,
                                         bias=negm[:, qt, 1:2]).then_inc(expd, 1)

            def emit(b, u, nxt, after):
                for qt in range(QT):
                    n = b * 2 + qt
                    for g in range(NG):
                        if g % 2 == 0:
                            wait(act, turned, n * NG + (g + 1))
                            tiles, w = (4, P) if g < 3 else (1, LAST)
                            nc.scalar.activation(ET[0:w, 4 * g:4 * g + tiles, :], t_ps[0][0:w, 0:tiles * P]
                                                 .rearrange("p (t q) -> p t q", q=P), ACT.Copy).then_inc(kept_a, 1)
                        if nxt and qt == 0:
                            keep_projection(b + 1, 1 - u, g)
                    if nxt and qt == 0:
                        keep_projection(b + 1, 1 - u, 4)
                    if qt == 0 or nxt:
                        exp(n + 1, 1 - qt)

            act.wait_ge(w_loaded, 4 * 16)
            first = Count(None, 0, 0)
            for k in range(NPROJ):
                keep_projection(first, 0, k)
            exp(first, 0)
            run(act, emit)

        @block.vector
        def _(dve):
            def maximum(n, qt):
                for j, (at, width) in enumerate(K_COLS):
                    wait(dve, scored, n * 4 + (j + 1))
                    if j == 0:
                        wait(dve, negated, (n - 1) * 2)
                    last = nc.vector.reduce_max(mpart[:, qt, j:j + 1], s_ps[j][:, 0:width], AX.X).then_inc(maxed, 1)
                wait(dve, maxed, n * 4 + 4)
                wait(dve, expd, (n - 1) * 4)
                nc.vector.tensor_reduce(negm[:, qt, 0:1], mpart[:, qt, :], axis=AX.X, op=ALU.max,
                                        negate=True).then_inc(negated, 1)
                wait(dve, negated, n * 2 + 1)
                nc.vector.tensor_scalar(negm[:, qt, 1:2], negm[:, qt, 0:1], SCALE, None, ALU.mult).then_inc(negated, 1)

            def emit(b, u, nxt, after):
                for qt in range(QT):
                    n = b * 2 + qt
                    if qt == 0 or nxt:
                        maximum(n + 1, 1 - qt)
                    for g in (1, 3):
                        wait(dve, turned, n * NG + (g + 1))
                        tiles, w = (4, P) if g < 3 else (1, LAST)
                        nc.vector.tensor_copy(ET[0:w, 4 * g:4 * g + tiles, :], t_ps[1][0:w, 0:tiles * P]
                                              .rearrange("p (t q) -> p t q", q=P)).then_inc(kept_v, 1)
                    wait(dve, summed, n + 1)
                    nc.vector.reciprocal(rl[:, qt:qt + 1], o_ps[:, D:D + 1]).then_inc(recip, 1)
                    wait(dve, recip, n + 1)
                    xb = X[:, bass.ds(n.v, 1), :].rearrange("p a d -> p (a d)")
                    nc.vector.scalar_tensor_tensor(out=xb, in0=o_ps[:, 0:D], scalar=rl[:, qt:qt + 1], in1=xb,
                                                   op0=ALU.mult, op1=ALU.add).then_inc(added, 1)

            maximum(Count(None, 0, 0), 0)
            run(dve, emit)


def history_kernels_stage(nc, stage, A, R, taps):
    C = 2 * D
    C4 = C // 4
    NF = (KT + 1) // 2
    NG = (KT + 3) // 4
    W = 2 * P + 2
    with Scope(nc, stage) as sc:
        hw = sc.sb("hw", [D, C])
        hb, hg, hbeta = (sc.sb(n, [P, C]) for n in ("hb", "hg", "hbeta"))
        w1 = sc.sb("w1", [P, 2, C4])
        b1, w2 = sc.sb("b1", [C4, 1]), sc.sb("w2", [C4, 1])
        b2 = sc.sb("b2", [P, 1])
        kw1, kw2 = sc.sb("kw1", [P, 2, D]), sc.sb("kw2", [D, H * 9])
        kb1, kg, kbeta = (sc.sb(n, [B, D]) for n in ("kb1", "kg", "kbeta"))
        kb2 = sc.sb("kb2", [B, H * 9])
        eps, ones = sc.sb("eps", [P, 1]), sc.sb("ones", [P, P])
        ctxT = [sc.sb(f"ctxT{u}", [D, S2]) for u in range(2)]
        pre = [sc.sb(f"pre{u}", [P, KT, C]) for u in range(2)]
        eh = [sc.sb(f"eh{u}", [P, KT, C]) for u in range(2)]
        st = [sc.sb(f"st{u}", [P, KT, 6]) for u in range(2)]
        mv = [sc.sb(f"mv{u}", [P, KT, 2]) for u in range(2)]
        sd, rstd = sc.sb("sd", [P, 2, KT]), sc.sb("rstd", [P, 2, KT])
        ehT = [sc.sb(f"ehT{u}", [P, 2, 4 * P]) for u in range(2)]
        h1T = sc.sb("h1T", [C4, 4 * P])
        aw, e = sc.sb("aw", [P, 2, KT]), sc.sb("e", [P, 2, KT])
        amax = sc.sb("amax", [P, 2, 3])
        esum = sc.sb("esum", [P, 2, 2])
        cc = sc.sb("cc", [P, 2, B])
        g1, gT = sc.sb("g1", [B, D]), sc.sb("gT", [D, B])
        kst, kmv = sc.sb("kst", [B, 6]), sc.sb("kmv", [B, 4])
        kp, kmax = sc.sb("kp", [B, H, 9]), sc.sb("kmax", [B, 3, H])
        rows0 = sc.sb("rows0", [B, H * 3, W])
        h_ps = [sc.ps(f"h_ps{u}", [P, 2, C]) for u in range(2)]
        t_ps = [sc.ps(f"t_ps{u}", [P, 4 * P]) for u in range(2)]
        w_ps = sc.ps("w_ps", [P, 4 * P])
        aw_ps = sc.ps("aw_ps", [P, KT])
        cc_ps = sc.ps("cc_ps", [P, C])
        cs_ps = sc.ps("cs_ps", [P, 3])
        partial = sc.sb("partial", [P, C])
        cc_cleared, partial_kept, collected = (sc.sem(n) for n in ("cc_cleared", "partial_kept", "collected"))
        w_loaded, made = sc.sem("w_loaded"), sc.sem("made")
        c_loaded = [sc.sem(f"c_loaded{u}") for u in range(2)]
        projected, biased, stats, aggr, rooted, scaled, centred, normed, eh_done, turned, kept, mixed, h1_done = (
            sc.sem(n) for n in ("projected", "biased", "stats", "aggr", "rooted", "scaled", "centred", "normed",
                                "eh_done", "turned", "kept", "mixed", "h1_done"))
        mlp, act_mlp, mstep, e_done, mvset, rows_done = (
            sc.sem(n) for n in ("mlp", "act_mlp", "mstep", "e_done", "mvset", "rows_done"))
        passed_v, divided = sc.sem("passed_v"), sc.sem("divided")
        weighed, aw_kept, pmax, allmax, negmax, exped, summed, pooled, cc_kept, passed, stored = (
            sc.sem(n) for n in ("weighed", "aw_kept", "pmax", "allmax", "negmax", "exped", "summed", "pooled",
                                "cc_kept", "passed", "stored"))
        block = sc.block()

        def run(engine, emit):
            def at(i):
                return Count(None, 0, i)

            emit(at(0), 0, False, True, True)
            emit(at(1), 1, True, True, True)
            with engine.Fori(0, (B - 4) // 2) as r:
                for u in range(2):
                    emit(Count(r, 2, 2 + u), u, True, True, True)
            emit(at(B - 2), 0, True, True, True)
            emit(at(B - 1), 1, True, True, False)
            emit(at(B), 0, True, False, False)

        def group(g):
            return range(4 * g, min(4 * g + 4, KT)), P if g < NG - 1 else LAST

        def fills_behind(g):
            return (range(0, 4), range(4, NF), range(0), range(0))[g]

        @block.sync
        def _(sp):
            loads = ((hw, A["hist_W"]), (hb, A["hist_b"].partition_broadcast(P)),
                     (hg, A["hist_ln_g"].partition_broadcast(P)), (hbeta, A["hist_ln_b"].partition_broadcast(P)),
                     (b1, A["ctx_b1"]), (w2, A["ctx_W2"]), (b2, A["ctx_b2"].partition_broadcast(P)),
                     (kw2, A["kg_W2"]), (kb1, A["kg_b1"].partition_broadcast(B)),
                     (kg, A["kg_ln_g"].partition_broadcast(B)), (kbeta, A["kg_ln_b"].partition_broadcast(B)),
                     (kb2, A["kg_b2"].partition_broadcast(B)))
            sp.dma_start(ctxT[0][:, :], A["ctxT"][0]).then_inc(c_loaded[0], 16)
            sp.dma_start(ctxT[1][:, :], A["ctxT"][1]).then_inc(c_loaded[1], 16)
            for dst, src in loads:
                sp.dma_start(dst[:, :], src).then_inc(w_loaded, 16)
            for dst, src in ((w1, A["ctx_W1"]), (kw1, A["kg_W1"])):
                sp.dma_start(dst[:, :, :], src.rearrange("(c p) n -> p c n", p=P)).then_inc(w_loaded, 16)

            def emit(b, u, prev, cur, nxt):
                if nxt and not (b.r is None and b.c == B - 2):
                    own_wait(sp, projected, b * NF + NF, passed)
                    sp.dma_start(ctxT[u][:, :], A["ctxT"][(b + 2).v]).then_inc(c_loaded[u], 16)

            run(sp, emit)
            sp.wait_ge(rows_done, 1)
            sp.dma_start(taps.rearrange("b h i w -> b (h i) w"), rows0[:, :, :]).then_inc(stored, 16)
            sp.wait_ge(stored, 16)

        NW = 14 * 16

        @block.gpsimd
        def _(pool):
            nc.gpsimd.memset(ones[:, :], 1.0).then_inc(made, 1)
            nc.gpsimd.memset(eps[:, :], LN_EPS).then_inc(made, 1)
            nc.gpsimd.memset(aw[:, :, :], -BIG).then_inc(made, 1)

            def emit(b, u, prev, cur, nxt):
                for g in range(NG if cur else 1):
                    if cur:
                        tiles, rows = group(g)
                        own_wait(pool, centred, b * NG + (g + 1), passed)
                        if g == 0:
                            own_wait(pool, scaled, b + 1, passed)
                        g_rows = pre[u][0:rows, tiles[0]:tiles[-1] + 1, :]
                        shape = [rows, len(tiles), C]
                        nc.gpsimd.tensor_tensor(g_rows, g_rows, rstd[0:rows, u, tiles[0]:tiles[-1] + 1]
                                                .unsqueeze(2).broadcast_to(shape), ALU.mult).then_inc(divided, 1)
                        own_wait(pool, divided, b * NG + (g + 1), passed)
                        nc.gpsimd.tensor_tensor(g_rows, g_rows, hbeta[0:rows, :].unsqueeze(1).broadcast_to(shape),
                                                ALU.add).then_inc(normed, 1)
                    if g == min(2, NG * cur) and prev:
                        p = b - 1
                        own_wait(pool, pmax, p + 1, passed)
                        nc.gpsimd.partition_all_reduce(amax[:, 1 - u, 1:2], amax[:, 1 - u, 0:1], channels=P,
                                                       reduce_op=bass.bass_isa.ReduceOp.max).then_inc(allmax, 1)

            run(pool, emit)

        @block.tensor
        def _(pe):
            pe.wait_ge(w_loaded, NW)
            pe.wait_ge(made, 3)
            pe.wait_ge(cc_cleared, 1)

            def fill(b, u, f):
                if f == 0:
                    wait(pe, c_loaded[u], b.half() * 16 + 16)
                wait(pe, biased, b * NF + (f if f == 0 else f - 1))
                for t in range(2 * f, min(2 * f + 2, KT)):
                    rows = rows_of(t)
                    last = nc.tensor.matmul(h_ps[f % 2][0:rows, t % 2, :], ctxT[u][:, t * P:t * P + rows], hw[:, :],
                                            start=True, stop=True)
                last.then_inc(projected, 1)

            def turn(b, u, g):
                tiles, rows = group(g)
                wait(pe, eh_done, b * NG + (g + 1))
                wait(pe, kept, b * NG + g)
                for half in range(2):
                    for t in tiles:
                        last = nc.tensor.transpose(t_ps[half][:, (t % 4) * P:(t % 4) * P + rows],
                                                   eh[u][0:rows, t, half * P:(half + 1) * P],
                                                   R["ident"][0:rows, 0:rows])
                last.then_inc(turned, 1)

            def mix(b, g):
                width = 4 * P if g < NG - 1 else LAST
                wait(pe, kept, b * NG + (g + 1))
                wait(pe, h1_done, b * NG + g)
                for half in range(2):
                    last = nc.tensor.matmul(w_ps[0:C4, 0:width], w1[:, half, :], ehT[g % 2][:, half, 0:width],
                                            start=(half == 0), stop=(half == 1))
                last.then_inc(mixed, 1)

            def weigh(b, g):
                tiles, rows = group(g)
                wait(pe, h1_done, b * NG + (g + 1))
                if g == 0:
                    wait(pe, aw_kept, b)
                for t in tiles:
                    k = (t % 4) * P
                    last = nc.tensor.matmul(aw_ps[0:rows, t:t + 1], h1T[:, k:k + rows], w2[:, :],
                                            start=True, stop=True)
                if g == NG - 1:
                    last.then_inc(weighed, 1)

            def emit(b, u, prev, cur, nxt):
                for g in range(NG if cur else 1):
                    if nxt:
                        for f in fills_behind(g)[:2]:
                            fill(b + 1, 1 - u, f)
                    if cur:
                        turn(b, u, g)
                    before = (b - 1, NG - 1) if g == 0 else (b, g - 1)
                    if g or prev:
                        mix(*before)
                    if nxt:
                        for f in fills_behind(g)[2:]:
                            fill(b + 1, 1 - u, f)
                    if g or prev:
                        weigh(*before)
                    if g == 0 and not (b.r is None and b.c < 2):
                        collect(b - 2, u)
                    if prev and (g == 2 or not cur):
                        wait(pe, exped, b)
                        wait(pe, partial_kept, b - 1)
                        pool_rows(b - 1, 1 - u)

            def pool_rows(p, u):
                for t in range(KT):
                    rows, k = rows_of(t), t % 4
                    last = nc.tensor.matmul(cc_ps[32 * k:32 * k + 1, :], e[0:rows, u, t:t + 1], eh[u][0:rows, t, :],
                                            start=(t < 4), stop=(t + 4 >= KT), tile_position=(0, 32 * k))
                last.then_inc(pooled, 1)

            def collect(p, u):
                wait(pe, partial_kept, p + 1)
                wait(pe, cc_kept, p)
                nc.tensor.matmul(cs_ps[:, 2:3], ones[:, :], esum[:, u, 0:1], start=True, stop=True)
                for half in range(2):
                    last = nc.tensor.matmul(cs_ps[:, half:half + 1], partial[:, half * P:(half + 1) * P],
                                            ones[:, 0:1], start=True, stop=True)
                last.then_inc(collected, 1)

            first = Count(None, 0, 0)
            for f in range(NF):
                fill(first, 0, f)
            run(pe, emit)
            collect(Count(None, 0, B - 1), (B - 1) % 2)
            pe.wait_ge(cc_kept, B)
            for half in range(2):
                last = nc.tensor.matmul(w_ps[0:B, 0:D], cc[:, half, :], kw1[:, half, :],
                                        start=(half == 0), stop=(half == 1))
            last.then_inc(mlp, 1)
            pe.wait_ge(act_mlp, 2)
            nc.tensor.transpose(t_ps[0][:, 0:B], g1[:, :], R["ident"][0:B, 0:B]).then_inc(mlp, 1)
            pe.wait_ge(mstep, 7)
            nc.tensor.matmul(w_ps[0:B, 0:H * 9], gT[:, :], kw2[:, :], start=True, stop=True).then_inc(mlp, 1)

        @block.scalar
        def _(act):
            act.wait_ge(made, 3)
            act.wait_ge(w_loaded, NW)

            def root(b, u):
                wait(act, aggr, b * KT + KT)
                nc.scalar.activation(sd[:, u, :], mv[u][:, :, 1], ACT.Sqrt, bias=eps[:, 0:1]).then_inc(rooted, 1)

            def exp(b, u):
                wait(act, negmax, b + 1)
                nc.scalar.activation(e[:, u, :], aw[:, u, :], ACT.Exp, bias=amax[:, u, 2:3]).then_inc(e_done, 1)

            def gelu(b, u, g):
                tiles, rows = group(g)
                wait(act, normed, b * NG + (g + 1))
                if g == 0:
                    wait(act, pooled, b - 1)
                nc.scalar.activation(eh[u][0:rows, tiles[0]:tiles[-1] + 1, :],
                                     pre[u][0:rows, tiles[0]:tiles[-1] + 1, :], ACT.Gelu).then_inc(eh_done, 1)

            def keep(b, g):
                width = 4 * P if g < NG - 1 else LAST
                wait(act, turned, b * NG + (g + 1))
                wait(act, mixed, b * NG + (g - 1))
                nc.scalar.activation(ehT[g % 2][:, 0, 0:width], t_ps[0][:, 0:width], ACT.Copy)
                nc.scalar.activation(ehT[g % 2][:, 1, 0:width], t_ps[1][:, 0:width], ACT.Copy).then_inc(kept, 1)

            def mixed_gelu(b, g):
                width = 4 * P if g < NG - 1 else LAST
                wait(act, mixed, b * NG + (g + 1))
                nc.scalar.activation(h1T[:, 0:width], w_ps[0:C4, 0:width], ACT.Gelu, bias=b1[:, 0:1])\
                  .then_inc(h1_done, 1)

            def emit(b, u, prev, cur, nxt):
                if cur:
                    gelu(b, u, 0)
                    gelu(b, u, 1)
                for g in range(NG if cur else 1):
                    if cur:
                        keep(b, g)
                    if g or prev:
                        mixed_gelu(*((b - 1, NG - 1) if g == 0 else (b, g - 1)))
                    if cur and g + 2 < NG:
                        gelu(b, u, g + 2)
                    if not cur or g == 1:
                        if prev:
                            exp(b - 1, 1 - u)
                        if nxt:
                            root(b + 1, 1 - u)

            root(Count(None, 0, 0), 0)
            run(act, emit)
            act.wait_ge(mstep, 3)
            nc.scalar.activation(kmv[:, 2:3], kmv[:, 1:2], ACT.Sqrt, bias=eps[0:B, 0:1]).then_inc(act_mlp, 1)
            act.wait_ge(mstep, 6)
            nc.scalar.activation(g1[:, :], g1[:, :], ACT.Gelu).then_inc(act_mlp, 1)
            act.wait_ge(mstep, 10)
            nc.scalar.activation(kp[:, :, :], kp[:, :, :], ACT.Exp).then_inc(act_mlp, 1)

        @block.vector
        def _(dve):
            dve.wait_ge(w_loaded, NW)
            dve.wait_ge(made, 3)

            def add_bias(b, u, f):
                tiles = range(2 * f, min(2 * f + 2, KT))
                rows = rows_of(tiles[-1])
                wait(dve, projected, b * NF + (f + 1))
                dst = pre[u][0:rows, tiles[0]:tiles[-1] + 1, :]
                nc.vector.tensor_tensor(dst, h_ps[f % 2][0:rows, 0:len(tiles), :],
                                        hb[0:rows, :].unsqueeze(1).broadcast_to([rows, len(tiles), C]),
                                        ALU.add).then_inc(biased, 1)
                wait(dve, biased, b * NF + (f + 1))
                for t in tiles:
                    nc.vector.bn_stats(st[u][0:rows, t, :], pre[u][0:rows, t, :]).then_inc(stats, 1)

            def aggregate(b, u):
                wait(dve, stats, b * KT + KT)
                dve.sem_inc(passed_v, 1)
                for t in range(KT):
                    nc.vector.bn_aggr(mv[u][0:rows_of(t), t, :], st[u][0:rows_of(t), t, :]).then_inc(aggr, 1)

            def keep_partial(p):
                wait(dve, pooled, p + 1)
                wait(dve, collected, p)
                nc.vector.tensor_copy(partial[:, :], cc_ps[:, :]).then_inc(partial_kept, 1)

            def keep_pool(p, u):
                wait(dve, collected, p + 1)
                nc.vector.reciprocal(esum[:, u, 1:2], cs_ps[:, 2:3]).then_inc(summed, 1)
                wait(dve, summed, p + 1)
                nc.vector.tensor_scalar(cc[:, :, bass.ds(p.v, 1)].rearrange("p a b -> p (a b)"), cs_ps[:, 0:2],
                                        esum[:, u, 1:2], None, ALU.mult).then_inc(cc_kept, 1)

            def centre(b, u, g):
                tiles, rows = group(g)
                if g == 0:
                    wait(dve, aggr, b * KT + KT)
                for t in tiles:
                    last = nc.vector.scalar_tensor_tensor(
                        out=pre[u][0:rows, t, :], in0=pre[u][0:rows, t, :], scalar=mv[u][0:rows, t, 0:1],
                        in1=hg[0:rows, :], op0=ALU.subtract, op1=ALU.mult)
                last.then_inc(centred, 1)

            def invert(b, u):
                wait(dve, rooted, b + 1)
                nc.vector.reciprocal(rstd[:, u, :], sd[:, u, :]).then_inc(scaled, 1)

            def keep_weights(b, u):
                wait(dve, weighed, b + 1)
                nc.vector.tensor_scalar(aw[:, u, 0:KT - 1], aw_ps[:, 0:KT - 1], b2[:, 0:1], None, ALU.add)
                nc.vector.tensor_scalar(aw[0:LAST, u, KT - 1:KT], aw_ps[0:LAST, KT - 1:KT], b2[0:LAST, 0:1], None,
                                        ALU.add).then_inc(aw_kept, 1)
                wait(dve, aw_kept, b + 1)
                nc.vector.reduce_max(amax[:, u, 0:1], aw[:, u, :], AX.X).then_inc(pmax, 1)

            def negate(b, u):
                wait(dve, allmax, b + 1)
                nc.vector.tensor_scalar(amax[:, u, 2:3], amax[:, u, 1:2], -1.0, None, ALU.mult).then_inc(negmax, 1)

            def sum_exp(b, u):
                wait(dve, e_done, b + 1)
                nc.vector.reduce_sum(esum[:, u, 0:1], e[:, u, :], AX.X).then_inc(exped, 1)

            def emit(b, u, prev, cur, nxt):
                for g in range(NG if cur else 1):
                    if g == 0 and prev and not cur:
                        keep_weights(b - 1, 1 - u)
                    if (g == 1 or not cur) and prev:
                        negate(b - 1, 1 - u)
                    if g == 1 and not (b.r is None and b.c < 2):
                        keep_pool(b - 2, u)
                    if nxt:
                        for f in fills_behind(g):
                            add_bias(b + 1, 1 - u, f)
                    if g == 0 and prev and cur:
                        keep_weights(b - 1, 1 - u)
                    if g == 2 and prev:
                        sum_exp(b - 1, 1 - u)
                if nxt:
                    aggregate(b + 1, 1 - u)
                    invert(b + 1, 1 - u)
                    for g in range(NG):
                        centre(b + 1, 1 - u, g)
                if not cur:
                    keep_pool(b - 2, u)
                    sum_exp(b - 1, 1 - u)
                if prev:
                    keep_partial(b - 1)

            nc.vector.memset(cc_ps[:, :], 0.0).then_inc(cc_cleared, 1)
            for u in range(2):
                nc.vector.memset(mv[u][:, :, :], 1.0).then_inc(mvset, 1)
            dve.wait_ge(mvset, 2)
            first = Count(None, 0, 0)
            for f in range(NF):
                add_bias(first, 0, f)
            aggregate(first, 0)
            invert(first, 0)
            for g in range(NG):
                centre(first, 0, g)
            run(dve, emit)
            keep_pool(Count(None, 0, B - 1), (B - 1) % 2)

            links = [0]

            def link(ins):
                links[0] += 1
                ins.then_inc(mstep, 1)
                dve.wait_ge(mstep, links[0])

            dve.wait_ge(mlp, 1)
            link(nc.vector.tensor_tensor(g1[:, :], w_ps[0:B, 0:D], kb1[:, :], ALU.add))
            link(nc.vector.bn_stats(kst[:, :], g1[:, :]))
            link(nc.vector.bn_aggr(kmv[:, 0:2], kst[:, :]))
            dve.wait_ge(act_mlp, 1)
            link(nc.vector.reciprocal(kmv[:, 3:4], kmv[:, 2:3]))
            link(nc.vector.scalar_tensor_tensor(out=g1[:, :], in0=g1[:, :], scalar=kmv[:, 0:1], in1=kg[:, :],
                                                op0=ALU.subtract, op1=ALU.mult))
            link(nc.vector.scalar_tensor_tensor(out=g1[:, :], in0=g1[:, :], scalar=kmv[:, 3:4], in1=kbeta[:, :],
                                                op0=ALU.mult, op1=ALU.add))
            dve.wait_ge(mlp, 2)
            link(nc.vector.tensor_copy(gT[:, :], t_ps[0][:, 0:B]))
            dve.wait_ge(mlp, 3)
            flat = kp[:, :, :].rearrange("b h k -> b (h k)")
            link(nc.vector.tensor_tensor(flat, w_ps[0:B, 0:H * 9], kb2[:, :], ALU.add))
            link(nc.vector.tensor_reduce(kmax[:, 0, :], kp[:, :, :], axis=AX.X, op=ALU.max))
            link(nc.vector.tensor_tensor(kp[:, :, :], kp[:, :, :], kmax[:, 0, :].unsqueeze(2).broadcast_to([B, H, 9]),
                                         ALU.subtract))
            dve.wait_ge(act_mlp, 3)
            link(nc.vector.reduce_sum(kmax[:, 1, :], kp[:, :, :], AX.X))
            link(nc.vector.reciprocal(kmax[:, 2, :], kmax[:, 1, :]))
            link(nc.vector.memset(rows0[:, :, :], 0.0))
            k4 = kp[:, :, :].rearrange("b h (i j) -> b h i j", i=3)
            r4 = rows0[:, :, :].rearrange("b (h i) w -> b h i w", i=3)
            for j in range(3):
                link(nc.vector.tensor_tensor(r4[:, :, :, P - 1 + j:P + j], k4[:, :, :, 2 - j:3 - j],
                                             kmax[:, 2, :].unsqueeze(2).unsqueeze(3).broadcast_to([B, H, 3, 1]),
                                             ALU.mult))
            dve.sem_inc(rows_done, 1)


def head_values_stage(nc, stage, XT, w, V):
    G = 4
    with Scope(nc, stage) as sc:
        wv = sc.sb("wv", [D, D])
        ps = [sc.ps(f"ps{u}", [P, G * D]) for u in range(2)]
        w_loaded, ones_set, product, kept = (sc.sem(n) for n in ("w_loaded", "ones_set", "product", "kept"))
        block = sc.block()

        @block.sync
        def _(sp):
            sp.dma_start(wv[:, :], w).then_inc(w_loaded, 16)

        @block.gpsimd
        def _(pool):
            nc.gpsimd.memset(V[:, :, :, :], 1.0).then_inc(ones_set, 1)

        @block.tensor
        def _(pe):
            pe.wait_ge(w_loaded, 16)
            for g in range(NT // G):
                if g >= 2:
                    pe.wait_ge(kept, g - 1)
                for k in range(G):
                    n = g * G + k
                    last = nc.tensor.matmul(ps[g % 2][:, k * D:(k + 1) * D], XT[:, n * P:(n + 1) * P], wv[:, :],
                                            start=True, stop=True)
                last.then_inc(product, 1)

        @block.scalar
        def _(act):
            act.wait_ge(ones_set, 1)
            for g in range(NT // G):
                act.wait_ge(product, g + 1)
                nc.scalar.activation(V[:, g * G:(g + 1) * G, :, 0:HD],
                                     ps[g % 2][:, :].rearrange("p (t h d) -> p t h d", h=H, d=HD),
                                     ACT.Copy).then_inc(kept, 1)



BAND = P + 2


def conv_attention_stage(nc, stage, A, R, V, qs, ks, taps):
    SCALE = float(HD) ** -0.5
    X = R["X"]
    QP = S + 2
    NET = 8
    NSLOTS = 4
    with Scope(nc, stage) as sc:
        wo, bo = sc.sb("wo", [D, D]), sc.sb("bo", [P, D])
        m8 = sc.sb("m8", [P, 2, QT, S], U8)
        keepT = sc.sb("keepT", [P, QT, S])
        neg = sc.sb("neg", [P, QT, S])
        K6 = [sc.sb(f"K6{u}", [P, NPAIR, S], BF16) for u in range(2)]
        Q6 = [sc.sb(f"Q6{u}", [P, H, S], BF16) for u in range(2)]
        band = [sc.sb(f"band{k}", [P, 2, 3, BAND]) for k in range(NSLOTS)]
        A0 = [sc.sb(f"A0{u}", [P, 2, QT, QP]) for u in range(2)]
        E = [sc.sb(f"E{u}", [P, QT, S]) for u in range(2)]
        ET = [sc.sb(f"ET{k}", [P, QT, S]) for k in range(NET)]
        Vb = [sc.sb(f"Vb{u}", [P, QT, H, HD + 1]) for u in range(2)]
        osb = sc.sb("osb", [P, S])
        mx = sc.sb("mx", [P, 2, QT])
        negm = sc.sb("negm", [P, 2, QT])
        rl = sc.sb("rl", [P, QT, 4])
        on = sc.sb("on", [P, QT, H, HD])
        oT = sc.sb("oT", [P, QT, P])
        xo = sc.sb("xo", [P, QT, D])
        qk_ps = [sc.ps(f"qk_ps{k}", [P, 2, S]) for k in range(QT)]
        c_ps = [sc.ps(f"c_ps{u}", [P, QT, S]) for u in range(2)]
        t_ps = [sc.ps(f"t_ps{u}", [P, QT, QT, P]) for u in range(2)]
        o_ps = sc.ps("o_ps", [P, S])
        f_ps = sc.ps("f_ps", [P, QT, D])
        v_copied, o_cleared, o_copied, o_full = (sc.sem(n) for n in ("v_copied", "o_cleared", "o_copied", "o_full"))
        w_loaded, cleared, masks = (sc.sem(n) for n in ("w_loaded", "cleared", "masks"))
        kq_loaded = [sc.sem(f"kq_loaded{u}") for u in range(2)]
        band_loaded = [sc.sem(f"band_loaded{k}") for k in range(NSLOTS)]
        scored, masked, convolved, added, negated, exped, turned, kept, weighted = (
            sc.sem(n) for n in ("scored", "masked", "convolved", "added", "negated", "exped", "turned", "kept",
                                "weighted"))
        inverted, o_read, o_turned, o_kept, projected, summed, x_done, passed, passed_v = (
            sc.sem(n) for n in ("inverted", "o_read", "o_turned", "o_kept", "projected", "summed", "x_done",
                                "passed", "passed_v"))
        passed_p = sc.sem("passed_p")
        block = sc.block()
        NCLEAR = 6

        def run(engine, emit):
            emit(Count(None, 0, 0), 0, True, False)
            with engine.Fori(0, (B - 2) // 2) as r:
                for v in range(2):
                    emit(Count(r, 2, 1 + v), (1 + v) % 2, False, False)
            emit(Count(None, 0, B - 1), 1, False, True)

        @block.sync
        def _(sp):
            for dst, src in ((m8[:, 0, :, :], A["L1_maskT"]), (m8[:, 1, :, :], A["L1_mask"]),
                             (wo[:, :], A["proj_W"]), (bo[:, :], A["proj_b"].partition_broadcast(P))):
                sp.dma_start(dst, src).then_inc(w_loaded, 16)
            sp.wait_ge(cleared, NCLEAR)

            def load_kq(b, u):
                for g in range(2):
                    rows = slice(64 * g, 64 * g + HD * NTERM)
                    for dst, src in ((K6[u][rows, :, :], ks),
                                     (Q6[u][rows, :, :].rearrange("r (p g) n -> r g p n", g=2)[:, g], qs)):
                        src = src.rearrange("(p g d) t n -> g (d t) p n", g=2, d=HD)[g]
                        sp.dma_start(dst, src[:, :, bass.ds((b * S).v, S)]).then_inc(kq_loaded[u], 16)

            def load_band(b, j):
                src = taps[(b * H + 2 * j).v]
                src = bass.AP(tensor=src.tensor, offset=src.offset,
                              ap=[[1, P], [3 * (2 * P + 2), 2], [2 * P + 2, 3], [1, BAND]])
                sp.dma_start(band[j % NSLOTS][:, :, :, :], src).then_inc(band_loaded[j % NSLOTS], 16)

            first = Count(None, 0, 0)
            load_kq(first, 0)
            for j in range(NSLOTS - 1):
                load_band(first, j)

            def emit(b, u, start, end):
                if not end:
                    own_wait(sp, scored, b * NPAIR, passed)
                    load_kq(b + 1, 1 - u)
                for j in range(NPAIR):
                    ahead = j + NSLOTS - 1
                    if ahead < NPAIR or not end:
                        own_wait(sp, convolved, b * H + 2 * j, passed)
                        load_band(b + ahead // NPAIR, ahead % NPAIR)

            run(sp, emit)

        @block.gpsimd
        def _(pool):
            for t in K6 + Q6:
                nc.gpsimd.memset(t[:, :, :], 0.0).then_inc(cleared, 1)
            for t in A0:
                nc.gpsimd.memset(t[:, :, :, :], 0.0).then_inc(cleared, 1)

            def copy_values(b, u):
                nc.gpsimd.tensor_copy(Vb[u][:, :, :, :], V[:, bass.ds((b * QT).v, QT), :, :]).then_inc(v_copied, 1)

            def emit(b, u, start, end):
                if not end:
                    own_wait(pool, weighted, b * 4, passed_p)
                    own_wait(pool, v_copied, b + 1, passed_p)
                    copy_values(b + 1, 1 - u)

            pool.wait_ge(cleared, NCLEAR)
            copy_values(Count(None, 0, 0), 0)
            run(pool, emit)

        @block.tensor
        def _(pe):
            pe.wait_ge(w_loaded, 4 * 16)
            pe.wait_ge(cleared, NCLEAR)
            pe.wait_ge(o_cleared, 1)

            def scores(b, u, j):
                if j == 0:
                    wait(pe, kq_loaded[u], b.half() * 64 + 64)
                wait(pe, masked, (b * NPAIR + j) * QT)
                for k in range(QT):
                    last = nc.tensor.matmul(qk_ps[k][:, :, :], K6[u][:, j, k * P:(k + 1) * P],
                                            Q6[u][:, 2 * j:2 * j + 2, :], start=True, stop=True)
                last.then_inc(scored, 1)

            def convolve(b, h):
                j, g = divmod(h, 2)
                n = b * H + h
                wait(pe, masked, (b * NPAIR + (j + 1)) * QT)
                wait(pe, band_loaded[j % NSLOTS], b * (16 * NPAIR // NSLOTS) + 16 * (j // NSLOTS + 1))
                wait(pe, added, (n - 1) * QT)
                for q in range(QT):
                    for k in range(QT):
                        first_col = 1 - k
                        out = c_ps[h % 2][:, q, k * (P - 1):k * (P - 1) + P + 1]
                        for a in range(3):
                            last = nc.tensor.matmul(
                                out, A0[j % 2][:, g, k, q * P + a:q * P + a + P],
                                band[j % NSLOTS][:, g, a, first_col:first_col + P + 1],
                                start=(q == 0 and k == 0 and a == 0), stop=(q == 1 and k == 1 and a == 2),
                                skip_group_check=True)
                last.then_inc(convolved, 1)

            def turn(b, h):
                n = b * H + h
                wait(pe, exped, n + 1)
                wait(pe, kept, n - 1)
                for k in range(QT):
                    for q in range(QT):
                        last = nc.tensor.transpose(t_ps[h % 2][:, k, q, :], E[h % 2][:, q, k * P:(k + 1) * P],
                                                   R["ident"][:, :])
                last.then_inc(turned, 1)

            def weight(b, u, quad):
                m = b * 4 + quad
                wait(pe, kept, m * 4 + 4)
                wait(pe, o_copied, m)
                if quad == 0:
                    wait(pe, v_copied, b + 1)
                for t in range(QT):
                    for k in range(4):
                        h = 4 * quad + k
                        last = nc.tensor.matmul(o_ps[32 * k:32 * k + HD + 1, :], Vb[u][:, t, h, :],
                                                ET[h % NET][:, t, :], start=(t == 0), stop=(t == QT - 1),
                                                tile_position=(0, 32 * k))
                last.then_inc(weighted, 1)

            def turn_quad(b, quad):
                m = b * 4 + quad
                wait(pe, o_copied, m + 1)
                if quad == 0:
                    wait(pe, summed, b)
                else:
                    wait(pe, o_read, m)
                for q in range(QT):
                    last = nc.tensor.transpose(f_ps[:, q, :], osb[:, q * P:(q + 1) * P], R["ident"][:, :])
                last.then_inc(o_full, 1)

            def turn_out(b):
                wait(pe, o_read, b * 4 + 4)
                for q in range(QT):
                    last = nc.tensor.transpose(f_ps[:, q, :], on[:, q, :, :].rearrange("p h d -> p (h d)"),
                                               R["ident"][:, :])
                last.then_inc(o_turned, 1)

            def project_out(b):
                wait(pe, o_kept, b + 1)
                for q in range(QT):
                    last = nc.tensor.matmul(f_ps[:, q, :], oT[:, q, :], wo[:, :], start=True, stop=True)
                last.then_inc(projected, 1)

            def emit(b, u, start, end):
                for h in range(H):
                    convolve(b, h)
                    if h % 2 == 0 and (h < H - 2 or not end):
                        if h < H - 2:
                            scores(b, u, h // 2 + 1)
                        else:
                            scores(b + 1, 1 - u, 0)
                    if h >= 1:
                        turn(b, h - 1)
                    elif not start:
                        turn(b - 1, H - 1)
                    if h % 4 == 1 and h > 1:
                        weight(b, u, h // 4 - 1)
                    if h % 4 == 2 and h > 2:
                        turn_quad(b, h // 4 - 1)
                    if not start:
                        if h == 1:
                            weight(b - 1, 1 - u, 3)
                        if h == 2:
                            turn_quad(b - 1, 3)
                        if h == 4:
                            turn_out(b - 1)
                        if h == 5:
                            project_out(b - 1)

            scores(Count(None, 0, 0), 0, 0)
            run(pe, emit)
            end = Count(None, 0, B - 1)
            turn(end, H - 1)
            weight(end, 1, 3)
            turn_quad(end, 3)
            turn_out(end)
            project_out(end)

        @block.scalar
        def _(act):
            def exp(b, h):
                n = b * H + h
                wait(act, negated, n + 1)
                for q in range(QT):
                    last = nc.scalar.activation(E[h % 2][:, q, :], E[h % 2][:, q, :], ACT.Exp,
                                                bias=negm[:, h % 2, q:q + 1])
                last.then_inc(exped, 1)

            def keep(b, h):
                n = b * H + h
                wait(act, turned, n + 1)
                wait(act, weighted, b * 4 + (h // 4 - 1))
                nc.scalar.activation(ET[h % NET][:, :, :], t_ps[h % 2][:, :, :, :].rearrange("p k q n -> p k (q n)"),
                                     ACT.Copy).then_inc(kept, 1)

            def keep_out(b):
                wait(act, o_turned, b + 1)
                wait(act, projected, b)
                nc.scalar.activation(oT[:, :, :], f_ps[:, :, :], ACT.Copy).then_inc(o_kept, 1)

            def emit(b, u, start, end):
                for h in range(H):
                    if h:
                        keep(b, h - 1)
                    elif not start:
                        keep(b - 1, H - 1)
                    exp(b, h)
                    if h == 4 and not start:
                        keep_out(b - 1)

            run(act, emit)
            end = Count(None, 0, B - 1)
            keep(end, H - 1)
            keep_out(end)

        @block.vector
        def _(dve):
            dve.wait_ge(w_loaded, 4 * 16)
            dve.wait_ge(cleared, NCLEAR)
            nc.vector.tensor_scalar(keepT[:, :, :], m8[:, 0, :, :], 0.0, None, ALU.is_equal).then_inc(masks, 1)
            nc.vector.tensor_scalar(neg[:, :, :], m8[:, 1, :, :], 0.0, -BIG, ALU.not_equal, ALU.mult).then_inc(masks, 1)
            dve.wait_ge(masks, 2)

            def mask(b, j):
                m = b * NPAIR + j
                wait(dve, scored, m + 1)
                for k in range(QT):
                    nc.vector.scalar_tensor_tensor(
                        out=A0[j % 2][:, :, k, 1:S + 1], in0=qk_ps[k][:, :, :], scalar=SCALE,
                        in1=keepT[:, k, :].unsqueeze(1).broadcast_to([P, 2, S]),
                        op0=ALU.mult, op1=ALU.mult).then_inc(masked, 1)

            def maximum(b, h):
                n = b * H + h
                wait(dve, convolved, n + 1)
                wait(dve, turned, n - 1)
                if n.r is not None:
                    dve.sem_inc(passed_v, 1)
                for q in range(QT):
                    nc.vector.tensor_tensor_reduce(
                        out=E[h % 2][:, q, :], in0=c_ps[h % 2][:, q, :], in1=neg[:, q, :], scale=1.0,
                        scalar=-3.0e38, op0=ALU.add, op1=ALU.max, accum_out=mx[:, h % 2, q:q + 1])\
                      .then_inc(added, 1)
                wait(dve, added, n * QT + QT)
                nc.vector.tensor_scalar(negm[:, h % 2, :], mx[:, h % 2, :], -1.0, None, ALU.mult).then_inc(negated, 1)

            def copy_quad(b, quad):
                m = b * 4 + quad
                wait(dve, weighted, m + 1)
                wait(dve, o_full, m)
                nc.vector.tensor_copy(osb[:, :], o_ps[:, :]).then_inc(o_copied, 1)

            def normalise(b, quad):
                m = b * 4 + quad
                wait(dve, o_full, m + 1)
                o = f_ps[:, :, :].rearrange("p q (h r) -> p q h r", h=4)
                nc.vector.reciprocal(rl[:, :, :], o[:, :, :, HD]).then_inc(inverted, 1)
                wait(dve, inverted, m + 1)
                if quad == 0:
                    wait(dve, o_turned, b)
                nc.vector.tensor_tensor(on[:, :, 4 * quad:4 * quad + 4, :], o[:, :, :, 0:HD],
                                        rl[:, :, :].unsqueeze(3).broadcast_to([P, QT, 4, HD]),
                                        ALU.mult).then_inc(o_read, 1)

            def add_out(b):
                wait(dve, projected, b + 1)
                xb = X[:, bass.ds((b * QT).v, QT), :]
                nc.vector.tensor_tensor(xo[:, :, :], f_ps[:, :, :], xb, ALU.add).then_inc(summed, 1)
                wait(dve, summed, b + 1)
                nc.vector.tensor_tensor(xb, xo[:, :, :], bo[:, :].unsqueeze(1).broadcast_to([P, QT, D]),
                                        ALU.add).then_inc(x_done, 1)

            def emit(b, u, start, end):
                for h in range(H):
                    maximum(b, h)
                    if h % 2 == 0 and (h < H - 2 or not end):
                        if h < H - 2:
                            mask(b, h // 2 + 1)
                        else:
                            mask(b + 1, 0)
                    if h % 4 == 1 and h > 1:
                        copy_quad(b, h // 4 - 1)
                    if h % 4 == 2 and h > 2:
                        normalise(b, h // 4 - 1)
                    if not start:
                        if h == 1:
                            copy_quad(b - 1, 3)
                        if h == 2:
                            normalise(b - 1, 3)
                        if h == 5:
                            add_out(b - 1)

            nc.vector.memset(o_ps[:, :], 0.0).then_inc(o_cleared, 1)
            mask(Count(None, 0, 0), 0)
            run(dve, emit)
            end = Count(None, 0, B - 1)
            copy_quad(end, 3)
            normalise(end, 3)
            add_out(end)


def store_stage(nc, stage, R, out):
    with Scope(nc, stage) as sc:
        stored = sc.sem("stored")
        block = sc.block()

        @block.sync
        def _(sp):
            sp.dma_start(out.rearrange("(n p) d -> p n d", p=P), R["X"][:, :, :]).then_inc(stored, 16)
            sp.wait_ge(stored, 16)


def cross_attention_layer(nc, name, A, R, masked):
    qs = scratch(nc, f"{name}_qs", [P, NTERM, TOK], BF16)
    ks = [scratch(nc, f"{name}_ks{u}", [P, NTERM, S2], BF16) for u in range(2)]
    mrow = scratch(nc, f"{name}_mrow", [2, 2, 16, P], BF16)
    w = {k: A[f"{name}_{k}"] for k in ("wk", "wv", "wo", "bk", "bv", "bo")}
    with Scope(nc, f"{name}_in") as sc:
        XT = sc.sb("XT", [D, TOK])
        layernorm_stage(nc, f"{name}_ln", R, XT=XT)
        head_operands_stage(nc, f"{name}_q", [(XT, A[f"{name}_wq"], A[f"{name}_bq"], qs, Q_PART)])
    attention_stage(nc, f"{name}_at", A, R, w, qs, ks, mrow, masked)


def conv_attention_layer(nc, name, A, R):
    taps = scratch(nc, f"{name}_taps", [B, H, 3, 2 * P + 2], F32)
    qs = scratch(nc, f"{name}_qs", [P, NTERM, TOK], BF16)
    ks = scratch(nc, f"{name}_ks", [P, NTERM, TOK], BF16)
    history_kernels_stage(nc, f"{name}_hk", A, R, taps)
    with Scope(nc, name) as sc:
        V = sc.sb("V", [P, NT, H, HD + 1])
        with Scope(nc, f"{name}_in") as inner:
            XT, XR = inner.sb("XT", [D, TOK]), inner.sb("XR", [D, TOK])
            layernorm_stage(nc, f"{name}_ln", R, XT=XT, XR=XR)
            head_operands_stage(nc, f"{name}_qk", [(XT, A[f"{name}_wq"], None, qs, Q_PART),
                                                   (XR, A[f"{name}_wk"], None, ks, K_PART)])
            head_values_stage(nc, f"{name}_v", XT, A[f"{name}_wv"], V)
        conv_attention_stage(nc, f"{name}_at", A, R, V, qs, ks, taps.rearrange("b h i w -> (b h) i w"))


def first_moe_layer(nc, name, A, R):
    xs, ys = (scratch(nc, f"{name}_{n}", [NBLK * BLK, D], F32) for n in ("xs", "ys"))
    with Scope(nc, name) as sc:
        XN, slot, gate = sc.sb("XN", [P, NT, D]), sc.sb("slot", [P, NT], U32), sc.sb("gate", [P, NT])
        weight_row = sc.sb("weight_row", [P, NBLK], U32)
        with Scope(nc, f"{name}_in") as inner:
            XT = inner.sb("XT", [D, TOK])
            layernorm_stage(nc, f"{name}_ln", R, XT=XT, XN=XN)
            top1_router_stage(nc, f"{name}_r", A, R, XT, slot, gate, weight_row, xs)
        blocked_ffn_stage(nc, f"{name}_e", R, XN, slot, gate, weight_row, A["L1_W1"].rearrange("e p f -> (e p) f"),
                          A["L1_W2"], A["L1_b1"].rearrange("e p f -> (e p) f"), xs, ys, ACT.Relu)


def second_moe_layer(nc, name, A, R):
    xs, ys = (scratch(nc, f"{name}_{n}", [2 * TOK, D], F32) for n in ("xs", "ys"))
    with Scope(nc, name) as sc:
        XN, slot, weight = sc.sb("XN", [P, NT, D]), sc.sb("slot", [P, 2, NT], U32), sc.sb("weight", [P, 2, NT])
        with Scope(nc, f"{name}_in") as inner:
            XT = inner.sb("XT", [D, TOK])
            layernorm_stage(nc, f"{name}_ln", R, XT=XT, XN=XN)
            top2_router_stage(nc, f"{name}_r", A, XT, slot, weight)
        dispatched_ffn_stage(nc, f"{name}_e", R, XN, slot, weight, A["L2_W1"], A["L2_W2"], xs, ys, ACT.Gelu)


def build_program(nc, A, out):
    with ExitStack() as stack:
        R = {"X": stack.enter_context(nc.sbuf_tensor("x", [P, NT, D], F32)),
             "ident": stack.enter_context(nc.sbuf_tensor("ident", [P, P], F32)),
             "identb": stack.enter_context(nc.sbuf_tensor("identb", [P, P], BF16))}
        constants_stage(nc, A, R)
        cross_attention_layer(nc, "L0", A, R, masked=False)
        with Scope(nc, "L0f") as sc:
            XN = sc.sb("XN", [P, NT, D])
            layernorm_stage(nc, "L0f_ln", R, XN=XN)
            quantised_ffn_stage(nc, "L0f_mm", A, R, XN)
        conv_attention_layer(nc, "L1", A, R)
        first_moe_layer(nc, "L1f", A, R)
        with Scope(nc, "L2a") as sc:
            XT = sc.sb("XT", [D, TOK])
            layernorm_stage(nc, "L2a_ln", R, XT=XT)
            wide_attention_stage(nc, "L2a_at", A, R, XT)
        second_moe_layer(nc, "L2f", A, R)
        cross_attention_layer(nc, "L3", A, R, masked=True)
        with Scope(nc, "L3f") as sc:
            XN = sc.sb("XN", [P, NT, D])
            layernorm_stage(nc, "L3f_ln", R, XN=XN)
            bitnet_ffn_stage(nc, "L3f_mm", A, R, XN)
        store_stage(nc, "store", R, out)


def kernel(**inputs):
    import numpy as np
    import concourse.bacc as bacc
    from concourse.bass_utils import run_bass_kernel_spmd

    I = {k: np.asarray(v) for k, v in inputs.items()}
    mask = I["mask_Bx1xSxS2_ik1"].reshape(B, S, S2)
    causal = I["mask_SxS_bc0"]
    L = {"x": I["x"].reshape(TOK, D), "ctx": I["ctx_1024"], "ctxT": I["ctx_1024"].transpose(0, 2, 1),
         "mask": mask, "maskT": mask.transpose(0, 2, 1),
         "L1_mask": causal.reshape(QT, P, S).transpose(1, 0, 2),
         "L1_maskT": causal.reshape(S, QT, P)[:, :, ::-1].transpose(2, 1, 0),
         "L0_rhsT": I["L0_ffn_rhs"].T}
    for n in ("L0", "L3"):
        for k in "qkvo":
            L[f"{n}_w{k}"] = I[f"{n}_xattn_W{k}"].T
            L[f"{n}_b{k}"] = I[f"{n}_xattn_b{k}"].reshape((D,) if k == "o" else (D, 1))
    for k in "qkv":
        L[f"L1_w{k}"] = I[f"L1_xattn_W{k}"]
    for k in ("hist_W", "hist_b", "hist_ln_g", "hist_ln_b", "ctx_W1", "ctx_W2", "ctx_b2", "kg_W1", "kg_b1",
              "kg_ln_g", "kg_ln_b", "kg_W2", "kg_b2", "proj_W", "proj_b"):
        L[k] = I[f"L1_xattn_{k}"]
    L["ctx_b1"] = I["L1_xattn_ctx_b1"].reshape(-1, 1)
    for k in ("Wr", "br", "W1", "W2", "b2"):
        L[f"L1_{k}"] = I[f"L1_ffn_{k}"]
    L["L1_W2"] = I["L1_ffn_W2"].reshape(8, 4, P, D).transpose(0, 2, 1, 3).reshape(8 * P, 4 * D)
    L["L1_b1"] = I["L1_ffn_b1"].reshape(8, 4, P).transpose(0, 2, 1)
    for k in "qk":
        L[f"L2_w{k}"] = I[f"L2_xattn_W{k}"].T
        L[f"L2_b{k}"] = I[f"L2_xattn_b{k}"].reshape(D, 1)
    L.update({"L2_Wr": I["L2_ffn_Wr"].T, "L2_W1": I["L2_ffn_W1"], "L2_W2": I["L2_ffn_W2"],
              "L3_w1T": I["L3_ffn_w1"].T, "L3_w2T": I["L3_ffn_w2"].T, "L3_cw": I["L3_ffn_conv_w"].reshape(-1, 3),
              "L3_cb": I["L3_ffn_conv_b"].reshape(4, P).T})

    nc = bacc.Bacc("TRN2", target_bir_lowering=False, num_devices=1)
    arrays, A = {}, {}
    for name, a in L.items():
        arrays[f"in_{name}_dram"] = a = np.ascontiguousarray(a)
        A[name] = nc.dram_tensor(f"in_{name}_dram", a.shape, mybir.dt.from_np(a.dtype), kind="ExternalInput").ap()
    out = nc.dram_tensor("out_dram", (TOK, D), F32, kind="ExternalOutput").ap()
    build_program(nc, A, out)
    r = run_bass_kernel_spmd(nc, [arrays], core_ids=[0])
    return r.results[0]["out_dram"].reshape(B, S, D)
```
